# Optimizing a Trainium2 kernel written in Bass

```python
import numpy as np
import jax
import jax.numpy as jnp

def _softmax(x, axis=-1):
    return jax.nn.softmax(x, axis=axis)

def _gelu(x):
    return jax.nn.gelu(x, approximate=True)

def _silu(x):
    return jax.nn.silu(x)

def _sigmoid(x):
    return jax.nn.sigmoid(x)

def _layernorm(x, axis=-1, eps=1e-05):
    m = jnp.mean(x, axis=axis, keepdims=True)
    v = jnp.var(x, axis=axis, keepdims=True)
    return (x - m) / jnp.sqrt(v + eps)

def _scatter_add(tgt, idx, src, axis=0):
    return tgt.at[idx].add(src)

def _segment_sum(src, seg, n):
    return jax.ops.segment_sum(src, seg, n)
kernel_name = 'mk_macaron_d1_jaxref_r4_966762'

def setup_inputs(seed: int=0):
    np.random.seed(seed)
    _w = jnp.asarray

    def _L0_attn_setup():
        import jax, jax.numpy as jnp
        import numpy as np
        D_MODEL = 256
        NUM_HEADS = 16
        HEAD_DIM = D_MODEL // NUM_HEADS
        key = jax.random.key(seed)
        ks = jax.random.split(key, 10)
        B, L = (2, 512)
        s = 1.0 / np.sqrt(D_MODEL)
        x = jax.random.normal(ks[0], (B, L, D_MODEL), dtype=jnp.float32)
        Wq = jax.random.normal(ks[1], (D_MODEL, D_MODEL), dtype=jnp.float32) * s
        bq = jnp.zeros((D_MODEL,), dtype=jnp.float32)
        Wk = jax.random.normal(ks[2], (D_MODEL, D_MODEL), dtype=jnp.float32) * s
        bk = jnp.zeros((D_MODEL,), dtype=jnp.float32)
        Wv = jax.random.normal(ks[3], (D_MODEL, D_MODEL), dtype=jnp.float32) * s
        bv = jnp.zeros((D_MODEL,), dtype=jnp.float32)
        Wo = jax.random.normal(ks[4], (D_MODEL, D_MODEL), dtype=jnp.float32) * s
        bo = jnp.zeros((D_MODEL,), dtype=jnp.float32)
        gamma = jax.random.uniform(ks[5], (NUM_HEADS,), dtype=jnp.float32, minval=0.95, maxval=1.0)
        return {'x': x, 'Wq': Wq, 'bq': bq, 'Wk': Wk, 'bk': bk, 'Wv': Wv, 'bv': bv, 'Wo': Wo, 'bo': bo, 'gamma': gamma}
    _L0_attn_in = _L0_attn_setup()

    def _L0_ffn_setup():
        import jax, jax.numpy as jnp
        import numpy as np
        B, S, D, E, F = (4, 512, 256, 8, 1024)
        key = jax.random.key(seed)
        k0, k1, k2, k3 = jax.random.split(key, 4)
        x = jax.random.normal(k0, (B, S, D), dtype=jnp.float32)
        wg = jax.random.normal(k1, (D, E), dtype=jnp.float32) * 0.02
        w_gate = jax.random.normal(k2, (E, D, F), dtype=jnp.float32) * 0.02
        w_down = jax.random.normal(k3, (E, F, D), dtype=jnp.float32) * 0.02
        return {'x': x, 'wg': wg, 'w_gate': w_gate, 'w_down': w_down}
    _L0_ffn_in = _L0_ffn_setup()
    _d = {'L0_attn_x': _L0_attn_in['x'], 'L0_attn_Wq': _L0_attn_in['Wq'], 'L0_attn_bq': _L0_attn_in['bq'], 'L0_attn_Wk': _L0_attn_in['Wk'], 'L0_attn_bk': _L0_attn_in['bk'], 'L0_attn_Wv': _L0_attn_in['Wv'], 'L0_attn_bv': _L0_attn_in['bv'], 'L0_attn_Wo': _L0_attn_in['Wo'], 'L0_attn_bo': _L0_attn_in['bo'], 'L0_attn_gamma': _L0_attn_in['gamma'], 'L0_ffn_wg': _L0_ffn_in['wg'], 'L0_ffn_w_gate': _L0_ffn_in['w_gate'], 'L0_ffn_w_down': _L0_ffn_in['w_down']}
    _x0 = _d['L0_attn_x']
    _d['L0_attn_x'] = jax.random.normal(jax.random.fold_in(jax.random.key(seed), 1), (8, 1024, 256), dtype=_x0.dtype)
    del _x0
    return _d

def reference(L0_attn_x, L0_attn_Wq, L0_attn_bq, L0_attn_Wk, L0_attn_bk, L0_attn_Wv, L0_attn_bv, L0_attn_Wo, L0_attn_bo, L0_attn_gamma, L0_ffn_wg, L0_ffn_w_gate, L0_ffn_w_down):

    def _L0_attn_ref(x, Wq, bq, Wk, bk, Wv, bv, Wo, bo, gamma):
        import jax, jax.numpy as jnp
        import numpy as np
        D_MODEL = 256
        NUM_HEADS = 16
        HEAD_DIM = D_MODEL // NUM_HEADS
        B, L, D = x.shape
        H, hd = (NUM_HEADS, HEAD_DIM)
        q = (x @ Wq.T + bq).reshape(B, L, H, hd).transpose(0, 2, 1, 3)
        k = (x @ Wk.T + bk).reshape(B, L, H, hd).transpose(0, 2, 1, 3)
        v = (x @ Wv.T + bv).reshape(B, L, H, hd).transpose(0, 2, 1, 3)
        idx = jnp.arange(L, dtype=x.dtype)
        decay = gamma[None, :, None, None] ** idx[None, None, :, None]
        scores = jnp.einsum('bhqd,bhkd->bhqk', q, k)
        causal = jnp.tril(jnp.ones((L, L), dtype=x.dtype))
        scores = scores * causal[None, None] * decay
        out = jnp.einsum('bhqk,bhkd->bhqd', scores, v)
        out = out.transpose(0, 2, 1, 3).reshape(B, L, D)
        return out @ Wo.T + bo

    def _L0_ffn_ref(x, wg, w_gate, w_down):
        import jax, jax.numpy as jnp
        import numpy as np
        B, S, D, E, F = (4, 512, 256, 8, 1024)
        Bb, Ss, Dd = x.shape
        Ee = wg.shape[1]
        T = Bb * Ss
        C = 2 * T // Ee
        tokens = x.reshape(T, Dd)
        logits = tokens.astype(jnp.float32) @ wg.astype(jnp.float32)
        gates = jax.nn.softmax(logits, axis=-1)
        idx1 = jnp.argmax(gates, axis=-1)
        mask1 = jax.nn.one_hot(idx1, Ee, dtype=jnp.int32)
        logits_no1 = jnp.where(mask1 > 0, -jnp.inf, logits)
        idx2 = jnp.argmax(logits_no1, axis=-1)
        mask2 = jax.nn.one_hot(idx2, Ee, dtype=jnp.int32)
        g1 = jnp.take_along_axis(gates, idx1[:, None], axis=-1)[:, 0]
        g2 = jnp.take_along_axis(gates, idx2[:, None], axis=-1)[:, 0]
        denom = jnp.clip(g1 + g2, 1e-09, None)
        g1, g2 = (g1 / denom, g2 / denom)
        loc1 = jnp.cumsum(mask1, axis=0) - mask1
        loc2 = jnp.cumsum(mask2, axis=0) - mask2 + jnp.sum(mask1, axis=0, keepdims=True)
        loc1_s = jnp.sum(loc1 * mask1, axis=-1)
        loc2_s = jnp.sum(loc2 * mask2, axis=-1)
        keep1 = (loc1_s < C).astype(x.dtype)
        keep2 = (loc2_s < C).astype(x.dtype)
        f1 = idx1 * C + jnp.minimum(loc1_s, C - 1)
        f2 = idx2 * C + jnp.minimum(loc2_s, C - 1)
        disp = jnp.zeros((Ee * C, Dd), dtype=x.dtype)
        disp = disp.at[f1].add(tokens * keep1[:, None])
        disp = disp.at[f2].add(tokens * keep2[:, None])
        disp = disp.reshape(Ee, C, Dd)
        h = jax.nn.gelu(jnp.einsum('ecd,edf->ecf', disp, w_gate), approximate=False)
        eo = jnp.einsum('ecf,efd->ecd', h, w_down).reshape(Ee * C, Dd)
        out = (g1 * keep1)[:, None].astype(x.dtype) * eo[f1] + (g2 * keep2)[:, None].astype(x.dtype) * eo[f2]
        return out.reshape(Bb, Ss, Dd)
    x = L0_attn_x
    x = x + 0.5 * _L0_ffn_ref(_layernorm(x, axis=-1), L0_ffn_wg, L0_ffn_w_gate, L0_ffn_w_down)
    x = x + _L0_attn_ref(_layernorm(x, axis=-1), L0_attn_Wq, L0_attn_bq, L0_attn_Wk, L0_attn_bk, L0_attn_Wv, L0_attn_bv, L0_attn_Wo, L0_attn_bo, L0_attn_gamma)
    x = x + 0.5 * _L0_ffn_ref(_layernorm(x, axis=-1), L0_ffn_wg, L0_ffn_w_gate, L0_ffn_w_down)
    return x

_drawn_inputs = setup_inputs


def setup_inputs(seed=0):
    import zlib

    import numpy as np

    out = dict(_drawn_inputs(seed))
    spreads = {'L0_attn_bq': (0.0, 0.1),
     'L0_attn_bk': (0.0, 0.1),
     'L0_attn_bv': (0.0, 0.1),
     'L0_attn_bo': (0.0, 0.784)}
    factors = {}
    for name, (base, spread) in spreads.items():
        noise = np.random.default_rng([zlib.crc32(name.encode()), seed]).standard_normal(out[name].shape)
        drawn = base * np.exp(spread * noise) if base else spread * noise
        out[name] = jnp.asarray(drawn.astype(out[name].dtype))
    for name, factor in factors.items():
        out[name] = (out[name] * factor).astype(out[name].dtype)
    return out
```

```python
from contextlib import ExitStack

import concourse.bass as bass
from concourse import mybir

F32 = mybir.dt.float32
F32R = mybir.dt.float32r
BF16 = mybir.dt.bfloat16
I32 = mybir.dt.int32
ALU = mybir.AluOpType
ACT = mybir.ActivationFunctionType
AX_X = mybir.AxisListType.X

P = 128
B, S, D = 8, 1024, 256
T = B * S
NT = T // P
E, F = 8, 1024
CAP = 2 * T // E
NSLOT = E * CAP
NCOL = NSLOT // P
TPB = 4
BLK = TPB * P
NB = NT // TPB
JB = CAP // BLK
NBLK = E * JB
KD = D // P
MF = F // P
ROW = D + 4
EPS = 1e-5
H = 16
HD = D // H
HH = H // KD
CH = 128
NEG = -3.0e38
PW = 32
assert PW * PW == S


class Count:

    def __init__(self, eng, sem, base=0):
        self.eng, self.sem, self.base, self.n = eng, sem, base, 0

    def link(self, ins):
        self.n += 1
        ins.then_inc(self.sem, 1)
        self.eng.wait_ge(self.sem, self.base + self.n)


def step_past(eng, passed):
    eng.sem_inc(passed, 1)


def split_low(nc, out, full, high):
    return nc.vector.tensor_tensor(out, full, high.bitcast(F32), ALU.subtract)


def three(nc, out, ah, al, bh, bl, first, final):
    nc.tensor.matmul(out, ah, bh, start=first, stop=False)
    nc.tensor.matmul(out, al, bh, start=False, stop=False)
    return nc.tensor.matmul(out, ah, bl, start=False, stop=final)


def build_constants(nc, c):
    with ExitStack() as ctx:
        made = ctx.enter_context(nc.semaphore("const_made"))
        chain = ctx.enter_context(nc.semaphore("const_chain"))
        iota_p = ctx.enter_context(nc.sbuf_tensor("iota_p", [P, 1], I32))
        iota_c = ctx.enter_context(nc.sbuf_tensor("iota_c", [P, P], I32))
        iota_id = ctx.enter_context(nc.sbuf_tensor("iota_id", [P, NT], I32))
        iota_dm = ctx.enter_context(nc.sbuf_tensor("iota_dm", [P, E, NCOL // E], I32))
        tri = ctx.enter_context(nc.sbuf_tensor("tri_f32", [P, P], F32))
        block = ctx.enter_context(nc.Block())

        @block.gpsimd
        def _(pool):
            nc.gpsimd.iota(iota_c[:], [[1, P]], base=0, channel_multiplier=0).then_inc(made, 1)
            nc.gpsimd.iota(iota_id[:], [[P, NT]], base=BLK + 1, channel_multiplier=1).then_inc(made, 1)
            nc.gpsimd.iota(iota_dm[:], [[0, E], [P, NCOL // E]], base=T + BLK + 1, channel_multiplier=1).then_inc(made, 1)
            ch = Count(pool, chain)
            ch.link(nc.gpsimd.memset(c["ident"][:], 0.0))
            nc.gpsimd.affine_select(out=c["ident"][:], in_=c["ident"][:], compare_op=ALU.not_equal, fill=1.0,
                                    base=0, pattern=[[-1, P]], channel_multiplier=1).then_inc(made, 1)
            ch.link(nc.gpsimd.memset(c["causal"][:], 1.0))
            nc.gpsimd.affine_select(out=c["causal"][:], in_=c["causal"][:], compare_op=ALU.is_ge, fill=0.0,
                                    base=0, pattern=[[1, P]], channel_multiplier=-1).then_inc(made, 1)
            ch.link(nc.gpsimd.memset(tri[:], 1.0))
            nc.gpsimd.affine_select(out=tri[:], in_=tri[:], compare_op=ALU.is_gt, fill=0.0,
                                    base=0, pattern=[[1, P]], channel_multiplier=-1).then_inc(made, 1)
            hm = c["head_mask"][:].rearrange("p (h d) -> p h d", d=HD)
            ch.link(nc.gpsimd.memset(c["head_mask"][:], 1.0))
            ch.link(nc.gpsimd.affine_select(out=hm, in_=hm, compare_op=ALU.is_ge, fill=0.0, base=0,
                                            pattern=[[-HD, HH], [0, HD]], channel_multiplier=1))
            nc.gpsimd.affine_select(out=hm, in_=hm, compare_op=ALU.is_ge, fill=0.0, base=HD - 1,
                                    pattern=[[HD, HH], [0, HD]], channel_multiplier=-1).then_inc(made, 1)

        @block.vector
        def _(dve):
            dve.wait_ge(made, 7)
            nc.vector.tensor_copy(c["iota"][:], iota_c[:])
            nc.vector.tensor_copy(c["token_id"][:], iota_id[:])
            nc.vector.tensor_copy(c["dummy_row"][:], iota_dm[:].rearrange("p e c -> p (e c)"))
            nc.vector.tensor_copy(c["before"][:], tri[:])
            nc.vector.memset(c["ones"][:], 1.0)
            for e in range(E):
                nc.vector.memset(c["rank"][:, e:e + 1], float(E - e))
            nc.vector.memset(c["restart"][:, :, 0:1], 0.0)
            nc.vector.memset(c["restart"][:, :, 1:NT], 1.0)


def normalise(nc, c, dve, ch, x, stats, mv, sd, rstd, out, sd_ready, sd_count, ve_ready):
    for i in range(TPB):
        last = nc.vector.bn_stats(stats[:, i, :], x[:, i, :])
    ch.link(last)
    step_past(dve, c["passed"])
    for i in range(TPB):
        last = nc.vector.bn_aggr(mv[:, i, :], stats[:, i, :])
    ch.link(last)
    nc.vector.tensor_scalar(sd[:], mv[:, :, 1], EPS, None, ALU.add).then_inc(ve_ready, 1)
    dve.wait_ge(sd_ready, sd_count)
    ch.link(nc.vector.reciprocal(rstd[:], sd[:]))
    for i in range(TPB):
        last = nc.vector.tensor_scalar(out[:, i, 0:D], x[:, i, :], mv[:, i, 0:1], rstd[:, i:i + 1],
                                       ALU.subtract, ALU.mult)
    return last


def route_first(nc, c, x, table, acc):
    with ExitStack() as ctx:
        def sb(name, shape, dt=F32):
            return ctx.enter_context(nc.sbuf_tensor(name, shape, dt))

        def sem(name):
            return ctx.enter_context(nc.semaphore(name))

        xb = [sb(f"r_x{i}", [P, TPB, D]) for i in range(2)]
        xn = [sb(f"r_xn{i}", [P, TPB, D]) for i in range(2)]
        xt = [sb(f"r_xt{i}", [P, KD, BLK]) for i in range(2)]
        stats = sb("r_stats", [P, TPB, 6])
        mv = sb("r_mv", [P, TPB, 2])
        sd = sb("r_sd", [P, TPB])
        rstd = sb("r_rstd", [P, TPB])
        ps_t = [ctx.enter_context(nc.psum_tensor(f"r_ps_t{i}", [P, KD, BLK], F32)) for i in range(2)]
        ps_l = [ctx.enter_context(nc.psum_tensor(f"r_ps_l{i}", [P, TPB * E], F32)) for i in range(2)]
        x_in = [sem(f"r_x_in{i}") for i in range(2)]
        xn_out = [sem(f"r_xn_out{i}") for i in range(2)]
        wg_in, acc_set, spare_set = sem("r_wg_in"), sem("r_acc_set"), sem("r_spare_set")
        ve_ready, sd_ready, xn_ready = sem("r_ve"), sem("r_sd_s"), sem("r_xn")
        t_done, xt_ready, l_done, l_copied, chain = (sem("r_t"), sem("r_xt_s"), sem("r_l"), sem("r_lc"), sem("r_chain"))
        xv = x.rearrange("(b i p) d -> b p i d", i=TPB, p=P)
        tv = table[BLK:, 0:D].rearrange("(b i p) d -> b p i d", i=TPB, p=P)
        block = ctx.enter_context(nc.Block())
        HALF = NB // 2

        @block.sync
        def _(sp):
            sp.dma_start(c["wg"][:], c["wg_dram"].rearrange("(k p) e -> p k e", p=P)).then_inc(wg_in, 16)
            for s in range(2):
                sp.dma_start(xb[s][:], xv[s]).then_inc(x_in[s], 16)
            sp.wait_ge(spare_set, 32)
            with sp.Fori(0, HALF - 1) as i:
                for s in range(2):
                    sp.wait_ge(xn_ready, 2 * i + s + 1)
                    sp.dma_start(xb[s][:], xv[2 * i + 2 + s]).then_inc(x_in[s], 16)
            sp.wait_ge(acc_set, 32)

        @block.gpsimd
        def _(pool):
            pool.wait_ge(x_in[0], 16)
            pool.dma_start(table[0:BLK, 0:D].rearrange("(i p) d -> p i d", p=P), xb[0][:]).then_inc(spare_set, 16)
            pool.dma_start(table[0:BLK, D:ROW].rearrange("(i p) w -> p i w", p=P), xb[0][:, :, 0:4]).then_inc(spare_set, 16)
            pool.wait_ge(spare_set, 32)
            with pool.Fori(0, HALF) as i:
                for s in range(2):
                    pool.wait_ge(xn_ready, 2 * i + s + 1)
                    pool.dma_start(tv[2 * i + s], xn[s][:]).then_inc(xn_out[s], 16)
            for s in range(2):
                pool.wait_ge(xn_out[s], 16 * HALF)

        @block.scalar
        def _(act):
            act.dma_start(acc[0:T].rearrange("(a b) d -> a (b d)", a=P),
                          x.rearrange("(a b) d -> a (b d)", a=P)).then_inc(acc_set, 16)
            act.dma_start(acc[T:T + CAP].rearrange("(a b) d -> a (b d)", a=P),
                          x[0:CAP].rearrange("(a b) d -> a (b d)", a=P)).then_inc(acc_set, 16)
            with act.Fori(0, HALF) as i:
                for s in range(2):
                    act.wait_ge(ve_ready, 2 * i + s + 1)
                    nc.scalar.activation(sd[:], sd[:], ACT.Sqrt).then_inc(sd_ready, 1)
                    act.wait_ge(t_done, 2 * i + s + 1)
                    nc.scalar.copy(xt[s][:], ps_t[s][:]).then_inc(xt_ready, 1)

        @block.vector
        def _(dve):
            with dve.Fori(0, HALF) as i:
                ch = Count(dve, chain, 6 * i)
                for s in range(2):
                    b = 2 * i + s
                    dve.wait_ge(x_in[s], 16 * i + 16)
                    dve.wait_ge(xn_out[s], 16 * i)
                    normalise(nc, c, dve, ch, xb[s], stats, mv, sd, rstd, xn[s], sd_ready, b + 1,
                              ve_ready).then_inc(xn_ready, 1)
                    dve.wait_ge(l_done, b + 1)
                    nc.vector.tensor_copy(c["logits"][:, b + 1, :], ps_l[s][:]).then_inc(l_copied, 1)
                assert ch.n == 6

        @block.tensor
        def _(pe):
            pe.wait_ge(wg_in, 16)
            with pe.Fori(0, HALF) as i:
                for s in range(2):
                    b = 2 * i + s
                    pe.wait_ge(xn_ready, b + 1)
                    for k in range(KD):
                        for t in range(TPB):
                            last = nc.tensor.transpose(ps_t[s][:, k, t * P:(t + 1) * P],
                                                       xn[s][:, t, k * P:(k + 1) * P], c["ident"][:])
                    last.then_inc(t_done, 1)
                    pe.wait_ge(xt_ready, b + 1)
                    for t in range(TPB):
                        for k in range(KD):
                            last = nc.tensor.matmul(ps_l[s][:, t * E:(t + 1) * E], xt[s][:, k, t * P:(t + 1) * P],
                                                    c["wg"][:, k, :], start=(k == 0), stop=(k == KD - 1))
                    last.then_inc(l_done, 1)


def moe(nc, c, w_gate, w_down, table, acc, tag, decay_needed):
    with ExitStack() as ctx:
        def sb(name, shape, dt=F32):
            return ctx.enter_context(nc.sbuf_tensor(f"{tag}_{name}", shape, dt))

        def sem(name):
            return ctx.enter_context(nc.semaphore(f"{tag}_{name}"))

        def ps(name, shape):
            return ctx.enter_context(nc.psum_tensor(f"{tag}_{name}", shape, F32))

        slot_row = sb("slot_row", [P, NCOL + 2 * TPB], I32)
        slot_acc = sb("slot_acc", [P, NCOL], I32)
        wg_raw = sb("wg_raw", [P, KD, F])
        wd_raw = sb("wd_raw", [P, MF, D])
        wraw_in = sem("wraw_in")
        w_hi_ready, w_lo_ready = sem("w_hi_ready"), sem("w_lo_ready")
        rows_sent = sem("rows_sent")

        with ExitStack() as rctx:
            def rb(name, shape, dt=F32):
                return rctx.enter_context(nc.sbuf_tensor(f"{tag}_{name}", shape, dt))

            te = [P, NT, E]
            lg = c["logits"][:, 1:, :].rearrange("p b (t e) -> p (b t) e", e=E)
            eq, sc, l2, ex, lc = (rb(n, te) for n in ("eq", "sc", "l2", "ex", "lc"))
            mask = [rb(f"mask{i}", te) for i in range(2)]
            mask16 = [rb(f"mask16_{i}", te, BF16) for i in range(2)]
            m = [rb(f"m{i}", [P, NT]) for i in range(2)]
            rk = [rb(f"rk{i}", [P, NT]) for i in range(2)]
            z, g1, g2, dn, d2, loc, over = (rb(n, [P, NT]) for n in ("z", "top_g1", "top_g2", "dn", "d2", "loc", "over"))
            et = [P, E, NT]
            tot, inc, base = rb("tot", et), rb("inc", et), rb("base", et)
            total1 = rb("total1", [P, E, 1])
            sloti, ai, bi = rb("sloti", [P, NT], I32), rb("ai", [P, NT], I32), rb("bi", [P, NT], I32)
            cola = [rb(f"cola{i}", [P, NT]) for i in range(2)]
            colb = [rb(f"colb{i}", [P, NT]) for i in range(2)]
            meta = rb("meta", [P, NT, 4])
            NOH = 4
            oha = [rb(f"oha{i}", [P, P]) for i in range(NOH)]
            ohb = [rb(f"ohb{i}", [P, P]) for i in range(NOH)]
            tab, emp = rb("tab", [P, NCOL]), rb("emp", [P, NCOL])
            ps_before = [rctx.enter_context(nc.psum_tensor(f"{tag}_ps_before{i}", [P, E * NT], F32)) for i in range(2)]
            ps_tot = [rctx.enter_context(nc.psum_tensor(f"{tag}_ps_tot{i}", [P, E * NT], F32)) for i in range(2)]
            ps_tab = rctx.enter_context(nc.psum_tensor(f"{tag}_ps_tab", [P, NCOL], F32))

            def rs(name):
                return rctx.enter_context(nc.semaphore(f"{tag}_{name}"))

            chain, mask_ready, counted = rs("chain"), rs("mask_ready"), rs("counted")
            ex_in, ex_out, meta_ready, hot, placed = rs("ex_in"), rs("ex_out"), rs("meta_ready"), rs("hot"), rs("placed")
            if decay_needed:
                step = rb("step", [P, 2, PW], I32)
                step_f, power = rb("step_f", [P, 2, PW]), rb("power", [P, KD, 2, PW])
                dk_chain, gamma_in = rs("dk_chain"), rs("gamma_in")
            block = rctx.enter_context(nc.Block())
            over_e = lambda a: a[:].unsqueeze(2).to_broadcast(te)
            rank = c["rank"][:].unsqueeze(1).to_broadcast(te)

            @block.sync
            def _(sp):
                sp.dma_start(wg_raw[:], w_gate[0].rearrange("(k p) f -> p k f", p=P)).then_inc(wraw_in, 16)
                sp.dma_start(wd_raw[:], w_down[0].rearrange("(m p) d -> p m d", p=P)).then_inc(wraw_in, 16)
                sp.wait_ge(meta_ready, 1)
                with nc.allow_non_contiguous_dma(reason="four words beside each row"):
                    sp.dma_start(table[BLK:, D:ROW].rearrange("(t p) w -> p t w", p=P), meta[:]).then_inc(rows_sent, 16)
                sp.wait_ge(rows_sent, 16)
                sp.wait_ge(wraw_in, 32)

            if decay_needed:
                @block.gpsimd
                def _(pool):
                    for k in range(KD):
                        for h in range(HH):
                            pool.dma_start(c["gamma_col"][h * HD:(h + 1) * HD, k:k + 1],
                                           c["gamma_dram"][k * HH + h:k * HH + h + 1].unsqueeze(0)
                                           .to_broadcast([HD, 1])).then_inc(gamma_in, 16)
                    pool.wait_ge(gamma_in, 16 * H)
                    nc.gpsimd.iota(step[:, 0, :], [[PW, PW]], base=0, channel_multiplier=0)
                    nc.gpsimd.iota(step[:, 1, :], [[1, PW]], base=0, channel_multiplier=0).then_inc(dk_chain, 1)
                    pool.wait_ge(dk_chain, 1)
                    nc.gpsimd.tensor_copy(step_f[:], step[:]).then_inc(dk_chain, 1)
                    pool.wait_ge(dk_chain, 2)
                    for k in range(KD):
                        last = nc.gpsimd.tensor_tensor(
                            power[:, k], c["gamma_col"][:, k:k + 1].unsqueeze(2).to_broadcast([P, 2, PW]),
                            step_f[:], ALU.pow)
                    last.then_inc(dk_chain, 1)
                    pool.wait_ge(dk_chain, 3)
                    for k in range(KD):
                        nc.gpsimd.tensor_tensor(
                            c["decay"][:, k, :].rearrange("p (a b) -> p a b", b=PW),
                            power[:, k, 0, :].unsqueeze(2).to_broadcast([P, PW, PW]),
                            power[:, k, 1, :].unsqueeze(1).to_broadcast([P, PW, PW]), ALU.mult)

            @block.scalar
            def _(act):
                act.wait_ge(ex_in, 1)
                nc.scalar.activation(ex[:], ex[:], ACT.Exp).then_inc(ex_out, 1)
                nc.scalar.activation(g2[:], g2[:], ACT.Exp).then_inc(ex_out, 1)

            @block.vector
            def _(dve):
                ch = Count(dve, chain)
                src = lg
                for i in range(2):
                    ch.link(nc.vector.tensor_reduce(m[i][:], src, AX_X, ALU.max))
                    ch.link(nc.vector.tensor_tensor(eq[:], src, over_e(m[i]), ALU.is_equal))
                    ch.link(nc.vector.tensor_tensor(sc[:], eq[:], rank, ALU.mult))
                    ch.link(nc.vector.tensor_reduce(rk[i][:], sc[:], AX_X, ALU.max))
                    ch.link(nc.vector.tensor_tensor(mask[i][:], sc[:], over_e(rk[i]), ALU.is_equal))
                    nc.vector.tensor_copy(mask16[i][:], mask[i][:]).then_inc(mask_ready, 1)
                    if i == 0:
                        ch.link(nc.vector.scalar_tensor_tensor(l2[:], mask[0][:], NEG, lg, ALU.mult, ALU.add))
                        src = l2[:]
                ch.link(nc.vector.tensor_tensor(g2[:], m[1][:], m[0][:], ALU.subtract))
                nc.vector.tensor_tensor(ex[:], lg, over_e(m[0]), ALU.subtract).then_inc(ex_in, 1)
                dve.wait_ge(ex_out, 2)
                ch.link(nc.vector.tensor_reduce(z[:], ex[:], AX_X, ALU.add))
                ch.link(nc.vector.reciprocal(g1[:], z[:]))
                ch.link(nc.vector.tensor_tensor(g2[:], g2[:], g1[:], ALU.mult))
                ch.link(nc.vector.tensor_tensor(dn[:], g1[:], g2[:], ALU.add))
                ch.link(nc.vector.tensor_scalar(dn[:], dn[:], 1e-9, None, ALU.max))
                ch.link(nc.vector.reciprocal(d2[:], dn[:]))
                ch.link(nc.vector.tensor_scalar(d2[:], d2[:], 0.5, None, ALU.mult))
                nc.vector.tensor_tensor(meta[:, :, 0], g1[:], d2[:], ALU.mult)
                nc.vector.tensor_tensor(meta[:, :, 1], g2[:], d2[:], ALU.mult)
                nc.vector.tensor_scalar(meta[:, :, 2], rk[0][:], -1.0, float(E), ALU.mult, ALU.add)
                nc.vector.tensor_scalar(meta[:, :, 3], rk[1][:], -1.0, float(E), ALU.mult, ALU.add).then_inc(meta_ready, 1)
                dve.wait_ge(meta_ready, 1)
                for i in range(2):
                    dve.wait_ge(counted, i + 1)
                    tot_f = tot[:].rearrange("p e t -> p (e t)")
                    inc_f = inc[:].rearrange("p e t -> p (e t)")
                    ch.link(nc.vector.tensor_copy(tot_f, ps_tot[i][:]))
                    ch.link(nc.vector.tensor_tensor_scan(inc_f, c["restart"][:].rearrange("p e t -> p (e t)"),
                                                         tot_f, 0.0, ALU.mult, ALU.add))
                    ch.link(nc.vector.tensor_tensor(base[:], inc[:], tot[:], ALU.subtract))
                    if i == 1:
                        ch.link(nc.vector.tensor_tensor(base[:], base[:], total1[:].to_broadcast(et), ALU.add))
                    else:
                        ch.link(nc.vector.tensor_copy(total1[:], inc[:, :, NT - 1:NT]))
                    ch.link(nc.vector.tensor_tensor(base[:], base[:],
                                                    ps_before[i][:].rearrange("p (e t) -> p e t", e=E), ALU.add))
                    ch.link(nc.vector.tensor_tensor(lc[:], mask[i][:], base[:].rearrange("p e t -> p t e"), ALU.mult))
                    ch.link(nc.vector.tensor_reduce(loc[:], lc[:], AX_X, ALU.add))
                    ch.link(nc.vector.tensor_scalar(over[:], loc[:], float(CAP), float(NSLOT), ALU.is_ge, ALU.mult))
                    ch.link(nc.vector.tensor_tensor(loc[:], loc[:], over[:], ALU.add))
                    ch.link(nc.vector.scalar_tensor_tensor(loc[:], meta[:, :, 2 + i], float(CAP), loc[:],
                                                           ALU.mult, ALU.add))
                    ch.link(nc.vector.tensor_copy(sloti[:], loc[:]))
                    nc.vector.tensor_scalar(ai[:], sloti[:], 7, None, ALU.arith_shift_right)
                    ch.link(nc.vector.tensor_scalar(bi[:], sloti[:], P - 1, None, ALU.bitwise_and))
                    nc.vector.tensor_copy(cola[i][:], ai[:])
                    ch.link(nc.vector.tensor_copy(colb[i][:], bi[:]))
                for i in range(2):
                    for t in range(NT):
                        n = i * NT + t
                        s = n % NOH
                        if n >= NOH:
                            dve.wait_ge(placed, n - NOH + 1)
                        nc.vector.tensor_scalar(ohb[s][:], c["iota"][:], colb[i][:, t:t + 1], None, ALU.is_equal)
                        nc.vector.tensor_scalar(oha[s][:], c["iota"][:], cola[i][:, t:t + 1],
                                                c["token_id"][:, t:t + 1], ALU.is_equal, ALU.mult).then_inc(hot, 1)
                dve.wait_ge(placed, 2 * NT)
                ch.link(nc.vector.tensor_copy(tab[:], ps_tab[:]))
                ch.link(nc.vector.tensor_scalar(emp[:], tab[:], 0.0, None, ALU.is_equal))
                ch.link(nc.vector.tensor_tensor(emp[:], emp[:], c["dummy_row"][:], ALU.mult))
                ch.link(nc.vector.tensor_tensor(emp[:], emp[:], tab[:], ALU.add))
                ch.link(nc.vector.tensor_scalar(emp[:], emp[:], -1.0 - BLK, None, ALU.add))
                nc.vector.tensor_copy(slot_acc[:], emp[:])
                ch.link(nc.vector.tensor_scalar(tab[:], tab[:], -1.0, 0.0, ALU.add, ALU.max))
                nc.vector.tensor_copy(slot_row[:, 0:NCOL], tab[:])
                nc.vector.memset(slot_row[:, NCOL:], 0)

            @block.tensor
            def _(pe):
                for i in range(2):
                    pe.wait_ge(mask_ready, i + 1)
                    by_expert = mask16[i][:].rearrange("p t e -> p e t")
                    nc.tensor.matmul(ps_before[i][:], c["before"][:], by_expert, start=True, stop=True)
                    nc.tensor.matmul(ps_tot[i][:], c["ones"][:], by_expert, start=True, stop=True).then_inc(counted, 1)
                for n in range(2 * NT):
                    pe.wait_ge(hot, n + 1)
                    nc.tensor.matmul(ps_tab[:], ohb[n % NOH][:], oha[n % NOH][:], start=(n == 0),
                                     stop=(n == 2 * NT - 1)).then_inc(placed, 1)

        xg = [sb(f"xg{i}", [P, TPB, ROW]) for i in range(2)]
        xh = [sb(f"xh{i}", [P, KD, BLK], F32R) for i in range(2)]
        xl = [sb(f"xl{i}", [P, KD, BLK], F32R) for i in range(2)]
        g = [sb(f"gelu{i}", [P, BLK]) for i in range(2)]
        gh = [sb(f"gh{i}", [P, BLK], F32R) for i in range(2)]
        gl = [sb(f"gl{i}", [P, BLK], F32R) for i in range(2)]
        eot = [sb(f"eot{k}", [P, BLK]) for k in range(KD)]
        rows = [sb(f"rows{i}", [P, TPB, D]) for i in range(2)]
        wgh, wgl = sb("wgh", [P, KD, F], F32R), sb("wgl", [P, KD, F], F32R)
        wdh, wdl = sb("wdh", [P, MF, D], F32R), sb("wdl", [P, MF, D], F32R)
        both = sb("both", [P, TPB, 2])
        gate = [sb(f"gate{i}", [P, TPB]) for i in range(2)]
        expert = sb("expert", [P, 1])
        idx_row, idx_acc = sb("idx_row", [P, TPB], I32), sb("idx_acc", [P, TPB], I32)
        ps_in = ps("ps_in", [P, KD, BLK])
        ps_up = [ps(f"ps_up{i}", [P, BLK]) for i in range(2)]
        ps_dn = [ps(f"ps_dn{k}", [P, BLK]) for k in range(KD)]
        ps_out = ps("ps_out", [P, TPB, D])
        gathered = [sem(f"gathered{i}") for i in range(2)]
        in_t, xh_ready, xl_ready = sem("in_t"), sem("xh_ready"), sem("xl_ready")
        up_done, g_ready, gh_ready, gl_ready, dn_done = (sem(n) for n in ("up_done", "g_ready", "gh_ready", "gl_ready", "dn_done"))
        eot_ready = [sem(f"eot_ready{k}") for k in range(KD)]
        out_t, rows_ready, added, idx_set = sem("out_t"), sem("rows_ready"), sem("added"), sem("idx_set")
        chain2 = sem("chain2")
        block = ctx.enter_context(nc.Block())

        @block.sync
        def _(sp):
            def weights(e, n):
                sp.wait_ge(w_hi_ready, MF * n)
                sp.wait_ge(w_lo_ready, MF * n)
                sp.dma_start(wg_raw[:], w_gate[e].rearrange("(k p) f -> p k f", p=P)).then_inc(wraw_in, 16)
                sp.dma_start(wd_raw[:], w_down[e].rearrange("(m p) d -> p m d", p=P)).then_inc(wraw_in, 16)

            with sp.Fori(0, E - 1) as e:
                weights(e + 1, e + 1)
            weights(0, E)
            sp.wait_ge(wraw_in, 32 * (E + 1))

        @block.gpsimd
        def _(pool):
            def gather(s, n_col, n_prev):
                ins = nc.gpsimd.tensor_copy(idx_row[:], slot_row[:, n_col:n_col + TPB] if isinstance(n_col, int)
                                            else slot_row[:, bass.ds(n_col, TPB)])
                ins.then_inc(idx_set, 1)
                pool.wait_ge(idx_set, n_prev)
                step_past(pool, c["passed"])
                for t in range(TPB):
                    nc.gpsimd.indirect_dma_start(xg[s][:, t, :], None, table,
                                                 bass.IndirectOffsetOnAxis(ap=idx_row[:, t:t + 1], axis=0)
                                                 ).then_inc(gathered[s], 16)

            gather(0, 0, 1)
            pool.wait_ge(gathered[0], 16 * TPB)
            gather(1, TPB, 2)
            with pool.Fori(0, E) as e:
                for j in range(JB):
                    s = j % 2
                    pool.wait_ge(rows_ready, JB * e + j + 2)
                    pool.wait_ge(added, 16 * TPB * (JB * e + j))
                    nc.gpsimd.tensor_copy(idx_acc[:], slot_acc[:, bass.ds((JB * e + j) * TPB, TPB)]).then_inc(idx_set, 1)
                    pool.wait_ge(idx_set, 2 * (JB * e + j) + 3)
                    step_past(pool, c["passed"])
                    for t in range(TPB):
                        nc.gpsimd.indirect_dma_start(acc, bass.IndirectOffsetOnAxis(ap=idx_acc[:, t:t + 1], axis=0),
                                                     rows[s][:, t, :], None, compute_op=ALU.add).then_inc(added, 16)
                    pool.wait_ge(xl_ready, JB * e + j + 1)
                    pool.wait_ge(gathered[1 - s], 16 * TPB * (2 * e + (j + 1) // 2 + 1))
                    gather(s, (JB * e + j + 2) * TPB, 2 * (JB * e + j) + 4)
            pool.wait_ge(added, 16 * TPB * NBLK)
            for s in range(2):
                pool.wait_ge(gathered[s], 16 * TPB * (NBLK // 2 + 1))

        @block.scalar
        def _(act):
            def high(m):
                nc.scalar.copy(wgh[:, :, m * P:(m + 1) * P], wg_raw[:, :, m * P:(m + 1) * P])
                nc.scalar.copy(wdh[:, m, :], wd_raw[:, m, :]).then_inc(w_hi_ready, 1)

            act.wait_ge(wraw_in, 32)
            for m in range(MF):
                high(m)
            act.wait_ge(in_t, 1)
            nc.scalar.copy(xh[0][:], ps_in[:]).then_inc(xh_ready, 1)
            with act.Fori(0, E) as e:
                for j in range(JB):
                    n = JB * e + j
                    if j == JB - 1:
                        act.wait_ge(wraw_in, 32 * (e + 2))
                    for m in range(MF):
                        act.wait_ge(up_done, MF * n + m + 1)
                        nc.scalar.activation(g[m % 2][:], ps_up[m % 2][:], ACT.Gelu).then_inc(g_ready, 1)
                        if j == JB - 1 and m >= 2:
                            act.wait_ge(dn_done, MF * n + m - 1)
                            high(m - 2)
                        if m == MF - 1:
                            act.wait_ge(in_t, n + 2)
                            nc.scalar.copy(xh[(j + 1) % 2][:], ps_in[:]).then_inc(xh_ready, 1)
                    if j == JB - 1:
                        act.wait_ge(dn_done, MF * n + MF - 1)
                        high(MF - 2)
                    act.wait_ge(dn_done, MF * n + MF)
                    act.wait_ge(out_t, n + 1)
                    nc.scalar.copy(eot[0][:], ps_dn[0][:]).then_inc(eot_ready[0], 1)
                    if j == JB - 1:
                        high(MF - 1)

        @block.vector
        def _(dve):
            def low(m):
                nc.vector.tensor_tensor(wgl[:, :, m * P:(m + 1) * P], wg_raw[:, :, m * P:(m + 1) * P],
                                        wgh[:, :, m * P:(m + 1) * P].bitcast(F32), ALU.subtract)
                split_low(nc, wdl[:, m, :], wd_raw[:, m, :], wdh[:, m, :]).then_inc(w_lo_ready, 1)

            def slot_gates(s):
                ch.link(nc.vector.scalar_tensor_tensor(both[:], xg[s][:, :, D + 2:D + 4], expert[:],
                                                       xg[s][:, :, D:D + 2], ALU.is_equal, ALU.mult))
                ch.link(nc.vector.tensor_reduce(gate[s][:], both[:], AX_X, ALU.add))

            def rows_out(s):
                for t in range(TPB):
                    last = nc.vector.tensor_scalar(rows[s][:, t, :], ps_out[:, t, :], gate[s][:, t:t + 1], None, ALU.mult)
                last.then_inc(rows_ready, 1)

            ch = Count(dve, chain2)
            nc.vector.memset(eot[0][:], 0.0).then_inc(eot_ready[0], 1)
            nc.vector.memset(eot[1][:], 0.0).then_inc(eot_ready[1], 1)
            nc.vector.memset(gate[1][:], 0.0)
            ch.link(nc.vector.memset(expert[:], 0.0))
            for m in range(MF):
                dve.wait_ge(w_hi_ready, m + 1)
                low(m)
            dve.wait_ge(xh_ready, 1)
            slot_gates(0)
            split_low(nc, xl[0][:], ps_in[:], xh[0][:]).then_inc(xl_ready, 1)
            per = 2 * JB + 1
            start = ch.n
            with dve.Fori(0, E) as e:
                ch = Count(dve, chain2, per * e + start)
                for j in range(JB):
                    n = JB * e + j
                    for m in range(MF):
                        dve.wait_ge(g_ready, MF * n + m + 1)
                        nc.vector.tensor_copy(gh[m % 2][:], g[m % 2][:]).then_inc(gh_ready, 1)
                        dve.wait_ge(gh_ready, MF * n + m + 1)
                        split_low(nc, gl[m % 2][:], g[m % 2][:], gh[m % 2][:]).then_inc(gl_ready, 1)
                        if m == 1:
                            dve.wait_ge(out_t, n + 1)
                            rows_out((j + 1) % 2)
                        if j == JB - 1 and m >= 2:
                            dve.wait_ge(w_hi_ready, MF * (e + 1) + m - 1)
                            low(m - 2)
                    if j == JB - 1:
                        ch.link(nc.vector.tensor_scalar(expert[:], expert[:], 1.0, None, ALU.add))
                    dve.wait_ge(xh_ready, n + 2)
                    slot_gates((j + 1) % 2)
                    split_low(nc, xl[(j + 1) % 2][:], ps_in[:], xh[(j + 1) % 2][:]).then_inc(xl_ready, 1)
                    if j == JB - 1:
                        dve.wait_ge(w_hi_ready, MF * (e + 1) + MF - 1)
                        low(MF - 2)
                    dve.wait_ge(dn_done, MF * n + MF)
                    dve.wait_ge(out_t, n + 1)
                    nc.vector.tensor_copy(eot[1][:], ps_dn[1][:]).then_inc(eot_ready[1], 1)
                    if j == JB - 1:
                        dve.wait_ge(w_hi_ready, MF * (e + 1) + MF)
                        low(MF - 1)
                assert ch.n == per
            dve.wait_ge(out_t, NBLK + 1)
            rows_out((NBLK - 1) % 2)

        @block.tensor
        def _(pe):
            def turn_in(s):
                for k in range(KD):
                    for t in range(TPB):
                        last = nc.tensor.transpose(ps_in[:, k, t * P:(t + 1) * P], xg[s][:, t, k * P:(k + 1) * P],
                                                   c["ident"][:])
                last.then_inc(in_t, 1)

            def turn_out(n_before):
                pe.wait_ge(eot_ready[0], n_before)
                pe.wait_ge(eot_ready[1], n_before)
                for k in range(KD):
                    for t in range(TPB):
                        last = nc.tensor.transpose(ps_out[:, t, k * P:(k + 1) * P], eot[k][:, t * P:(t + 1) * P],
                                                   c["ident"][:])
                last.then_inc(out_t, 1)

            def up(m, s):
                for k in range(KD):
                    last = three(nc, ps_up[m % 2][:], wgh[:, k, m * P:(m + 1) * P], wgl[:, k, m * P:(m + 1) * P],
                                 xh[s][:, k, :], xl[s][:, k, :], k == 0, k == KD - 1)
                last.then_inc(up_done, 1)

            def down(m, n):
                pe.wait_ge(gl_ready, MF * n + m + 1)
                for k in range(KD):
                    last = three(nc, ps_dn[k][:], wdh[:, m, k * P:(k + 1) * P], wdl[:, m, k * P:(k + 1) * P],
                                 gh[m % 2][:], gl[m % 2][:], m == 0, m == MF - 1)
                last.then_inc(dn_done, 1)

            pe.wait_ge(gathered[0], 16 * TPB)
            turn_in(0)
            with pe.Fori(0, E) as e:
                for j in range(JB):
                    n = JB * e + j
                    s = j % 2
                    pe.wait_ge(xl_ready, n + 1)
                    for m in range(MF):
                        if j == 0:
                            pe.wait_ge(w_lo_ready, MF * e + m + 1)
                        up(m, s)
                        if m == 1:
                            pe.wait_ge(rows_ready, n)
                            turn_out(n + 1)
                        if m >= 1:
                            if m == MF - 1:
                                pe.wait_ge(gathered[1 - s], 16 * TPB * (2 * e + (j + 1) // 2 + 1))
                                turn_in(1 - s)
                            down(m - 1, n)
                    down(MF - 1, n)
            turn_out(NBLK + 1)


USES = (["kv0", "s00", "s01", "s02", "s03", "kv1", "s10", "s11", "s12", "s13", "y0", "kv2", "s20", "s21", "s22", "s23",
         "y1", "q0", "q1", "k0", "k1", "kv3", "s30", "s31", "s32", "s33", "y2", "y3"])
NW = 4
PER_BANK = len(USES) // NW


def attention(nc, c, acc, q_in, k_in, v_in, o_in, table, out):
    with ExitStack() as ctx:
        def sb(name, shape, dt=F32):
            return ctx.enter_context(nc.sbuf_tensor(f"a_{name}", shape, dt))

        def sem(name):
            return ctx.enter_context(nc.semaphore(f"a_{name}"))

        def ps(name, shape):
            return ctx.enter_context(nc.psum_tensor(f"a_{name}", shape, F32))

        def pair(name, shape, dt=F32):
            return [sb(f"{name}{i}", shape, dt) for i in range(2)]

        w_hi = {n: sb(f"w{n}h", [P, KD, D], F32R) for n in "qkvo"}
        w_lo = {n: sb(f"w{n}l", [P, KD, D], F32R) for n in "qkvo"}
        bq_c, bk_c = sb("bq_c", [P, KD]), sb("bk_c", [P, KD])
        bkv_r = sb("bkv_r", [P, 2 * D])
        bo_r = sb("bo_r", [P, D])
        xb, x2 = pair("xb", [P, TPB, D]), pair("x2", [P, TPB, D])
        xn, xn3 = sb("xn", [P, TPB, D]), sb("xn3", [P, TPB, D])
        xth, xtl = pair("xth", [P, KD, BLK], F32R), pair("xtl", [P, KD, BLK], F32R)
        xt3 = sb("xt3", [P, KD, BLK])
        qt, kt = pair("qt", [P, KD, BLK]), pair("kt", [P, KD, BLK])
        q2 = pair("q2", [P, 2, KD, BLK], F32R)
        kh, kl = pair("kh", [P, KD, BLK], F32R), pair("kl", [P, KD, BLK], F32R)
        qd = pair("qd", [P, 2, KD, HH, CH], F32R)
        ss = pair("ss", [P, H, CH])
        kv = pair("kv", [P, 2 * D])
        vx = pair("vx", [P, H, 2 * HD])
        oth, otl = pair("oth", [P, KD, CH], F32R), pair("otl", [P, KD, CH], F32R)
        state, fresh = pair("state", [P, KD, P]), sb("fresh", [P, KD, P])
        stats2, mv2, sd2, rs2 = sb("st2", [P, TPB, 6]), sb("mv2", [P, TPB, 2]), sb("sd2", [P, TPB]), sb("rs2", [P, TPB])
        stats3, mv3, sd3, rs3 = sb("st3", [P, TPB, 6]), sb("mv3", [P, TPB, 2]), sb("sd3", [P, TPB]), sb("rs3", [P, TPB])
        ps_t = ps("ps_t", [P, KD, BLK])
        ps_w = [ps(f"ps_w{i}", [P, BLK]) for i in range(NW)]
        ps_o = ps("ps_o", [P, KD, CH])
        ps_st = ps("ps_st", [P, KD, P])

        w_in, w_ready, zeroed = sem("w_in"), sem("w_ready"), sem("zeroed")
        chain = sem("chain")
        x_in, x2_out = [sem(f"x_in{i}") for i in range(2)], [sem(f"x2_out{i}") for i in range(2)]
        qd_in = [sem(f"qd_in{i}") for i in range(2)]
        full, free = [sem(f"full{i}") for i in range(NW)], [sem(f"free{i}") for i in range(NW)]
        ve2, sd2_ready, xn_ready, xr_ready = sem("ve2"), sem("sd2_s"), sem("xn_s"), sem("xr_s")
        ve3, sd3_ready, xn3_ready, xn3_out = sem("ve3"), sem("sd3_s"), sem("xn3_s"), sem("xn3_out")
        x_turned, xth_ready, xtl_ready = sem("x_turned"), sem("xth_s"), sem("xtl_s")
        qh_ready, q2_ready, kl_ready = sem("qh_s"), sem("q2_s"), sem("kl_s")
        vx_ready, o_done, oth_ready, otl_ready = (sem(n) for n in ("vx_s", "o_done", "oth_s", "otl_s"))
        st_done, st_added = sem("st_done"), sem("st_added")
        t3_done, xt3_ready, lg_done, lg_copied = (sem(n) for n in ("t3_done", "xt3_s", "lg_done", "lg_copied"))

        xv = acc[0:T + BLK].rearrange("(b i p) d -> b p i d", i=TPB, p=P)
        ov = out[0:T].rearrange("(b i p) d -> b p i d", i=TPB, p=P)
        tv = table[:, 0:D].rearrange("(b i p) d -> b p i d", i=TPB, p=P)
        RPB = S // BLK
        NC_ROW = S // CH

        def use(name, b):
            u = USES.index(name)
            return u % NW, PER_BANK * b + u // NW + 1

        def filled(eng, name, b):
            bank, n = use(name, b)
            eng.wait_ge(full[bank], n + 1)

        def emptied(eng, name, b):
            bank, n = use(name, b)
            eng.wait_ge(free[bank], n + 1)

        with ExitStack() as sctx:
            raw = {n: sctx.enter_context(nc.sbuf_tensor(f"a_raw{n}", [P, KD, D], F32)) for n in "qkvo"}
            block = sctx.enter_context(nc.Block())

            @block.sync
            def _(sp):
                for n, (w, _b) in zip("qkvo", (q_in, k_in, v_in, o_in)):
                    sp.dma_start(raw[n][:], w.rearrange("(k p) f -> p k f", p=P)).then_inc(w_in, 16)
                with nc.allow_non_contiguous_dma(reason="two columns of biases"):
                    sp.dma_start(bq_c[:], q_in[1].rearrange("(k p) -> p k", p=P)).then_inc(w_in, 16)
                    sp.dma_start(bk_c[:], k_in[1].rearrange("(k p) -> p k", p=P)).then_inc(w_in, 16)
                sp.dma_start(bkv_r[:, D:], v_in[1].unsqueeze(0).to_broadcast([P, D])).then_inc(w_in, 16)
                sp.dma_start(bo_r[:], o_in[1].unsqueeze(0).to_broadcast([P, D])).then_inc(w_in, 16)
                sp.wait_ge(w_in, 16 * 8)

            @block.gpsimd
            def _(pool):
                nc.gpsimd.memset(qd[0][:].bitcast(F32), 0.0)
                nc.gpsimd.memset(vx[0][:], 0.0)
                nc.gpsimd.memset(vx[1][:], 0.0)
                nc.gpsimd.memset(x2[1][:], 1.0)
                nc.gpsimd.memset(bkv_r[:, 0:D], 0.0)

            @block.vector
            def _(dve):
                nc.vector.memset(qd[1][:].bitcast(F32), 0.0)
                dve.wait_ge(w_in, 16 * 8)
                for n in "qkvo":
                    last = nc.vector.tensor_copy(w_hi[n][:], raw[n][:])
                last.then_inc(w_ready, 1)
                dve.wait_ge(w_ready, 1)
                for n in "qkvo":
                    split_low(nc, w_lo[n][:], raw[n][:], w_hi[n][:])

        block = ctx.enter_context(nc.Block())

        @block.sync
        def _(sp):
            sp.dma_start(xb[0][:], xv[0]).then_inc(x_in[0], 16)
            with sp.Fori(0, B) as r:
                for s in range(RPB):
                    b = RPB * r + s
                    sp.wait_ge(q2_ready, b + 1)
                    for t in range(TPB):
                        if t == 1:
                            filled(sp, "kv0", b)
                        if t >= 2:
                            filled(sp, f"s{t - 2}3", b)
                        for h in range(HH):
                            rows = slice(h * HD, (h + 1) * HD)
                            sp.dma_start(qd[t % 2][rows, :, :, h, :].bitcast(F32),
                                         q2[s][rows, :, :, t * CH:(t + 1) * CH].bitcast(F32)).then_inc(qd_in[t % 2], 16)
                        if t == 0:
                            sp.wait_ge(free[use("y3", b)[0]], use("y3", b)[1] - PER_BANK + 1)
                            sp.dma_start(xb[1 - s][:], xv[b + 1]).then_inc(x_in[1 - s], 16)
            sp.wait_ge(x_in[0], 16 * (B + 1))

        @block.gpsimd
        def _(pool):
            def residual(s, n):
                pool.wait_ge(xn_ready, n)
                nc.gpsimd.tensor_tensor(xb[s][:], xb[s][:], bo_r[:].unsqueeze(1).to_broadcast([P, TPB, D]),
                                        ALU.add).then_inc(xr_ready, 1)

            def store_xn3(n):
                pool.wait_ge(xn3_ready, n + 1)
                pool.dma_start(tv[n], xn3[:]).then_inc(xn3_out, 16)

            residual(0, 1)
            with pool.Fori(0, B) as r:
                for s in range(RPB):
                    b = RPB * r + s
                    for t in range(TPB):
                        p = t % 2
                        emptied(pool, f"kv{t}", b)
                        step_past(pool, c["passed"])
                        v4 = kv[p][:, D:].rearrange("p (g e d) -> p g e d", e=2, d=HD)
                        x4 = vx[p][:].rearrange("p (g e) d -> p g e d", e=2)
                        nc.gpsimd.tensor_copy(x4[:, :, 0, 0:HD], v4[:, :, 0, :])
                        nc.gpsimd.tensor_copy(x4[:, :, 1, HD:], v4[:, :, 1, :]).then_inc(vx_ready, 1)
                        if t == 1:
                            residual(1 - s, b + 2)
                    store_xn3(b)
                    emptied(pool, "y3", b)
                    pool.dma_start(ov[b], x2[s][:]).then_inc(x2_out[s], 16)
            store_xn3(NB)
            pool.wait_ge(xn3_out, 16 * (NB + 1))
            for s in range(2):
                pool.wait_ge(x2_out[s], 16 * B)

        @block.scalar
        def _(act):
            def root(sd, ve, ready, n):
                act.wait_ge(ve, n)
                nc.scalar.activation(sd[:], sd[:], ACT.Sqrt).then_inc(ready, 1)

            def turned(s, n):
                act.wait_ge(x_turned, n)
                nc.scalar.copy(xth[s][:], ps_t[:]).then_inc(xth_ready, 1)

            def keys(s, banks, q_bank, q_n):
                for k, (bank, n) in enumerate(banks):
                    act.wait_ge(full[bank], n)
                    nc.scalar.activation(kt[s][:, k, :], ps_w[bank][:], ACT.Identity, bias=bk_c[:, k:k + 1])
                    nc.scalar.activation(kh[s][:, k, :], ps_w[bank][:], ACT.Identity,
                                         bias=bk_c[:, k:k + 1]).then_inc(free[bank], 1)
                act.wait_ge(free[q_bank], q_n)
                nc.scalar.copy(q2[s][:, 0], qt[s][:]).then_inc(qh_ready, 1)

            def heads(t, q):
                act.wait_ge(o_done, q + 1)
                nc.scalar.copy(oth[t % 2][:], ps_o[:]).then_inc(oth_ready, 1)

            def rows3(n):
                act.wait_ge(t3_done, n)
                nc.scalar.copy(xt3[:], ps_t[:]).then_inc(xt3_ready, 1)

            root(sd2, ve2, sd2_ready, 1)
            turned(0, 1)
            keys(0, [(2, 1), (3, 1)], 1, 1)
            with act.Fori(0, B) as r:
                for s in range(RPB):
                    b = RPB * r + s
                    root(sd2, ve2, sd2_ready, b + 2)
                    heads(0, TPB * b)
                    root(sd3, ve3, sd3_ready, b + 1)
                    turned(1 - s, b + 2)
                    heads(1, TPB * b + 1)
                    keys(1 - s, [(bank, n + 1) for bank, n in (use("k0", b), use("k1", b))],
                         use("q1", b)[0], use("q1", b)[1] + 1)
                    rows3(b + 1)
                    heads(2, TPB * b + 2)
                    heads(3, TPB * b + 3)
            root(sd3, ve3, sd3_ready, NB + 1)
            rows3(NB + 1)

        @block.vector
        def _(dve):
            def norm_in(ch, s, n_in, n):
                dve.wait_ge(x_in[s], n_in)
                dve.wait_ge(x_turned, n - 1)
                normalise(nc, c, dve, ch, xb[s], stats2, mv2, sd2, rs2, xn, sd2_ready, n, ve2).then_inc(xn_ready, 1)

            def norm_out(ch, s, n):
                dve.wait_ge(t3_done, n)
                dve.wait_ge(xn3_out, 16 * n)
                dve.wait_ge(free[use("y3", 0)[0]], PER_BANK * n + 1)
                normalise(nc, c, dve, ch, x2[s], stats3, mv3, sd3, rs3, xn3, sd3_ready, n + 1, ve3).then_inc(xn3_ready, 1)

            def turned(s, n):
                dve.wait_ge(xth_ready, n)
                split_low(nc, xtl[s][:], ps_t[:], xth[s][:]).then_inc(xtl_ready, 1)

            def queries(s, half, n, banks, k_bank, k_n):
                for k, (bank, m) in enumerate(banks):
                    dve.wait_ge(full[bank], m)
                    nc.vector.scalar_tensor_tensor(qt[s][:, k, :], ps_w[bank][:], bq_c[:, k:k + 1],
                                                   c["decay"][:, k, half * BLK:(half + 1) * BLK],
                                                   ALU.add, ALU.mult).then_inc(free[bank], 1)
                dve.wait_ge(free[k_bank], k_n)
                split_low(nc, kl[s][:], kt[s][:], kh[s][:]).then_inc(kl_ready, 1)
                dve.wait_ge(qh_ready, n)
                split_low(nc, q2[s][:, 1], qt[s][:], q2[s][:, 0]).then_inc(q2_ready, 1)

            def keys_values(t, b):
                bank, n = use(f"kv{t}", b)
                dve.wait_ge(full[bank], n + 1)
                nc.vector.tensor_tensor(kv[t % 2][:], ps_w[bank][:], bkv_r[:], ALU.add).then_inc(free[bank], 1)

            def scores(t, b):
                for g in range(4):
                    bank, n = use(f"s{t}{g}", b)
                    dve.wait_ge(full[bank], n + 1)
                    nc.vector.tensor_tensor(ss[t % 2][:, 4 * g:4 * g + 4, :],
                                            ps_w[bank][:].rearrange("p (h i) -> p h i", h=4),
                                            c["causal"][:].unsqueeze(1).to_broadcast([P, 4, CH]),
                                            ALU.mult).then_inc(free[bank], 1)

            def outputs(ch, t, b, s, r):
                q = TPB * b + t
                dve.wait_ge(oth_ready, q + 1)
                split_low(nc, otl[t % 2][:], ps_o[:], oth[t % 2][:]).then_inc(otl_ready, 1)
                i = TPB * s + t
                if i < NC_ROW - 1:
                    dve.wait_ge(st_done, (NC_ROW - 1) * r + i + 1)
                    mask = c["head_mask"][:].unsqueeze(1).to_broadcast([P, KD, P])
                    if i == 0:
                        nc.vector.tensor_tensor(state[0][:], ps_st[:], mask, ALU.mult).then_inc(st_added, 1)
                    else:
                        ch.link(nc.vector.tensor_tensor(fresh[:], ps_st[:], mask, ALU.mult))
                        nc.vector.tensor_tensor(state[i % 2][:], fresh[:], state[(i - 1) % 2][:],
                                                ALU.add).then_inc(st_added, 1)

            def projected(t, b, s, r):
                bank, n = use(f"y{t}", b)
                dve.wait_ge(full[bank], n + 1)
                if t == 0:
                    dve.wait_ge(xr_ready, b + 1)
                    dve.wait_ge(x2_out[s], 16 * r)
                nc.vector.tensor_tensor(x2[s][:, t, :], ps_w[bank][:, 0:D], xb[s][:, t, :],
                                        ALU.add).then_inc(free[bank], 1)

            ch = Count(dve, chain)
            norm_in(ch, 0, 16, 1)
            turned(0, 1)
            queries(0, 0, 1, [(0, 1), (1, 1)], 3, 1)
            start, per = ch.n, 2 * 6 + NC_ROW - 2
            with dve.Fori(0, B) as r:
                ch = Count(dve, chain, per * r + start)
                for s in range(RPB):
                    b = RPB * r + s
                    keys_values(0, b)
                    scores(0, b)
                    norm_in(ch, 1 - s, 16 * (r + 1 + s), b + 2)
                    keys_values(1, b)
                    scores(1, b)
                    outputs(ch, 0, b, s, r)
                    projected(0, b, s, r)
                    norm_out(ch, 1 - s, b)
                    keys_values(2, b)
                    scores(2, b)
                    turned(1 - s, b + 2)
                    outputs(ch, 1, b, s, r)
                    projected(1, b, s, r)
                    queries(1 - s, 1 - s, b + 2, [(bank, n + 1) for bank, n in (use("q0", b), use("q1", b))],
                            use("k1", b)[0], use("k1", b)[1] + 1)
                    keys_values(3, b)
                    scores(3, b)
                    dve.wait_ge(lg_done, b + 1)
                    nc.vector.tensor_copy(c["logits"][:, b, :], ps_t[:, 0, 0:TPB * E]).then_inc(lg_copied, 1)
                    outputs(ch, 2, b, s, r)
                    projected(2, b, s, r)
                    outputs(ch, 3, b, s, r)
                    projected(3, b, s, r)
                assert ch.n == per
            ch = Count(dve, chain, per * B + start)
            norm_out(ch, 1, NB)
            dve.wait_ge(lg_done, NB + 1)
            nc.vector.tensor_copy(c["logits"][:, NB, :], ps_t[:, 0, 0:TPB * E])

        @block.tensor
        def _(pe):
            def turn(src):
                for k in range(KD):
                    for t in range(TPB):
                        last = nc.tensor.transpose(ps_t[:, k, t * P:(t + 1) * P], src[:, t, k * P:(k + 1) * P],
                                                   c["ident"][:])
                return last

            def project(name, k, s, bank):
                for j in range(KD):
                    cols = slice(k * P, (k + 1) * P)
                    last = three(nc, ps_w[bank][:], w_hi[name][:, j, cols], w_lo[name][:, j, cols],
                                 xth[s][:, j, :], xtl[s][:, j, :], j == 0, j == KD - 1)
                last.then_inc(full[bank], 1)

            def take(name, b):
                bank, n = use(name, b)
                pe.wait_ge(free[bank], n)
                return bank

            def keys_values(t, b, s):
                bank = take(f"kv{t}", b)
                pos = slice(t * CH, (t + 1) * CH)
                for k in range(KD):
                    nc.tensor.transpose(ps_w[bank][:, k * P:(k + 1) * P], kt[s][:, k, pos], c["ident"][:])
                for k in range(KD):
                    last = three(nc, ps_w[bank][:, D:], xth[s][:, k, pos], xtl[s][:, k, pos],
                                 w_hi["v"][:, k, :], w_lo["v"][:, k, :], k == 0, k == KD - 1)
                last.then_inc(full[bank], 1)

            def scores(t, b, s):
                pe.wait_ge(qd_in[t % 2], 16 * HH * (2 * b + t // 2 + 1))
                pos = slice(t * CH, (t + 1) * CH)
                for g in range(4):
                    bank = take(f"s{t}{g}", b)
                    k, hs = g // 2, slice(4 * (g % 2), 4 * (g % 2) + 4)
                    last = three(nc, ps_w[bank][:], kh[s][:, k, pos], kl[s][:, k, pos],
                                 qd[t % 2][:, 0, k, hs, :], qd[t % 2][:, 1, k, hs, :], True, True)
                    last.then_inc(full[bank], 1)

            def outputs(t, b, s, r):
                q, i, p = TPB * b + t, TPB * s + t, t % 2
                emptied(pe, f"s{t}3", b)
                pe.wait_ge(vx_ready, q + 1)
                pe.wait_ge(otl_ready, q)
                if i > 0:
                    pe.wait_ge(st_added, (NC_ROW - 1) * r + i)
                for k in range(KD):
                    if i > 0:
                        nc.tensor.matmul(ps_o[:, k, :], state[(i - 1) % 2][:, k, :], qt[s][:, k, t * CH:(t + 1) * CH],
                                         start=True, stop=False, skip_group_check=True)
                    for odd in range(2):
                        for g in range(HH // 2):
                            h = HH * k + 2 * g + odd
                            last = nc.tensor.matmul(ps_o[32 * g:32 * g + 32, k, :], vx[p][:, h, :], ss[p][:, h, :],
                                                    start=(i == 0 and odd == 0), stop=(odd == 1), skip_group_check=True)
                last.then_inc(o_done, 1)
                if i < NC_ROW - 1:
                    for k in range(KD):
                        last = nc.tensor.matmul(ps_st[:, k, :], kv[p][:, k * P:(k + 1) * P],
                                                kv[p][:, D + k * P:D + (k + 1) * P], start=True, stop=True)
                    last.then_inc(st_done, 1)

            def result(t, b):
                pe.wait_ge(otl_ready, TPB * b + t + 1)
                bank = take(f"y{t}", b)
                for k in range(KD):
                    last = three(nc, ps_w[bank][:, 0:D], oth[t % 2][:, k, :], otl[t % 2][:, k, :],
                                 w_hi["o"][:, k, :], w_lo["o"][:, k, :], k == 0, k == KD - 1)
                last.then_inc(full[bank], 1)

            def turn_rows3(n):
                pe.wait_ge(xn3_ready, n)
                turn(xn3).then_inc(t3_done, 1)

            def logits(n):
                pe.wait_ge(xt3_ready, n)
                for t in range(TPB):
                    for k in range(KD):
                        last = nc.tensor.matmul(ps_t[:, 0, t * E:(t + 1) * E], xt3[:, k, t * P:(t + 1) * P],
                                                c["wg"][:, k, :], start=(k == 0), stop=(k == KD - 1))
                last.then_inc(lg_done, 1)

            pe.wait_ge(xn_ready, 1)
            turn(xn).then_inc(x_turned, 1)
            pe.wait_ge(xtl_ready, 1)
            for bank, (name, k) in enumerate((("q", 0), ("q", 1), ("k", 0), ("k", 1))):
                project(name, k, 0, bank)
            with pe.Fori(0, B) as r:
                for s in range(RPB):
                    b = RPB * r + s
                    pe.wait_ge(kl_ready, b + 1)
                    keys_values(0, b, s)
                    scores(0, b, s)
                    keys_values(1, b, s)
                    scores(1, b, s)
                    outputs(0, b, s, r)
                    result(0, b)
                    pe.wait_ge(lg_copied, b)
                    pe.wait_ge(xn_ready, b + 2)
                    turn(xn).then_inc(x_turned, 1)
                    keys_values(2, b, s)
                    scores(2, b, s)
                    outputs(1, b, s, r)
                    result(1, b)
                    pe.wait_ge(xtl_ready, b + 2)
                    for name, k in (("q", 0), ("q", 1), ("k", 0), ("k", 1)):
                        project(name, k, 1 - s, take(f"{name}{k}", b))
                    turn_rows3(b + 1)
                    keys_values(3, b, s)
                    scores(3, b, s)
                    logits(b + 1)
                    outputs(2, b, s, r)
                    result(2, b)
                    outputs(3, b, s, r)
                    result(3, b)
            turn_rows3(NB + 1)
            logits(NB + 1)


def macaron(nc, x, wqt, bq, wkt, bk, wvt, bv, wot, bo, gamma, wg, w_gate, w_down, out, phases=4):
    with ExitStack() as ctx:
        def sb(name, shape, dt=F32):
            return ctx.enter_context(nc.sbuf_tensor(name, shape, dt))

        c = {
            "ident": sb("ident", [P, P]), "causal": sb("causal", [P, P]), "before": sb("before", [P, P], BF16),
            "ones": sb("ones", [P, P], BF16), "iota": sb("iota", [P, P]), "token_id": sb("token_id", [P, NT]),
            "dummy_row": sb("dummy_row", [P, NCOL]), "rank": sb("rank", [P, E]),
            "restart": sb("restart", [P, E, NT]), "head_mask": sb("head_mask", [P, P]),
            "passed": ctx.enter_context(nc.semaphore("passed")), "decay": sb("decay", [P, KD, S]), "gamma_col": sb("gamma_col", [P, KD]), "gamma_dram": gamma,
            "wg": sb("wg", [P, KD, E]), "logits": sb("logits", [P, NB + 1, TPB * E]), "wg_dram": wg,
        }
        table = nc.dram_tensor("dispatch_rows", (BLK + T, ROW), F32, kind="Internal").ap()
        acc = nc.dram_tensor("after_moe1", (T + CAP, D), F32, kind="Internal").ap()
        if phases == 1:
            acc = out
        build_constants(nc, c)
        route_first(nc, c, x, table, acc)
        moe(nc, c, w_gate, w_down, table, acc, "f1", True)
        if phases > 1:
            attention(nc, c, acc, (wqt, bq), (wkt, bk), (wvt, bv), (wot, bo), table, out)
        if phases > 3:
            moe(nc, c, w_gate, w_down, table, out, "f2", False)


def kernel(**inputs):
    import numpy as np
    from concourse import bacc
    from concourse.bass_utils import run_bass_kernel_spmd

    given = {n.removeprefix("L0_"): np.asarray(a) for n, a in inputs.items()}
    laid = {"x": given["attn_x"].reshape(T, D)}
    for n in "qkvo":
        laid[f"w{n}"] = given[f"attn_W{n}"].T
        laid[f"b{n}"] = given[f"attn_b{n}"]
    laid["gamma"] = given["attn_gamma"]
    laid["wg"] = given["ffn_wg"]
    laid["w_gate"] = given["ffn_w_gate"]
    laid["w_down"] = given["ffn_w_down"]
    nc = bacc.Bacc("TRN2", target_bir_lowering=False, num_devices=1)
    arrays, args = {}, []
    for n, a in laid.items():
        arrays[f"in_{n}"] = np.ascontiguousarray(a)
        args.append(nc.dram_tensor(f"in_{n}", a.shape, F32, kind="ExternalInput").ap())
    args.append(nc.dram_tensor("out_rows", (T + CAP, D), F32, kind="ExternalOutput").ap())
    macaron(nc, *args)
    got = run_bass_kernel_spmd(nc, [arrays], core_ids=[0]).results[0]["out_rows"]
    return got[:T].reshape(B, S, D)
```

```python
from contextlib import ExitStack

import concourse.bass as bass
from concourse import mybir

F32 = mybir.dt.float32
F32R = mybir.dt.float32r
BF16 = mybir.dt.bfloat16
I32 = mybir.dt.int32
ALU = mybir.AluOpType
ACT = mybir.ActivationFunctionType
AX_X = mybir.AxisListType.X

P = 128
B, S, D = 8, 1024, 256
T = B * S
NT = T // P
E, F = 8, 1024
CAP = 2 * T // E
NSLOT = E * CAP
NCOL = NSLOT // P
TPB = 4
TURN = 4
BLK = TPB * P
NB = NT // TPB
JB = CAP // BLK
NBLK = E * JB
KD = D // P
MF = F // P
ROW = D + 4
EPS = 1e-5
H = 16
HD = D // H
HH = H // KD
CH = 128
NEG = -3.0e38
PW = 32
assert PW * PW == S


class Count:

    def __init__(self, eng, sem, base=0):
        self.eng, self.sem, self.base, self.n = eng, sem, base, 0

    def link(self, ins):
        self.n += 1
        ins.then_inc(self.sem, 1)
        self.eng.wait_ge(self.sem, self.base + self.n)


def step_past(eng, passed):
    eng.sem_inc(passed, 1)


def split_low(nc, out, full, high):
    return nc.vector.tensor_tensor(out, full, high.bitcast(F32), ALU.subtract)


def three(nc, out, ah, al, bh, bl, first, final):
    nc.tensor.matmul(out, ah, bh, start=first, stop=False)
    nc.tensor.matmul(out, al, bh, start=False, stop=False)
    return nc.tensor.matmul(out, ah, bl, start=False, stop=final)


def build_constants(nc, c):
    with ExitStack() as ctx:
        made = ctx.enter_context(nc.semaphore("const_made"))
        chain = ctx.enter_context(nc.semaphore("const_chain"))
        iota_p = ctx.enter_context(nc.sbuf_tensor("iota_p", [P, 1], I32))
        iota_c = ctx.enter_context(nc.sbuf_tensor("iota_c", [P, P], I32))
        iota_id = ctx.enter_context(nc.sbuf_tensor("iota_id", [P, NT], I32))
        iota_dm = ctx.enter_context(nc.sbuf_tensor("iota_dm", [P, E, NCOL // E], I32))
        tri = ctx.enter_context(nc.sbuf_tensor("tri_f32", [P, P], F32))
        block = ctx.enter_context(nc.Block())

        @block.gpsimd
        def _(pool):
            nc.gpsimd.iota(iota_c[:], [[1, P]], base=0, channel_multiplier=0).then_inc(made, 1)
            nc.gpsimd.iota(iota_id[:], [[P, NT]], base=BLK + 1, channel_multiplier=1).then_inc(made, 1)
            nc.gpsimd.iota(iota_dm[:], [[0, E], [P, NCOL // E]], base=T + BLK + 1, channel_multiplier=1).then_inc(made, 1)
            ch = Count(pool, chain)
            ch.link(nc.gpsimd.memset(c["ident"][:], 0.0))
            nc.gpsimd.affine_select(out=c["ident"][:], in_=c["ident"][:], compare_op=ALU.not_equal, fill=1.0,
                                    base=0, pattern=[[-1, P]], channel_multiplier=1).then_inc(made, 1)
            ch.link(nc.gpsimd.memset(c["causal"][:], 1.0))
            nc.gpsimd.affine_select(out=c["causal"][:], in_=c["causal"][:], compare_op=ALU.is_ge, fill=0.0,
                                    base=0, pattern=[[1, P]], channel_multiplier=-1).then_inc(made, 1)
            ch.link(nc.gpsimd.memset(tri[:], 1.0))
            nc.gpsimd.affine_select(out=tri[:], in_=tri[:], compare_op=ALU.is_gt, fill=0.0,
                                    base=0, pattern=[[1, P]], channel_multiplier=-1).then_inc(made, 1)
            hm = c["head_mask"][:].rearrange("p (h d) -> p h d", d=HD)
            ch.link(nc.gpsimd.memset(c["head_mask"][:], 1.0))
            ch.link(nc.gpsimd.affine_select(out=hm, in_=hm, compare_op=ALU.is_ge, fill=0.0, base=0,
                                            pattern=[[-HD, HH], [0, HD]], channel_multiplier=1))
            nc.gpsimd.affine_select(out=hm, in_=hm, compare_op=ALU.is_ge, fill=0.0, base=HD - 1,
                                    pattern=[[HD, HH], [0, HD]], channel_multiplier=-1).then_inc(made, 1)

        @block.vector
        def _(dve):
            dve.wait_ge(made, 7)
            nc.vector.tensor_copy(c["iota"][:], iota_c[:])
            nc.vector.tensor_copy(c["token_id"][:], iota_id[:])
            nc.vector.tensor_copy(c["dummy_row"][:], iota_dm[:].rearrange("p e c -> p (e c)"))
            nc.vector.tensor_copy(c["before"][:], tri[:])
            nc.vector.memset(c["ones"][:], 1.0)
            for e in range(E):
                nc.vector.memset(c["rank"][:, e:e + 1], float(E - e))
            nc.vector.memset(c["restart"][:, :, 0:1], 0.0)
            nc.vector.memset(c["restart"][:, :, 1:NT], 1.0)


def statistics(nc, c, dve, ch, x, stats, mv, sd, ve_ready, tiles):
    for i in range(tiles):
        last = nc.vector.bn_stats(stats[:, i, :], x[:, i, :])
    ch.link(last)
    step_past(dve, c["passed"])
    for i in range(tiles):
        last = nc.vector.bn_aggr(mv[:, i, :], stats[:, i, :])
    ch.link(last)
    nc.vector.tensor_scalar(sd[:], mv[:, :, 1], EPS, None, ALU.add).then_inc(ve_ready, 1)


def normalise(nc, dve, ch, x, mv, sd, rstd, out, sd_ready, sd_count, tiles):
    dve.wait_ge(sd_ready, sd_count)
    ch.link(nc.vector.reciprocal(rstd[:], sd[:]))
    for i in range(tiles):
        last = nc.vector.tensor_scalar(out[:, i, 0:D], x[:, i, :], mv[:, i, 0:1], rstd[:, i:i + 1],
                                       ALU.subtract, ALU.mult)
    return last


def route_first(nc, c, x, table):
    TPR = 2 * TPB
    NR = NT // TPR
    with ExitStack() as ctx:
        def sb(name, shape, dt=F32):
            return ctx.enter_context(nc.sbuf_tensor(name, shape, dt))

        def sem(name):
            return ctx.enter_context(nc.semaphore(name))

        xb = [sb(f"r_x{i}", [P, TPR, D]) for i in range(2)]
        xn = [sb(f"r_xn{i}", [P, TPR, D]) for i in range(2)]
        xt = [sb(f"r_xt{i}", [P, KD, BLK]) for i in range(2)]
        stats = [sb(f"r_stats{i}", [P, TPR, 6]) for i in range(2)]
        mv = [sb(f"r_mv{i}", [P, TPR, 2]) for i in range(2)]
        sd = [sb(f"r_sd{i}", [P, TPR]) for i in range(2)]
        rstd = [sb(f"r_rstd{i}", [P, TPR]) for i in range(2)]
        ps_t = [ctx.enter_context(nc.psum_tensor(f"r_ps_t{i}", [P, KD, BLK], F32)) for i in range(2)]
        ps_l = [ctx.enter_context(nc.psum_tensor(f"r_ps_l{i}", [P, TPB * E], F32)) for i in range(2)]
        x_in = [sem(f"r_x_in{i}") for i in range(2)]
        xn_out = [sem(f"r_xn_out{i}") for i in range(2)]
        wg_in = sem("r_wg_in")
        ve_ready, sd_ready, xn_ready = sem("r_ve"), sem("r_sd_s"), sem("r_xn_s")
        t_done, xt_ready, l_done, chain = sem("r_t"), sem("r_xt_s"), sem("r_l"), sem("r_chain")
        xv = x.rearrange("(b i p) d -> b p i d", i=TPR, p=P)
        tv = table[BLK:, 0:D].rearrange("(b i p) d -> b p i d", i=TPR, p=P)
        block = ctx.enter_context(nc.Block())
        HALF = NR // 2

        @block.sync
        def _(sp):
            for s in range(2):
                sp.dma_start(xb[s][:], xv[s]).then_inc(x_in[s], 16)
            sp.dma_start(c["wg"][:], c["wg_dram"].rearrange("(k p) e -> p k e", p=P)).then_inc(wg_in, 16)
            for s in range(2):
                sp.wait_ge(xn_out[s], 16)
            with sp.Fori(0, HALF - 1) as i:
                for s in range(2):
                    sp.wait_ge(xn_ready, 2 * i + s + 1)
                    sp.dma_start(xb[s][:], xv[2 * i + 2 + s]).then_inc(x_in[s], 16)

        @block.gpsimd
        def _(pool):
            pool.wait_ge(x_in[0], 16)
            pool.dma_start(table[0:BLK, 0:D].rearrange("(i p) d -> p i d", p=P),
                           xb[0][:, 0:TPB, :]).then_inc(xn_out[0], 16)
            pool.dma_start(table[0:BLK, D:ROW].rearrange("(i p) w -> p i w", p=P),
                           xb[0][:, 0:TPB, 0:ROW - D]).then_inc(xn_out[1], 16)
            with pool.Fori(0, HALF) as i:
                for s in range(2):
                    pool.wait_ge(xn_ready, 2 * i + s + 1)
                    pool.dma_start(tv[2 * i + s], xn[s][:]).then_inc(xn_out[s], 16)
            for s in range(2):
                pool.wait_ge(xn_out[s], 16 * (HALF + 1))

        @block.scalar
        def _(act):
            def root(s, n):
                act.wait_ge(ve_ready, n)
                nc.scalar.activation(sd[s][:], sd[s][:], ACT.Sqrt).then_inc(sd_ready, 1)

            def turned(h, n):
                act.wait_ge(t_done, n)
                nc.scalar.copy(xt[h][:], ps_t[h][:]).then_inc(xt_ready, 1)

            def logits(h, n, b):
                act.wait_ge(l_done, n)
                nc.scalar.copy(c["logits"][:, b + 1, :], ps_l[h][:])

            root(0, 1)
            with act.Fori(0, HALF) as i:
                for s in range(2):
                    n = 4 * i + 2 * s
                    if s == 0:
                        root(1, 2 * i + 2)
                    turned(0, n + 1)
                    turned(1, n + 2)
                    if s == 1:
                        root(0, 2 * i + 3)
                    logits(0, n + 1, n)
                    logits(1, n + 2, n + 1)

        @block.vector
        def _(dve):
            def stats_of(ch, s, n_in):
                dve.wait_ge(x_in[s], n_in)
                statistics(nc, c, dve, ch, xb[s], stats[s], mv[s], sd[s], ve_ready, TPR)

            ch = Count(dve, chain)
            stats_of(ch, 0, 16)
            start, per = ch.n, 6
            with dve.Fori(0, HALF - 1) as i:
                ch = Count(dve, chain, per * i + start)
                for s in range(2):
                    stats_of(ch, 1 - s, 16 * (i + 1 + s))
                    dve.wait_ge(xn_out[s], 16 * i + 16)
                    normalise(nc, dve, ch, xb[s], mv[s], sd[s], rstd[s], xn[s], sd_ready, 2 * i + s + 1,
                              TPR).then_inc(xn_ready, 1)
                assert ch.n == per
            ch = Count(dve, chain, per * (HALF - 1) + start)
            stats_of(ch, 1, 16 * HALF)
            for s in range(2):
                dve.wait_ge(xn_out[s], 16 * HALF)
                normalise(nc, dve, ch, xb[s], mv[s], sd[s], rstd[s], xn[s], sd_ready, NR - 1 + s,
                          TPR).then_inc(xn_ready, 1)
            nc.vector.memset(sd[0][:], 1.0).then_inc(ve_ready, 1)

        @block.tensor
        def _(pe):
            pe.wait_ge(wg_in, 16)
            with pe.Fori(0, HALF) as i:
                for s in range(2):
                    n = 4 * i + 2 * s
                    pe.wait_ge(xn_ready, 2 * i + s + 1)
                    for h in range(2):
                        for k in range(KD):
                            for t in range(TPB):
                                last = nc.tensor.transpose(ps_t[h][:, k, t * P:(t + 1) * P],
                                                           xn[s][:, h * TPB + t, k * P:(k + 1) * P], c["ident"][:])
                        last.then_inc(t_done, 1)
                    for h in range(2):
                        pe.wait_ge(xt_ready, n + h + 1)
                        for t in range(TPB):
                            for k in range(KD):
                                last = nc.tensor.matmul(ps_l[h][:, t * E:(t + 1) * E],
                                                        xt[h][:, k, t * P:(t + 1) * P],
                                                        c["wg"][:, k, :], start=(k == 0), stop=(k == KD - 1))
                        last.then_inc(l_done, 1)


def moe(nc, c, w_gate, w_down, table, acc, tag, acc_from):
    with ExitStack() as ctx:
        def sb(name, shape, dt=F32):
            return ctx.enter_context(nc.sbuf_tensor(f"{tag}_{name}", shape, dt))

        def sem(name):
            return ctx.enter_context(nc.semaphore(f"{tag}_{name}"))

        def ps(name, shape):
            return ctx.enter_context(nc.psum_tensor(f"{tag}_{name}", shape, F32))

        slot_row = sb("slot_row", [P, NCOL + 2 * TPB], I32)
        slot_acc = sb("slot_acc", [P, NCOL], I32)
        wg_raw = sb("wg_raw", [P, KD, F])
        wd_raw = sb("wd_raw", [P, MF, D])
        wraw_in = sem("wraw_in")
        w_hi_ready, w_lo_ready = sem("w_hi_ready"), sem("w_lo_ready")
        rows_sent, acc_set = sem("rows_sent"), sem("acc_set")

        with ExitStack() as rctx:
            def rb(name, shape, dt=F32):
                return rctx.enter_context(nc.sbuf_tensor(f"{tag}_{name}", shape, dt))

            te = [P, NT, E]
            lg = c["logits"][:, 1:, :].rearrange("p b (t e) -> p (b t) e", e=E)
            eq, sc, l2, ex, lc = (rb(n, te) for n in ("eq", "sc", "l2", "ex", "lc"))
            mask = [rb(f"mask{i}", te) for i in range(2)]
            mask16 = [rb(f"mask16_{i}", te, BF16) for i in range(2)]
            m = [rb(f"m{i}", [P, NT]) for i in range(2)]
            rk = [rb(f"rk{i}", [P, NT]) for i in range(2)]
            z, g1, g2, dn, d2, loc, over = (rb(n, [P, NT]) for n in ("z", "top_g1", "top_g2", "dn", "d2", "loc", "over"))
            et = [P, E, NT]
            tot, inc, base = rb("tot", et), rb("inc", et), rb("base", et)
            total1 = rb("total1", [P, E, 1])
            sloti, ai, bi = rb("sloti", [P, NT], I32), rb("ai", [P, NT], I32), rb("bi", [P, NT], I32)
            cola = [rb(f"cola{i}", [P, NT]) for i in range(2)]
            colb = [rb(f"colb{i}", [P, NT]) for i in range(2)]
            meta = rb("meta", [P, NT, 4])
            NOH = 4
            oha = [rb(f"oha{i}", [P, P]) for i in range(NOH)]
            ohb = [rb(f"ohb{i}", [P, P]) for i in range(NOH)]
            tab, emp = rb("tab", [P, NCOL]), rb("emp", [P, NCOL])
            ps_before = [rctx.enter_context(nc.psum_tensor(f"{tag}_ps_before{i}", [P, E * NT], F32)) for i in range(2)]
            ps_tot = [rctx.enter_context(nc.psum_tensor(f"{tag}_ps_tot{i}", [P, E * NT], F32)) for i in range(2)]
            ps_tab = rctx.enter_context(nc.psum_tensor(f"{tag}_ps_tab", [P, NCOL], F32))

            def rs(name):
                return rctx.enter_context(nc.semaphore(f"{tag}_{name}"))

            chain, mask_ready, counted = rs("chain"), rs("mask_ready"), rs("counted")
            ex_in, ex_out, meta_ready, hot, placed = rs("ex_in"), rs("ex_out"), rs("meta_ready"), rs("hot"), rs("placed")
            if acc_from is not None:
                step = rb("step", [P, 2, PW], I32)
                step_f, power = rb("step_f", [P, 2, PW]), rb("power", [P, KD, 2, PW])
                dk_chain, gamma_in = rs("dk_chain"), rs("gamma_in")
            block = rctx.enter_context(nc.Block())
            over_e = lambda a: a[:].unsqueeze(2).to_broadcast(te)
            rank = c["rank"][:].unsqueeze(1).to_broadcast(te)

            @block.sync
            def _(sp):
                sp.dma_start(wg_raw[:], w_gate[0].rearrange("(k p) f -> p k f", p=P)).then_inc(wraw_in, 16)
                sp.dma_start(wd_raw[:], w_down[0].rearrange("(m p) d -> p m d", p=P)).then_inc(wraw_in, 16)
                sp.wait_ge(meta_ready, 1)
                with nc.allow_non_contiguous_dma(reason="four words beside each row"):
                    sp.dma_start(table[BLK:, D:ROW].rearrange("(t p) w -> p t w", p=P), meta[:]).then_inc(rows_sent, 16)
                sp.wait_ge(rows_sent, 16)
                if acc_from is not None:
                    sp.dma_start(acc[0:T].rearrange("(a b) d -> a (b d)", a=P),
                                 acc_from.rearrange("(a b) d -> a (b d)", a=P)).then_inc(acc_set, 16)
                    sp.dma_start(acc[T:T + CAP].rearrange("(a b) d -> a (b d)", a=P),
                                 acc_from[0:CAP].rearrange("(a b) d -> a (b d)", a=P)).then_inc(acc_set, 16)
                    sp.wait_ge(acc_set, 32)
                sp.wait_ge(wraw_in, 32)

            if acc_from is not None:
                @block.gpsimd
                def _(pool):
                    for k in range(KD):
                        for h in range(HH):
                            pool.dma_start(c["gamma_col"][h * HD:(h + 1) * HD, k:k + 1],
                                           c["gamma_dram"][k * HH + h:k * HH + h + 1].unsqueeze(0)
                                           .to_broadcast([HD, 1])).then_inc(gamma_in, 16)
                    pool.wait_ge(gamma_in, 16 * H)
                    nc.gpsimd.iota(step[:, 0, :], [[PW, PW]], base=0, channel_multiplier=0)
                    nc.gpsimd.iota(step[:, 1, :], [[1, PW]], base=0, channel_multiplier=0).then_inc(dk_chain, 1)
                    pool.wait_ge(dk_chain, 1)
                    nc.gpsimd.tensor_copy(step_f[:], step[:]).then_inc(dk_chain, 1)
                    pool.wait_ge(dk_chain, 2)
                    for k in range(KD):
                        last = nc.gpsimd.tensor_tensor(
                            power[:, k], c["gamma_col"][:, k:k + 1].unsqueeze(2).to_broadcast([P, 2, PW]),
                            step_f[:], ALU.pow)
                    last.then_inc(dk_chain, 1)
                    pool.wait_ge(dk_chain, 3)
                    for k in range(KD):
                        nc.gpsimd.tensor_tensor(
                            c["decay"][:, k, :].rearrange("p (a b) -> p a b", b=PW),
                            power[:, k, 0, :].unsqueeze(2).to_broadcast([P, PW, PW]),
                            power[:, k, 1, :].unsqueeze(1).to_broadcast([P, PW, PW]), ALU.mult)

            @block.scalar
            def _(act):
                act.wait_ge(ex_in, 1)
                nc.scalar.activation(ex[:], ex[:], ACT.Exp).then_inc(ex_out, 1)
                nc.scalar.activation(g2[:], g2[:], ACT.Exp).then_inc(ex_out, 1)

            @block.vector
            def _(dve):
                ch = Count(dve, chain)
                src = lg
                for i in range(2):
                    ch.link(nc.vector.tensor_reduce(m[i][:], src, AX_X, ALU.max))
                    ch.link(nc.vector.tensor_tensor(eq[:], src, over_e(m[i]), ALU.is_equal))
                    ch.link(nc.vector.tensor_tensor(sc[:], eq[:], rank, ALU.mult))
                    ch.link(nc.vector.tensor_reduce(rk[i][:], sc[:], AX_X, ALU.max))
                    ch.link(nc.vector.tensor_tensor(mask[i][:], sc[:], over_e(rk[i]), ALU.is_equal))
                    nc.vector.tensor_copy(mask16[i][:], mask[i][:]).then_inc(mask_ready, 1)
                    if i == 0:
                        ch.link(nc.vector.scalar_tensor_tensor(l2[:], mask[0][:], NEG, lg, ALU.mult, ALU.add))
                        src = l2[:]
                ch.link(nc.vector.tensor_tensor(g2[:], m[1][:], m[0][:], ALU.subtract))
                nc.vector.tensor_tensor(ex[:], lg, over_e(m[0]), ALU.subtract).then_inc(ex_in, 1)
                dve.wait_ge(ex_out, 2)
                ch.link(nc.vector.tensor_reduce(z[:], ex[:], AX_X, ALU.add))
                ch.link(nc.vector.reciprocal(g1[:], z[:]))
                ch.link(nc.vector.tensor_tensor(g2[:], g2[:], g1[:], ALU.mult))
                ch.link(nc.vector.tensor_tensor(dn[:], g1[:], g2[:], ALU.add))
                ch.link(nc.vector.tensor_scalar(dn[:], dn[:], 1e-9, None, ALU.max))
                ch.link(nc.vector.reciprocal(d2[:], dn[:]))
                ch.link(nc.vector.tensor_scalar(d2[:], d2[:], 0.5, None, ALU.mult))
                nc.vector.tensor_tensor(meta[:, :, 0], g1[:], d2[:], ALU.mult)
                nc.vector.tensor_tensor(meta[:, :, 1], g2[:], d2[:], ALU.mult)
                nc.vector.tensor_scalar(meta[:, :, 2], rk[0][:], -1.0, float(E), ALU.mult, ALU.add)
                nc.vector.tensor_scalar(meta[:, :, 3], rk[1][:], -1.0, float(E), ALU.mult, ALU.add).then_inc(meta_ready, 1)
                dve.wait_ge(meta_ready, 1)
                for i in range(2):
                    dve.wait_ge(counted, i + 1)
                    tot_f = tot[:].rearrange("p e t -> p (e t)")
                    inc_f = inc[:].rearrange("p e t -> p (e t)")
                    ch.link(nc.vector.tensor_copy(tot_f, ps_tot[i][:]))
                    ch.link(nc.vector.tensor_tensor_scan(inc_f, c["restart"][:].rearrange("p e t -> p (e t)"),
                                                         tot_f, 0.0, ALU.mult, ALU.add))
                    ch.link(nc.vector.tensor_tensor(base[:], inc[:], tot[:], ALU.subtract))
                    if i == 1:
                        ch.link(nc.vector.tensor_tensor(base[:], base[:], total1[:].to_broadcast(et), ALU.add))
                    else:
                        ch.link(nc.vector.tensor_copy(total1[:], inc[:, :, NT - 1:NT]))
                    ch.link(nc.vector.tensor_tensor(base[:], base[:],
                                                    ps_before[i][:].rearrange("p (e t) -> p e t", e=E), ALU.add))
                    ch.link(nc.vector.tensor_tensor(lc[:], mask[i][:], base[:].rearrange("p e t -> p t e"), ALU.mult))
                    ch.link(nc.vector.tensor_reduce(loc[:], lc[:], AX_X, ALU.add))
                    ch.link(nc.vector.tensor_scalar(over[:], loc[:], float(CAP), float(NSLOT), ALU.is_ge, ALU.mult))
                    ch.link(nc.vector.tensor_tensor(loc[:], loc[:], over[:], ALU.add))
                    ch.link(nc.vector.scalar_tensor_tensor(loc[:], meta[:, :, 2 + i], float(CAP), loc[:],
                                                           ALU.mult, ALU.add))
                    ch.link(nc.vector.tensor_copy(sloti[:], loc[:]))
                    nc.vector.tensor_scalar(ai[:], sloti[:], 7, None, ALU.arith_shift_right)
                    ch.link(nc.vector.tensor_scalar(bi[:], sloti[:], P - 1, None, ALU.bitwise_and))
                    nc.vector.tensor_copy(cola[i][:], ai[:])
                    ch.link(nc.vector.tensor_copy(colb[i][:], bi[:]))
                for i in range(2):
                    for t in range(NT):
                        n = i * NT + t
                        s = n % NOH
                        if n >= NOH:
                            dve.wait_ge(placed, n - NOH + 1)
                        nc.vector.tensor_scalar(ohb[s][:], c["iota"][:], colb[i][:, t:t + 1], None, ALU.is_equal)
                        nc.vector.tensor_scalar(oha[s][:], c["iota"][:], cola[i][:, t:t + 1],
                                                c["token_id"][:, t:t + 1], ALU.is_equal, ALU.mult).then_inc(hot, 1)
                dve.wait_ge(placed, 2 * NT)
                ch.link(nc.vector.tensor_copy(tab[:], ps_tab[:]))
                ch.link(nc.vector.tensor_scalar(emp[:], tab[:], 0.0, None, ALU.is_equal))
                ch.link(nc.vector.tensor_tensor(emp[:], emp[:], c["dummy_row"][:], ALU.mult))
                ch.link(nc.vector.tensor_tensor(emp[:], emp[:], tab[:], ALU.add))
                ch.link(nc.vector.tensor_scalar(emp[:], emp[:], -1.0 - BLK, None, ALU.add))
                nc.vector.tensor_copy(slot_acc[:], emp[:])
                ch.link(nc.vector.tensor_scalar(tab[:], tab[:], -1.0, 0.0, ALU.add, ALU.max))
                nc.vector.tensor_copy(slot_row[:, 0:NCOL], tab[:])
                nc.vector.memset(slot_row[:, NCOL:], 0)

            @block.tensor
            def _(pe):
                for i in range(2):
                    pe.wait_ge(mask_ready, i + 1)
                    by_expert = mask16[i][:].rearrange("p t e -> p e t")
                    nc.tensor.matmul(ps_before[i][:], c["before"][:], by_expert, start=True, stop=True)
                    nc.tensor.matmul(ps_tot[i][:], c["ones"][:], by_expert, start=True, stop=True).then_inc(counted, 1)
                for n in range(2 * NT):
                    pe.wait_ge(hot, n + 1)
                    nc.tensor.matmul(ps_tab[:], ohb[n % NOH][:], oha[n % NOH][:], start=(n == 0),
                                     stop=(n == 2 * NT - 1)).then_inc(placed, 1)

        xg = [sb(f"xg{i}", [P, TPB, ROW]) for i in range(2)]
        xh = [sb(f"xh{i}", [P, KD, BLK], F32R) for i in range(2)]
        xl = [sb(f"xl{i}", [P, KD, BLK], F32R) for i in range(2)]
        g = [sb(f"gelu{i}", [P, BLK]) for i in range(2)]
        gh = [sb(f"gh{i}", [P, BLK], F32R) for i in range(2)]
        gl = [sb(f"gl{i}", [P, BLK], F32R) for i in range(2)]
        rows = [sb(f"rows{i}", [P, TPB, D]) for i in range(2)]
        wgh, wgl = sb("wgh", [P, KD, F], F32R), sb("wgl", [P, KD, F], F32R)
        wdh, wdl = sb("wdh", [P, MF, D], F32R), sb("wdl", [P, MF, D], F32R)
        both = sb("both", [P, TPB, 2])
        gate = [sb(f"gate{i}", [P, TPB]) for i in range(2)]
        expert = sb("expert", [P, 1])
        idx_row, idx_acc = sb("idx_row", [P, TPB], I32), sb("idx_acc", [P, TPB], I32)
        ps_in = ps("ps_in", [P, KD, BLK])
        ps_up = [ps(f"ps_up{i}", [P, BLK]) for i in range(2)]
        ps_out = [ps(f"ps_out{i}", [P, TPB, D]) for i in range(2)]
        gathered = [sem(f"gathered{i}") for i in range(2)]
        in_t, xh_ready, xl_ready = sem("in_t"), sem("xh_ready"), sem("xl_ready")
        up_done, g_ready, gh_ready, gl_ready, dn_done = (sem(n) for n in ("up_done", "g_ready", "gh_ready", "gl_ready", "dn_done"))
        rows_ready, added, idx_set = sem("rows_ready"), sem("added"), sem("idx_set")
        chain2 = sem("chain2")
        block = ctx.enter_context(nc.Block())

        @block.sync
        def _(sp):
            def weights(e, n):
                sp.wait_ge(w_hi_ready, MF * n)
                sp.wait_ge(w_lo_ready, MF * n)
                sp.dma_start(wg_raw[:], w_gate[e].rearrange("(k p) f -> p k f", p=P)).then_inc(wraw_in, 16)
                sp.dma_start(wd_raw[:], w_down[e].rearrange("(m p) d -> p m d", p=P)).then_inc(wraw_in, 16)

            with sp.Fori(0, E - 1) as e:
                weights(e + 1, e + 1)
            weights(0, E)
            sp.wait_ge(wraw_in, 32 * (E + 1))

        @block.gpsimd
        def _(pool):
            def gather(s, n_col, n_prev):
                ins = nc.gpsimd.tensor_copy(idx_row[:], slot_row[:, n_col:n_col + TPB] if isinstance(n_col, int)
                                            else slot_row[:, bass.ds(n_col, TPB)])
                ins.then_inc(idx_set, 1)
                pool.wait_ge(idx_set, n_prev)
                step_past(pool, c["passed"])
                for t in range(TPB):
                    nc.gpsimd.indirect_dma_start(xg[s][:, t, :], None, table,
                                                 bass.IndirectOffsetOnAxis(ap=idx_row[:, t:t + 1], axis=0)
                                                 ).then_inc(gathered[s], 16)

            gather(0, 0, 1)
            pool.wait_ge(gathered[0], 16 * TPB)
            gather(1, TPB, 2)
            with pool.Fori(0, E) as e:
                for j in range(JB):
                    n, s = JB * e + j, j % 2
                    pool.wait_ge(xl_ready, n + 1)
                    pool.wait_ge(gathered[1 - s], 16 * TPB * (2 * e + (j + 1) // 2 + 1))
                    gather(s, (n + 2) * TPB, 2 * n + 3)
                    pool.wait_ge(rows_ready, 2 * n + 2)
                    nc.gpsimd.tensor_copy(idx_acc[:], slot_acc[:, bass.ds(n * TPB, TPB)]).then_inc(idx_set, 1)
                    pool.wait_ge(idx_set, 2 * n + 4)
                    step_past(pool, c["passed"])
                    for t in range(TPB):
                        nc.gpsimd.indirect_dma_start(acc, bass.IndirectOffsetOnAxis(ap=idx_acc[:, t:t + 1], axis=0),
                                                     rows[s][:, t, :], None, compute_op=ALU.add).then_inc(added, 16)
                    pool.wait_ge(added, 16 * TPB * (n + 1))
            for s in range(2):
                pool.wait_ge(gathered[s], 16 * TPB * (NBLK // 2 + 1))

        @block.scalar
        def _(act):
            def high(m):
                nc.scalar.copy(wgh[:, :, m * P:(m + 1) * P], wg_raw[:, :, m * P:(m + 1) * P])
                nc.scalar.copy(wdh[:, m, :], wd_raw[:, m, :]).then_inc(w_hi_ready, 1)

            def gelu(s, n_up):
                act.wait_ge(up_done, n_up)
                nc.scalar.activation(g[s][:], ps_up[s][:], ACT.Gelu).then_inc(g_ready, 1)

            act.wait_ge(wraw_in, 32)
            for m in range(MF):
                high(m)
            act.wait_ge(in_t, 1)
            nc.scalar.copy(xh[0][:], ps_in[:]).then_inc(xh_ready, 1)
            gelu(0, 1)
            with act.Fori(0, E) as e:
                for j in range(JB):
                    n = JB * e + j
                    if j == JB - 1:
                        act.wait_ge(wraw_in, 32 * (e + 2))
                    for m in range(MF):
                        gelu((m + 1) % 2, MF * n + m + 2)
                        if j == JB - 1 and m >= 1:
                            act.wait_ge(dn_done, MF * n + m)
                            high(m - 1)
                        if m == TURN:
                            act.wait_ge(in_t, n + 2)
                            nc.scalar.copy(xh[(j + 1) % 2][:], ps_in[:]).then_inc(xh_ready, 1)
                    act.wait_ge(dn_done, MF * n + MF)
                    for t in range(TPB // 2):
                        last = nc.scalar.activation(rows[j % 2][:, t, :], ps_out[j % 2][:, t, :], ACT.Copy,
                                                    scale=gate[j % 2][:, t:t + 1])
                    last.then_inc(rows_ready, 1)
                    if j == JB - 1:
                        high(MF - 1)

        @block.vector
        def _(dve):
            def low(m):
                nc.vector.tensor_tensor(wgl[:, :, m * P:(m + 1) * P], wg_raw[:, :, m * P:(m + 1) * P],
                                        wgh[:, :, m * P:(m + 1) * P].bitcast(F32), ALU.subtract)
                split_low(nc, wdl[:, m, :], wd_raw[:, m, :], wdh[:, m, :]).then_inc(w_lo_ready, 1)

            def slot_gates(s):
                ch.link(nc.vector.scalar_tensor_tensor(both[:], xg[s][:, :, D + 2:D + 4], expert[:],
                                                       xg[s][:, :, D:D + 2], ALU.is_equal, ALU.mult))
                ch.link(nc.vector.tensor_reduce(gate[s][:], both[:], AX_X, ALU.add))

            def rows_out(s):
                for t in range(TPB // 2, TPB):
                    last = nc.vector.tensor_scalar(rows[s][:, t, :], ps_out[s][:, t, :], gate[s][:, t:t + 1], None, ALU.mult)
                last.then_inc(rows_ready, 1)

            def parts(s, n):
                dve.wait_ge(g_ready, n)
                nc.vector.tensor_copy(gh[s][:], g[s][:]).then_inc(gh_ready, 1)
                dve.wait_ge(gh_ready, n)
                split_low(nc, gl[s][:], g[s][:], gh[s][:]).then_inc(gl_ready, 1)

            ch = Count(dve, chain2)
            ch.link(nc.vector.memset(expert[:], 0.0))
            for m in range(MF):
                dve.wait_ge(w_hi_ready, m + 1)
                low(m)
            dve.wait_ge(xh_ready, 1)
            slot_gates(0)
            split_low(nc, xl[0][:], ps_in[:], xh[0][:]).then_inc(xl_ready, 1)
            per = 2 * JB + 1
            start = ch.n
            parts(0, 1)
            with dve.Fori(0, E) as e:
                ch = Count(dve, chain2, per * e + start)
                for j in range(JB):
                    n = JB * e + j
                    for m in range(MF):
                        parts((m + 1) % 2, MF * n + m + 2)
                        if j == JB - 1 and m >= 1:
                            dve.wait_ge(w_hi_ready, MF * (e + 1) + m)
                            low(m - 1)
                        if m == TURN:
                            if j == JB - 1:
                                ch.link(nc.vector.tensor_scalar(expert[:], expert[:], 1.0, None, ALU.add))
                            dve.wait_ge(xh_ready, n + 2)
                            slot_gates((j + 1) % 2)
                            split_low(nc, xl[(j + 1) % 2][:], ps_in[:], xh[(j + 1) % 2][:]).then_inc(xl_ready, 1)
                    dve.wait_ge(dn_done, MF * n + MF)
                    rows_out(j % 2)
                    if j == JB - 1:
                        dve.wait_ge(w_hi_ready, MF * (e + 1) + MF)
                        low(MF - 1)
                assert ch.n == per

        @block.tensor
        def _(pe):
            def turn_in(s):
                for k in range(KD):
                    for t in range(TPB):
                        last = nc.tensor.transpose(ps_in[:, k, t * P:(t + 1) * P], xg[s][:, t, k * P:(k + 1) * P],
                                                   c["ident"][:])
                last.then_inc(in_t, 1)

            def up(m, s):
                for k in range(KD):
                    last = three(nc, ps_up[m % 2][:], wgh[:, k, m * P:(m + 1) * P], wgl[:, k, m * P:(m + 1) * P],
                                 xh[s][:, k, :], xl[s][:, k, :], k == 0, k == KD - 1)
                last.then_inc(up_done, 1)

            def down(m, s, n):
                pe.wait_ge(gl_ready, MF * n + m + 1)
                for t in range(TPB):
                    slots = slice(t * P, (t + 1) * P)
                    last = three(nc, ps_out[s][:, t, :], gh[m % 2][:, slots], gl[m % 2][:, slots],
                                 wdh[:, m, :], wdl[:, m, :], m == 0 and t % 2 == 0, m == MF - 1 and t % 2 == 1)
                last.then_inc(dn_done, 1)

            pe.wait_ge(gathered[0], 16 * TPB)
            turn_in(0)
            pe.wait_ge(xl_ready, 1)
            pe.wait_ge(w_lo_ready, 1)
            up(0, 0)
            with pe.Fori(0, E) as e:
                for j in range(JB):
                    n = JB * e + j
                    s = j % 2
                    for m in range(MF):
                        if m == TURN:
                            pe.wait_ge(gathered[1 - s], 16 * TPB * (2 * e + (j + 1) // 2 + 1))
                            turn_in(1 - s)
                        if m + 1 < MF:
                            if j == 0:
                                pe.wait_ge(w_lo_ready, MF * e + m + 2)
                            up(m + 1, s)
                        else:
                            pe.wait_ge(xl_ready, n + 2)
                            if j == JB - 1:
                                pe.wait_ge(w_lo_ready, MF * e + MF + 1)
                            up(0, 1 - s)
                        down(m, s, n)


USES = (["kv0", "s00", "s01", "s02", "s03", "kv1", "s10", "s11", "s12", "s13", "y0", "kv2", "s20", "s21", "s22", "s23",
         "y1", "q0", "q1", "k0", "k1", "kv3", "s30", "s31", "s32", "s33", "y2", "y3"])
NW = 4
PER_BANK = len(USES) // NW


def attention(nc, c, acc, q_in, k_in, v_in, o_in, table, out):
    with ExitStack() as ctx:
        def sb(name, shape, dt=F32):
            return ctx.enter_context(nc.sbuf_tensor(f"a_{name}", shape, dt))

        def sem(name):
            return ctx.enter_context(nc.semaphore(f"a_{name}"))

        def ps(name, shape):
            return ctx.enter_context(nc.psum_tensor(f"a_{name}", shape, F32))

        def pair(name, shape, dt=F32):
            return [sb(f"{name}{i}", shape, dt) for i in range(2)]

        w_hi = {n: sb(f"w{n}h", [P, KD, D], F32R) for n in "qkvo"}
        w_lo = {n: sb(f"w{n}l", [P, KD, D], F32R) for n in "qkvo"}
        bq_c, bk_c = sb("bq_c", [P, KD]), sb("bk_c", [P, KD])
        bkv_r = sb("bkv_r", [P, 2 * D])
        bo_r = sb("bo_r", [P, D])
        xb, x2 = pair("xb", [P, TPB, D]), pair("x2", [P, TPB, D])
        xn, xn3 = sb("xn", [P, TPB, D]), sb("xn3", [P, TPB, D])
        xth, xtl = pair("xth", [P, KD, BLK], F32R), pair("xtl", [P, KD, BLK], F32R)
        xt3 = sb("xt3", [P, KD, BLK])
        qt, kt = pair("qt", [P, KD, BLK]), pair("kt", [P, KD, BLK])
        q2 = pair("q2", [P, 2, KD, BLK], F32R)
        kh, kl = pair("kh", [P, KD, BLK], F32R), pair("kl", [P, KD, BLK], F32R)
        qd = pair("qd", [P, 2, KD, HH, CH], F32R)
        ss = pair("ss", [P, H, CH])
        kv = pair("kv", [P, 2 * D])
        vx = pair("vx", [P, H, 2 * HD])
        oth, otl = pair("oth", [P, KD, CH], F32R), pair("otl", [P, KD, CH], F32R)
        state, fresh = pair("state", [P, KD, P]), sb("fresh", [P, KD, P])
        stats2, mv2, sd2, rs2 = sb("st2", [P, TPB, 6]), sb("mv2", [P, TPB, 2]), sb("sd2", [P, TPB]), sb("rs2", [P, TPB])
        stats3, mv3, sd3, rs3 = sb("st3", [P, TPB, 6]), sb("mv3", [P, TPB, 2]), sb("sd3", [P, TPB]), sb("rs3", [P, TPB])
        ps_t = ps("ps_t", [P, KD, BLK])
        ps_w = [ps(f"ps_w{i}", [P, BLK]) for i in range(NW)]
        ps_o = ps("ps_o", [P, KD, CH])
        ps_st = ps("ps_st", [P, KD, P])

        w_in, w_ready, zeroed = sem("w_in"), sem("w_ready"), sem("zeroed")
        chain = sem("chain")
        x_in, x2_out = [sem(f"x_in{i}") for i in range(2)], [sem(f"x2_out{i}") for i in range(2)]
        qd_in = [sem(f"qd_in{i}") for i in range(2)]
        full, free = [sem(f"full{i}") for i in range(NW)], [sem(f"free{i}") for i in range(NW)]
        ve2, sd2_ready, xn_ready, xr_ready = sem("ve2"), sem("sd2_s"), sem("xn_s"), sem("xr_s")
        ve3, sd3_ready, xn3_ready, xn3_out = sem("ve3"), sem("sd3_s"), sem("xn3_s"), sem("xn3_out")
        x_turned, xth_ready, xtl_ready = sem("x_turned"), sem("xth_s"), sem("xtl_s")
        qh_ready, q2_ready, kl_ready = sem("qh_s"), sem("q2_s"), sem("kl_s")
        vx_ready, o_done, oth_ready, otl_ready = (sem(n) for n in ("vx_s", "o_done", "oth_s", "otl_s"))
        st_done, st_added = sem("st_done"), sem("st_added")
        t3_done, xt3_ready, lg_done = (sem(n) for n in ("t3_done", "xt3_s", "lg_done"))

        xv = acc[0:T + BLK].rearrange("(b i p) d -> b p i d", i=TPB, p=P)
        ov = out[0:T + BLK].rearrange("(b i p) d -> b p i d", i=TPB, p=P)
        tv = table[:, 0:D].rearrange("(b i p) d -> b p i d", i=TPB, p=P)
        RPB = S // BLK
        NC_ROW = S // CH

        def use(name, b):
            u = USES.index(name)
            return u % NW, PER_BANK * b + u // NW + 1

        def filled(eng, name, b):
            bank, n = use(name, b)
            eng.wait_ge(full[bank], n + 1)

        def emptied(eng, name, b):
            bank, n = use(name, b)
            eng.wait_ge(free[bank], n + 1)

        with ExitStack() as sctx:
            raw = {n: sctx.enter_context(nc.sbuf_tensor(f"a_raw{n}", [P, KD, D], F32)) for n in "qkvo"}
            block = sctx.enter_context(nc.Block())

            @block.sync
            def _(sp):
                for n, (w, _b) in zip("qkvo", (q_in, k_in, v_in, o_in)):
                    sp.dma_start(raw[n][:], w.rearrange("(k p) f -> p k f", p=P)).then_inc(w_in, 16)
                with nc.allow_non_contiguous_dma(reason="two columns of biases"):
                    sp.dma_start(bq_c[:], q_in[1].rearrange("(k p) -> p k", p=P)).then_inc(w_in, 16)
                    sp.dma_start(bk_c[:], k_in[1].rearrange("(k p) -> p k", p=P)).then_inc(w_in, 16)
                sp.dma_start(bkv_r[:, D:], v_in[1].unsqueeze(0).to_broadcast([P, D])).then_inc(w_in, 16)
                sp.dma_start(bo_r[:], o_in[1].unsqueeze(0).to_broadcast([P, D])).then_inc(w_in, 16)
                sp.wait_ge(w_in, 16 * 8)

            @block.gpsimd
            def _(pool):
                nc.gpsimd.memset(qd[0][:].bitcast(F32), 0.0)
                nc.gpsimd.memset(vx[0][:], 0.0)
                nc.gpsimd.memset(vx[1][:], 0.0)
                nc.gpsimd.memset(x2[1][:], 1.0)
                nc.gpsimd.memset(bkv_r[:, 0:D], 0.0)

            @block.vector
            def _(dve):
                nc.vector.memset(qd[1][:].bitcast(F32), 0.0)
                dve.wait_ge(w_in, 16 * 8)
                for n in "qkvo":
                    last = nc.vector.tensor_copy(w_hi[n][:], raw[n][:])
                last.then_inc(w_ready, 1)
                dve.wait_ge(w_ready, 1)
                for n in "qkvo":
                    split_low(nc, w_lo[n][:], raw[n][:], w_hi[n][:])

        block = ctx.enter_context(nc.Block())

        @block.sync
        def _(sp):
            sp.dma_start(xb[0][:], xv[0]).then_inc(x_in[0], 16)
            with sp.Fori(0, B) as r:
                for s in range(RPB):
                    b = RPB * r + s
                    sp.wait_ge(q2_ready, b + 1)
                    for t in range(TPB):
                        if t == 1:
                            filled(sp, "kv0", b)
                        if t >= 2:
                            filled(sp, f"s{t - 2}3", b)
                        for h in range(HH):
                            rows = slice(h * HD, (h + 1) * HD)
                            sp.dma_start(qd[t % 2][rows, :, :, h, :].bitcast(F32),
                                         q2[s][rows, :, :, t * CH:(t + 1) * CH].bitcast(F32)).then_inc(qd_in[t % 2], 16)
                        if t == 0:
                            sp.wait_ge(free[use("y3", b)[0]], use("y3", b)[1] - PER_BANK + 1)
                            sp.dma_start(xb[1 - s][:], xv[b + 1]).then_inc(x_in[1 - s], 16)
            sp.wait_ge(x_in[0], 16 * (B + 1))

        @block.gpsimd
        def _(pool):
            def residual(s, n):
                pool.wait_ge(xn_ready, n)
                nc.gpsimd.tensor_tensor(xb[s][:], xb[s][:], bo_r[:].unsqueeze(1).to_broadcast([P, TPB, D]),
                                        ALU.add).then_inc(xr_ready, 1)

            def store_xn3(n):
                pool.wait_ge(xn3_ready, n + 1)
                pool.dma_start(tv[n], xn3[:]).then_inc(xn3_out, 16)

            pool.dma_start(ov[NB], x2[1][:]).then_inc(x2_out[1], 16)
            residual(0, 1)
            with pool.Fori(0, B) as r:
                for s in range(RPB):
                    b = RPB * r + s
                    for t in range(TPB):
                        p = t % 2
                        emptied(pool, f"kv{t}", b)
                        step_past(pool, c["passed"])
                        v4 = kv[p][:, D:].rearrange("p (g e d) -> p g e d", e=2, d=HD)
                        x4 = vx[p][:].rearrange("p (g e) d -> p g e d", e=2)
                        nc.gpsimd.tensor_copy(x4[:, :, 0, 0:HD], v4[:, :, 0, :])
                        nc.gpsimd.tensor_copy(x4[:, :, 1, HD:], v4[:, :, 1, :]).then_inc(vx_ready, 1)
                        if t == 1:
                            residual(1 - s, b + 2)
                    store_xn3(b)
                    emptied(pool, "y3", b)
                    pool.dma_start(ov[b], x2[s][:]).then_inc(x2_out[s], 16)
            store_xn3(NB)
            pool.wait_ge(xn3_out, 16 * (NB + 1))
            for s in range(2):
                pool.wait_ge(x2_out[s], 16 * (B + s))

        @block.scalar
        def _(act):
            def root(sd, ve, ready, n):
                act.wait_ge(ve, n)
                nc.scalar.activation(sd[:], sd[:], ACT.Sqrt).then_inc(ready, 1)

            def turned(s, n):
                act.wait_ge(x_turned, n)
                nc.scalar.copy(xth[s][:], ps_t[:]).then_inc(xth_ready, 1)

            def keys(s, banks, q_bank, q_n):
                for k, (bank, n) in enumerate(banks):
                    act.wait_ge(full[bank], n)
                    nc.scalar.activation(kt[s][:, k, :], ps_w[bank][:], ACT.Identity, bias=bk_c[:, k:k + 1])
                    nc.scalar.activation(kh[s][:, k, :], ps_w[bank][:], ACT.Identity,
                                         bias=bk_c[:, k:k + 1]).then_inc(free[bank], 1)
                act.wait_ge(free[q_bank], q_n)
                nc.scalar.copy(q2[s][:, 0], qt[s][:]).then_inc(qh_ready, 1)

            def heads(t, q):
                act.wait_ge(o_done, q + 1)
                nc.scalar.copy(oth[t % 2][:], ps_o[:]).then_inc(oth_ready, 1)

            def rows3(n):
                act.wait_ge(t3_done, n)
                nc.scalar.copy(xt3[:], ps_t[:]).then_inc(xt3_ready, 1)

            root(sd2, ve2, sd2_ready, 1)
            turned(0, 1)
            keys(0, [(2, 1), (3, 1)], 1, 1)
            with act.Fori(0, B) as r:
                for s in range(RPB):
                    b = RPB * r + s
                    root(sd2, ve2, sd2_ready, b + 2)
                    heads(0, TPB * b)
                    root(sd3, ve3, sd3_ready, b + 1)
                    turned(1 - s, b + 2)
                    heads(1, TPB * b + 1)
                    keys(1 - s, [(bank, n + 1) for bank, n in (use("k0", b), use("k1", b))],
                         use("q1", b)[0], use("q1", b)[1] + 1)
                    rows3(b + 1)
                    heads(2, TPB * b + 2)
                    heads(3, TPB * b + 3)
            root(sd3, ve3, sd3_ready, NB + 1)
            rows3(NB + 1)

        @block.vector
        def _(dve):
            first_in = 16

            def norm_in(ch, s, n_in, n):
                dve.wait_ge(x_in[s], n_in)
                if n_in is not first_in:
                    dve.wait_ge(x_turned, n - 1)
                statistics(nc, c, dve, ch, xb[s], stats2, mv2, sd2, ve2, TPB)
                normalise(nc, dve, ch, xb[s], mv2, sd2, rs2, xn, sd2_ready, n, TPB).then_inc(xn_ready, 1)

            def norm_out(ch, s, n):
                dve.wait_ge(free[use("y3", 0)[0]], PER_BANK * n + 1)
                statistics(nc, c, dve, ch, x2[s], stats3, mv3, sd3, ve3, TPB)
                normalise(nc, dve, ch, x2[s], mv3, sd3, rs3, xn3, sd3_ready, n + 1, TPB).then_inc(xn3_ready, 1)

            def turned(s, n):
                dve.wait_ge(xth_ready, n)
                split_low(nc, xtl[s][:], ps_t[:], xth[s][:]).then_inc(xtl_ready, 1)

            def queries(s, half, n, banks, k_bank, k_n):
                for k, (bank, m) in enumerate(banks):
                    dve.wait_ge(full[bank], m)
                    nc.vector.scalar_tensor_tensor(qt[s][:, k, :], ps_w[bank][:], bq_c[:, k:k + 1],
                                                   c["decay"][:, k, half * BLK:(half + 1) * BLK],
                                                   ALU.add, ALU.mult).then_inc(free[bank], 1)
                dve.wait_ge(free[k_bank], k_n)
                split_low(nc, kl[s][:], kt[s][:], kh[s][:]).then_inc(kl_ready, 1)
                dve.wait_ge(qh_ready, n)
                split_low(nc, q2[s][:, 1], qt[s][:], q2[s][:, 0]).then_inc(q2_ready, 1)

            def keys_values(t, b):
                bank, n = use(f"kv{t}", b)
                dve.wait_ge(full[bank], n + 1)
                nc.vector.tensor_tensor(kv[t % 2][:], ps_w[bank][:], bkv_r[:], ALU.add).then_inc(free[bank], 1)

            def scores(t, b):
                for g in range(4):
                    bank, n = use(f"s{t}{g}", b)
                    dve.wait_ge(full[bank], n + 1)
                    nc.vector.tensor_tensor(ss[t % 2][:, 4 * g:4 * g + 4, :],
                                            ps_w[bank][:].rearrange("p (h i) -> p h i", h=4),
                                            c["causal"][:].unsqueeze(1).to_broadcast([P, 4, CH]),
                                            ALU.mult).then_inc(free[bank], 1)

            def outputs(ch, t, b, s, r):
                q = TPB * b + t
                dve.wait_ge(oth_ready, q + 1)
                split_low(nc, otl[t % 2][:], ps_o[:], oth[t % 2][:]).then_inc(otl_ready, 1)
                i = TPB * s + t
                if i < NC_ROW - 1:
                    dve.wait_ge(st_done, (NC_ROW - 1) * r + i + 1)
                    mask = c["head_mask"][:].unsqueeze(1).to_broadcast([P, KD, P])
                    if i == 0:
                        nc.vector.tensor_tensor(state[0][:], ps_st[:], mask, ALU.mult).then_inc(st_added, 1)
                    else:
                        ch.link(nc.vector.tensor_tensor(fresh[:], ps_st[:], mask, ALU.mult))
                        nc.vector.tensor_tensor(state[i % 2][:], fresh[:], state[(i - 1) % 2][:],
                                                ALU.add).then_inc(st_added, 1)

            def buffers_left(b, s, r):
                dve.wait_ge(xn3_out, 16 * (b + 1))
                dve.wait_ge(x2_out[1 - s], 16 * (r + 1))

            def projected(t, b, s, r):
                bank, n = use(f"y{t}", b)
                dve.wait_ge(full[bank], n + 1)
                if t == 0:
                    dve.wait_ge(xr_ready, b + 1)
                nc.vector.tensor_tensor(x2[s][:, t, :], ps_w[bank][:, 0:D], xb[s][:, t, :],
                                        ALU.add).then_inc(free[bank], 1)

            ch = Count(dve, chain)
            norm_in(ch, 0, first_in, 1)
            turned(0, 1)
            queries(0, 0, 1, [(0, 1), (1, 1)], 3, 1)
            start, per = ch.n, 2 * 6 + NC_ROW - 2
            with dve.Fori(0, B) as r:
                ch = Count(dve, chain, per * r + start)
                for s in range(RPB):
                    b = RPB * r + s
                    keys_values(0, b)
                    scores(0, b)
                    norm_in(ch, 1 - s, 16 * (r + 1 + s), b + 2)
                    keys_values(1, b)
                    scores(1, b)
                    outputs(ch, 0, b, s, r)
                    projected(0, b, s, r)
                    norm_out(ch, 1 - s, b)
                    keys_values(2, b)
                    scores(2, b)
                    turned(1 - s, b + 2)
                    outputs(ch, 1, b, s, r)
                    projected(1, b, s, r)
                    queries(1 - s, 1 - s, b + 2, [(bank, n + 1) for bank, n in (use("q0", b), use("q1", b))],
                            use("k1", b)[0], use("k1", b)[1] + 1)
                    keys_values(3, b)
                    scores(3, b)
                    dve.wait_ge(lg_done, b + 1)
                    nc.vector.tensor_copy(c["logits"][:, b, :], ps_t[:, 0, 0:TPB * E])
                    outputs(ch, 2, b, s, r)
                    projected(2, b, s, r)
                    outputs(ch, 3, b, s, r)
                    projected(3, b, s, r)
                    buffers_left(b, s, r)
                assert ch.n == per
            ch = Count(dve, chain, per * B + start)
            norm_out(ch, 1, NB)
            dve.wait_ge(lg_done, NB + 1)
            nc.vector.tensor_copy(c["logits"][:, NB, :], ps_t[:, 0, 0:TPB * E])

        @block.tensor
        def _(pe):
            def turn(src):
                for k in range(KD):
                    for t in range(TPB):
                        last = nc.tensor.transpose(ps_t[:, k, t * P:(t + 1) * P], src[:, t, k * P:(k + 1) * P],
                                                   c["ident"][:])
                return last

            def project(name, k, s, bank):
                for j in range(KD):
                    cols = slice(k * P, (k + 1) * P)
                    last = three(nc, ps_w[bank][:], w_hi[name][:, j, cols], w_lo[name][:, j, cols],
                                 xth[s][:, j, :], xtl[s][:, j, :], j == 0, j == KD - 1)
                last.then_inc(full[bank], 1)

            def take(name, b):
                bank, n = use(name, b)
                pe.wait_ge(free[bank], n)
                return bank

            def keys_values(t, b, s):
                bank = take(f"kv{t}", b)
                pos = slice(t * CH, (t + 1) * CH)
                for k in range(KD):
                    nc.tensor.transpose(ps_w[bank][:, k * P:(k + 1) * P], kt[s][:, k, pos], c["ident"][:])
                for k in range(KD):
                    last = three(nc, ps_w[bank][:, D:], xth[s][:, k, pos], xtl[s][:, k, pos],
                                 w_hi["v"][:, k, :], w_lo["v"][:, k, :], k == 0, k == KD - 1)
                last.then_inc(full[bank], 1)

            def scores(t, b, s):
                pe.wait_ge(qd_in[t % 2], 16 * HH * (2 * b + t // 2 + 1))
                pos = slice(t * CH, (t + 1) * CH)
                for g in range(4):
                    bank = take(f"s{t}{g}", b)
                    k, hs = g // 2, slice(4 * (g % 2), 4 * (g % 2) + 4)
                    last = three(nc, ps_w[bank][:], kh[s][:, k, pos], kl[s][:, k, pos],
                                 qd[t % 2][:, 0, k, hs, :], qd[t % 2][:, 1, k, hs, :], True, True)
                    last.then_inc(full[bank], 1)

            def outputs(t, b, s, r):
                q, i, p = TPB * b + t, TPB * s + t, t % 2
                emptied(pe, f"s{t}3", b)
                pe.wait_ge(vx_ready, q + 1)
                if i > 0:
                    pe.wait_ge(st_added, (NC_ROW - 1) * r + i)
                for k in range(KD):
                    if i > 0:
                        nc.tensor.matmul(ps_o[:, k, :], state[(i - 1) % 2][:, k, :], qt[s][:, k, t * CH:(t + 1) * CH],
                                         start=True, stop=False, skip_group_check=True)
                    for odd in range(2):
                        for g in range(HH // 2):
                            h = HH * k + 2 * g + odd
                            last = nc.tensor.matmul(ps_o[32 * g:32 * g + 32, k, :], vx[p][:, h, :], ss[p][:, h, :],
                                                    start=(i == 0 and odd == 0), stop=(odd == 1), skip_group_check=True)
                last.then_inc(o_done, 1)
                if i < NC_ROW - 1:
                    for k in range(KD):
                        last = nc.tensor.matmul(ps_st[:, k, :], kv[p][:, k * P:(k + 1) * P],
                                                kv[p][:, D + k * P:D + (k + 1) * P], start=True, stop=True)
                    last.then_inc(st_done, 1)

            def result(t, b):
                pe.wait_ge(otl_ready, TPB * b + t + 1)
                bank = take(f"y{t}", b)
                for k in range(KD):
                    last = three(nc, ps_w[bank][:, 0:D], oth[t % 2][:, k, :], otl[t % 2][:, k, :],
                                 w_hi["o"][:, k, :], w_lo["o"][:, k, :], k == 0, k == KD - 1)
                last.then_inc(full[bank], 1)

            def turn_rows3(n):
                pe.wait_ge(xn3_ready, n)
                turn(xn3).then_inc(t3_done, 1)

            def logits(n):
                pe.wait_ge(xt3_ready, n)
                for t in range(TPB):
                    for k in range(KD):
                        last = nc.tensor.matmul(ps_t[:, 0, t * E:(t + 1) * E], xt3[:, k, t * P:(t + 1) * P],
                                                c["wg"][:, k, :], start=(k == 0), stop=(k == KD - 1))
                last.then_inc(lg_done, 1)

            pe.wait_ge(xn_ready, 1)
            turn(xn).then_inc(x_turned, 1)
            pe.wait_ge(xtl_ready, 1)
            for bank, (name, k) in enumerate((("q", 0), ("q", 1), ("k", 0), ("k", 1))):
                project(name, k, 0, bank)
            with pe.Fori(0, B) as r:
                for s in range(RPB):
                    b = RPB * r + s
                    pe.wait_ge(kl_ready, b + 1)
                    keys_values(0, b, s)
                    scores(0, b, s)
                    keys_values(1, b, s)
                    scores(1, b, s)
                    outputs(0, b, s, r)
                    result(0, b)
                    pe.wait_ge(xn_ready, b + 2)
                    turn(xn).then_inc(x_turned, 1)
                    keys_values(2, b, s)
                    scores(2, b, s)
                    outputs(1, b, s, r)
                    result(1, b)
                    pe.wait_ge(xtl_ready, b + 2)
                    for name, k in (("q", 0), ("q", 1), ("k", 0), ("k", 1)):
                        project(name, k, 1 - s, take(f"{name}{k}", b))
                    turn_rows3(b + 1)
                    keys_values(3, b, s)
                    scores(3, b, s)
                    logits(b + 1)
                    outputs(2, b, s, r)
                    result(2, b)
                    outputs(3, b, s, r)
                    result(3, b)
            turn_rows3(NB + 1)
            logits(NB + 1)


def macaron(nc, x, wqt, bq, wkt, bk, wvt, bv, wot, bo, gamma, wg, w_gate, w_down, out, phases=4):
    with ExitStack() as ctx:
        def sb(name, shape, dt=F32):
            return ctx.enter_context(nc.sbuf_tensor(name, shape, dt))

        c = {
            "ident": sb("ident", [P, P]), "causal": sb("causal", [P, P]), "before": sb("before", [P, P], BF16),
            "ones": sb("ones", [P, P], BF16), "iota": sb("iota", [P, P]), "token_id": sb("token_id", [P, NT]),
            "dummy_row": sb("dummy_row", [P, NCOL]), "rank": sb("rank", [P, E]),
            "restart": sb("restart", [P, E, NT]), "head_mask": sb("head_mask", [P, P]),
            "passed": ctx.enter_context(nc.semaphore("passed")), "decay": sb("decay", [P, KD, S]), "gamma_col": sb("gamma_col", [P, KD]), "gamma_dram": gamma,
            "wg": sb("wg", [P, KD, E]), "logits": sb("logits", [P, NB + 1, TPB * E]), "wg_dram": wg,
        }
        table = nc.dram_tensor("dispatch_rows", (BLK + T, ROW), F32, kind="Internal").ap()
        acc = nc.dram_tensor("after_moe1", (T + CAP, D), F32, kind="Internal").ap()
        if phases == 1:
            acc = out
        build_constants(nc, c)
        route_first(nc, c, x, table)
        moe(nc, c, w_gate, w_down, table, acc, "f1", x)
        if phases > 1:
            attention(nc, c, acc, (wqt, bq), (wkt, bk), (wvt, bv), (wot, bo), table, out)
        if phases > 3:
            moe(nc, c, w_gate, w_down, table, out, "f2", None)


def kernel(**inputs):
    import numpy as np
    from concourse import bacc
    from concourse.bass_utils import run_bass_kernel_spmd

    given = {n.removeprefix("L0_"): np.asarray(a) for n, a in inputs.items()}
    laid = {"x": given["attn_x"].reshape(T, D)}
    for n in "qkvo":
        laid[f"w{n}"] = given[f"attn_W{n}"].T
        laid[f"b{n}"] = given[f"attn_b{n}"]
    laid["gamma"] = given["attn_gamma"]
    laid["wg"] = given["ffn_wg"]
    laid["w_gate"] = given["ffn_w_gate"]
    laid["w_down"] = given["ffn_w_down"]
    nc = bacc.Bacc("TRN2", target_bir_lowering=False, num_devices=1)
    arrays, args = {}, []
    for n, a in laid.items():
        arrays[f"in_{n}"] = np.ascontiguousarray(a)
        args.append(nc.dram_tensor(f"in_{n}", a.shape, F32, kind="ExternalInput").ap())
    args.append(nc.dram_tensor("out_rows", (T + CAP, D), F32, kind="ExternalOutput").ap())
    macaron(nc, *args)
    got = run_bass_kernel_spmd(nc, [arrays], core_ids=[0]).results[0]["out_rows"]
    return got[:T].reshape(B, S, D)
```

```python
from contextlib import ExitStack

import concourse.bass as bass
from concourse import mybir

F32 = mybir.dt.float32
F32R = mybir.dt.float32r
BF16 = mybir.dt.bfloat16
I32 = mybir.dt.int32
ALU = mybir.AluOpType
ACT = mybir.ActivationFunctionType
AX_X = mybir.AxisListType.X

P = 128
B, S, D = 8, 1024, 256
T = B * S
NT = T // P
E, F = 8, 1024
CAP = 2 * T // E
NSLOT = E * CAP
NCOL = NSLOT // P
TPB = 4
TURN = 4
BLK = TPB * P
NB = NT // TPB
JB = CAP // BLK
NBLK = E * JB
KD = D // P
MF = F // P
MW = 6
ROW = D + 4
EPS = 1e-5
H = 16
HD = D // H
HH = H // KD
CH = 128
NEG = -3.0e38
PW = 32
assert PW * PW == S


class Count:

    def __init__(self, eng, sem, base=0):
        self.eng, self.sem, self.base, self.n = eng, sem, base, 0

    def link(self, ins):
        self.n += 1
        ins.then_inc(self.sem, 1)
        self.eng.wait_ge(self.sem, self.base + self.n)


def step_past(eng, passed):
    eng.sem_inc(passed, 1)


def split_low(nc, out, full, high):
    return nc.vector.tensor_tensor(out, full, high.bitcast(F32), ALU.subtract)


def three(nc, out, ah, al, bh, bl, first, final):
    nc.tensor.matmul(out, ah, bh, start=first, stop=False)
    nc.tensor.matmul(out, al, bh, start=False, stop=False)
    return nc.tensor.matmul(out, ah, bl, start=False, stop=final)


def build_constants(nc, c):
    with ExitStack() as ctx:
        made = ctx.enter_context(nc.semaphore("const_made"))
        chain = ctx.enter_context(nc.semaphore("const_chain"))
        iota_p = ctx.enter_context(nc.sbuf_tensor("iota_p", [P, 1], I32))
        iota_c = ctx.enter_context(nc.sbuf_tensor("iota_c", [P, P], I32))
        iota_id = ctx.enter_context(nc.sbuf_tensor("iota_id", [P, NT], I32))
        iota_dm = ctx.enter_context(nc.sbuf_tensor("iota_dm", [P, E, NCOL // E], I32))
        tri = ctx.enter_context(nc.sbuf_tensor("tri_f32", [P, P], F32))
        block = ctx.enter_context(nc.Block())

        @block.gpsimd
        def _(pool):
            nc.gpsimd.iota(iota_c[:], [[1, P]], base=0, channel_multiplier=0).then_inc(made, 1)
            nc.gpsimd.iota(iota_id[:], [[1, NT]], base=TPB, channel_multiplier=0).then_inc(made, 1)
            nc.gpsimd.iota(iota_p[:], [[0, 1]], base=1, channel_multiplier=1).then_inc(made, 1)
            nc.gpsimd.iota(iota_dm[:], [[0, E], [P, NCOL // E]], base=T + BLK + 1, channel_multiplier=1).then_inc(made, 1)
            ch = Count(pool, chain)
            ch.link(nc.gpsimd.memset(c["ident"][:], 0.0))
            nc.gpsimd.affine_select(out=c["ident"][:], in_=c["ident"][:], compare_op=ALU.not_equal, fill=1.0,
                                    base=0, pattern=[[-1, P]], channel_multiplier=1).then_inc(made, 1)
            ch.link(nc.gpsimd.memset(c["causal"][:], 1.0))
            nc.gpsimd.affine_select(out=c["causal"][:], in_=c["causal"][:], compare_op=ALU.is_ge, fill=0.0,
                                    base=0, pattern=[[1, P]], channel_multiplier=-1).then_inc(made, 1)
            ch.link(nc.gpsimd.memset(tri[:], 1.0))
            nc.gpsimd.affine_select(out=tri[:], in_=tri[:], compare_op=ALU.is_gt, fill=0.0,
                                    base=0, pattern=[[1, P]], channel_multiplier=-1).then_inc(made, 1)
            hm = c["head_mask"][:].rearrange("p (h d) -> p h d", d=HD)
            ch.link(nc.gpsimd.memset(c["head_mask"][:], 1.0))
            ch.link(nc.gpsimd.affine_select(out=hm, in_=hm, compare_op=ALU.is_ge, fill=0.0, base=0,
                                            pattern=[[-HD, HH], [0, HD]], channel_multiplier=1))
            nc.gpsimd.affine_select(out=hm, in_=hm, compare_op=ALU.is_ge, fill=0.0, base=HD - 1,
                                    pattern=[[HD, HH], [0, HD]], channel_multiplier=-1).then_inc(made, 1)

        @block.vector
        def _(dve):
            dve.wait_ge(made, 8)
            nc.vector.tensor_copy(c["iota"][:], iota_c[:])
            nc.vector.tensor_copy(c["part_id"][:], iota_p[:])
            nc.vector.tensor_copy(c["tile_id"][:], iota_id[:])
            nc.vector.tensor_copy(c["dummy_row"][:], iota_dm[:].rearrange("p e c -> p (e c)"))
            nc.vector.tensor_copy(c["before"][:], tri[:])
            nc.vector.memset(c["ones"][:], 1.0)
            nc.vector.memset(c["wg"][:], 0.0)
            for e in range(E):
                nc.vector.memset(c["rank"][:, e:e + 1], float(E - e))
            nc.vector.memset(c["restart"][:, :, 0:1], 0.0)
            nc.vector.memset(c["restart"][:, :, 1:NT], 1.0)


def statistics(nc, x, stats, tiles):
    for i in tiles:
        last = nc.vector.bn_stats(stats[:, i, :], x[:, i, :])
    return last


def variances(nc, c, dve, ch, last_stats, stats, mv, sd, ve_ready, tiles):
    ch.link(last_stats)
    step_past(dve, c["passed"])
    for i in range(tiles):
        last = nc.vector.bn_aggr(mv[:, i, :], stats[:, i, :])
    ch.link(last)
    nc.vector.tensor_scalar(sd[:], mv[:, :, 1], EPS, None, ALU.add).then_inc(ve_ready, 1)


def normalise(eng, x, mv, rstd, out, tiles):
    for i in range(tiles):
        last = eng.tensor_scalar(out[:, i, 0:D], x[:, i, :], mv[:, i, 0:1], rstd[:, i:i + 1], ALU.subtract, ALU.mult)
    return last


def logits_by_expert(nc, c, out, xt):
    for k in range(KD):
        for t in range(TPB):
            last = nc.tensor.matmul(out[32 * t:32 * t + 32, :], c["wg"][:, k, :], xt[:, k, t * P:(t + 1) * P],
                                    start=(k == 0), stop=(k == KD - 1), skip_group_check=True)
    return last


def of_experts(turned):
    return turned.rearrange("p (t w) -> p t w", w=32)[:, :, 0:E]


def route_first(nc, c, x):
    TPR = 2 * TPB
    NR = NT // TPR
    with ExitStack() as ctx:
        def sb(name, shape, dt=F32):
            return ctx.enter_context(nc.sbuf_tensor(name, shape, dt))

        def sem(name):
            return ctx.enter_context(nc.semaphore(name))

        xb = sb("r_x", [P, NR, TPR, D])
        xn = [sb(f"r_xn{i}", [P, TPR, D]) for i in range(2)]
        xt = [sb(f"r_xt{i}", [P, KD, BLK]) for i in range(2)]
        stats = [sb(f"r_stats{i}", [P, TPR, 6]) for i in range(2)]
        mv = [sb(f"r_mv{i}", [P, TPR, 2]) for i in range(2)]
        sd = [sb(f"r_sd{i}", [P, TPR]) for i in range(2)]
        rstd = [sb(f"r_rstd{i}", [P, TPR]) for i in range(2)]
        ps_t = [ctx.enter_context(nc.psum_tensor(f"r_ps_t{i}", [P, KD, BLK], F32)) for i in range(2)]
        ps_l = [ctx.enter_context(nc.psum_tensor(f"r_ps_l{i}", [P, 2, P], F32)) for i in range(2)]
        lt = [sb(f"r_lt{i}", [P, P]) for i in range(2)]
        step = sb("r_step", [P, 2, PW], I32)
        step_f, power = sb("r_step_f", [P, 2, PW]), sb("r_power", [P, KD, 2, PW])
        gamma_in, powers = sem("r_gamma_in"), sem("r_powers")
        x_in = [sem(f"r_x_in{i}") for i in range(2)]
        wg_in = sem("r_wg_in")
        ve_ready, sd_ready, xn_ready = sem("r_ve"), sem("r_sd_s"), sem("r_xn_s")
        t_done, xt_ready, l_done, chain = sem("r_t"), sem("r_xt_s"), sem("r_l"), sem("r_chain")
        lt_done, lt_ready = sem("r_lt"), sem("r_lt_s")
        xv = x.rearrange("(b i p) d -> b p i d", i=TPR, p=P)
        block = ctx.enter_context(nc.Block())
        HALF = NR // 2
        AHEAD = 4

        @block.sync
        def _(sp):
            for s in range(2):
                sp.dma_start(xb[:, s], xv[s]).then_inc(x_in[s], 16)
            sp.dma_start(c["wg"][:, :, 0:E], c["wg_dram"].rearrange("(k p) e -> p k e", p=P)).then_inc(wg_in, 16)
            with sp.Fori(0, HALF - 1) as i:
                for s in range(2):
                    sp.wait_ge(x_in[s], 16 * (i + 1))
                    sp.dma_start(xb[:, 2 * i + 2 + s], xv[2 * i + 2 + s]).then_inc(x_in[s], 16)
            for k in range(KD):
                for h in range(HH):
                    sp.dma_start(c["gamma_col"][h * HD:(h + 1) * HD, k:k + 1],
                                 c["gamma_dram"][k * HH + h:k * HH + h + 1].unsqueeze(0)
                                 .to_broadcast([HD, 1])).then_inc(gamma_in, 16)

        @block.gpsimd
        def _(pool):
            nc.gpsimd.iota(step[:, 0, :], [[PW, PW]], base=0, channel_multiplier=0)
            nc.gpsimd.iota(step[:, 1, :], [[1, PW]], base=0, channel_multiplier=0).then_inc(powers, 1)
            pool.wait_ge(powers, 1)
            nc.gpsimd.tensor_copy(step_f[:], step[:]).then_inc(powers, 1)
            pool.wait_ge(powers, 2)
            pool.wait_ge(gamma_in, 16 * H)
            for k in range(KD):
                last = nc.gpsimd.tensor_tensor(
                    power[:, k], c["gamma_col"][:, k:k + 1].unsqueeze(2).to_broadcast([P, 2, PW]),
                    step_f[:], ALU.pow)
            last.then_inc(powers, 1)
            pool.wait_ge(powers, 3)
            for k in range(KD):
                nc.gpsimd.tensor_tensor(
                    c["decay"][:, k, :].rearrange("p (a b) -> p a b", b=PW),
                    power[:, k, 0, :].unsqueeze(2).to_broadcast([P, PW, PW]),
                    power[:, k, 1, :].unsqueeze(1).to_broadcast([P, PW, PW]), ALU.mult)

        @block.scalar
        def _(act):
            def root(s, n):
                act.wait_ge(ve_ready, n)
                nc.scalar.activation(sd[s][:], sd[s][:], ACT.Sqrt).then_inc(sd_ready, 1)

            def turned(h, n):
                act.wait_ge(t_done, n + AHEAD)
                nc.scalar.copy(xt[h][:], ps_t[h][:]).then_inc(xt_ready, 1)

            def logits(h, n, b):
                act.wait_ge(l_done, n)
                nc.scalar.copy(c["logits"][:, b + 1, :].rearrange("p (t e) -> p t e", e=E), of_experts(ps_l[h][:, 1, :]))

            def by_expert(h, n):
                act.wait_ge(lt_done, n)
                nc.scalar.copy(lt[h][:], ps_l[h][:, 0, :]).then_inc(lt_ready, 1)

            root(0, 1)
            with act.Fori(0, HALF) as i:
                for s in range(2):
                    n = 4 * i + 2 * s
                    if s == 0:
                        root(1, 2 * i + 2)
                    turned(0, n + 1)
                    turned(1, n + 2)
                    if s == 1:
                        root(0, 2 * i + 3)
                    by_expert(0, n + 1)
                    by_expert(1, n + 2)
                    logits(0, n + 1, n)
                    logits(1, n + 2, n + 1)

        @block.vector
        def _(dve):
            def stats_of(ch, s, n, n_in):
                dve.wait_ge(x_in[s], n_in)
                last = statistics(nc, xb[:, n], stats[s], range(TPR))
                variances(nc, c, dve, ch, last, stats[s], mv[s], sd[s], ve_ready, TPR)

            def norm_of(ch, s, n):
                dve.wait_ge(sd_ready, n + 1)
                ch.link(nc.vector.reciprocal(rstd[s][:], sd[s][:]))
                nc.vector.tensor_copy(c["mean"][:, n, :], mv[s][:, :, 0])
                nc.vector.tensor_copy(c["rstd"][:, n, :], rstd[s][:])
                dve.wait_ge(t_done, 2 * n - 2 + AHEAD)
                normalise(nc.vector, xb[:, n], mv[s], rstd[s], xn[s], TPR).then_inc(xn_ready, 1)

            ch = Count(dve, chain)
            stats_of(ch, 0, 0, 16)
            start, per = ch.n, 6
            with dve.Fori(0, HALF - 1) as i:
                ch = Count(dve, chain, per * i + start)
                for s in range(2):
                    stats_of(ch, 1 - s, 2 * i + s + 1, 16 * (i + 1 + s))
                    norm_of(ch, s, 2 * i + s)
                assert ch.n == per
            ch = Count(dve, chain, per * (HALF - 1) + start)
            stats_of(ch, 1, NR - 1, 16 * HALF)
            for s in range(2):
                norm_of(ch, s, NR - 2 + s)
            nc.vector.memset(sd[0][:], 1.0).then_inc(ve_ready, 1)

        @block.tensor
        def _(pe):
            pe.wait_ge(wg_in, 16)
            pe.sem_inc(t_done, AHEAD)
            with pe.Fori(0, HALF) as i:
                for s in range(2):
                    n = 4 * i + 2 * s
                    pe.wait_ge(xn_ready, 2 * i + s + 1)
                    for h in range(2):
                        for k in range(KD):
                            for t in range(TPB):
                                last = nc.tensor.transpose(ps_t[h][:, k, t * P:(t + 1) * P],
                                                           xn[s][:, h * TPB + t, k * P:(k + 1) * P], c["ident"][:])
                        last.then_inc(t_done, 1)
                    for h in range(2):
                        pe.wait_ge(xt_ready, n + h + 1)
                        logits_by_expert(nc, c, ps_l[h][:, 0, :], xt[h]).then_inc(lt_done, 1)
                    for h in range(2):
                        pe.wait_ge(lt_ready, n + h + 1)
                        nc.tensor.transpose(ps_l[h][:, 1, :], lt[h][:], c["ident"][:]).then_inc(l_done, 1)


def moe(nc, c, w_gate, w_down, table, acc, tag, x=None, x_meta=None, w_next=()):
    with ExitStack() as ctx:
        def sb(name, shape, dt=F32):
            return ctx.enter_context(nc.sbuf_tensor(f"{tag}_{name}", shape, dt))

        def sem(name):
            return ctx.enter_context(nc.semaphore(f"{tag}_{name}"))

        def ps(name, shape):
            return ctx.enter_context(nc.psum_tensor(f"{tag}_{name}", shape, F32))

        slot_row = sb("slot_row", [P, NCOL + 2 * TPB], I32)
        slot_acc = sb("slot_acc", [P, NCOL], I32)
        wg_raw = sb("wg_raw", [P, KD, F])
        wd_raw = sb("wd_raw", [P, MF, D])
        wgh, wgl = sb("wgh", [P, KD, F], F32R), sb("wgl", [P, KD, F], F32R)
        wdh, wdl = sb("wdh", [P, MF, D], F32R), sb("wdl", [P, MF, D], F32R)
        wraw_in = sem("wraw_in")
        w_hi_ready, w_lo_ready = sem("w_hi_ready"), sem("w_lo_ready")
        rows_sent, acc_set = sem("rows_sent"), sem("acc_set")

        def high(m):
            nc.scalar.copy(wgh[:, :, m * P:(m + 1) * P], wg_raw[:, :, m * P:(m + 1) * P])
            nc.scalar.copy(wdh[:, m, :], wd_raw[:, m, :]).then_inc(w_hi_ready, 1)

        def low(eng, m):
            eng.tensor_tensor(wgl[:, :, m * P:(m + 1) * P], wg_raw[:, :, m * P:(m + 1) * P],
                              wgh[:, :, m * P:(m + 1) * P].bitcast(F32), ALU.subtract)
            eng.tensor_tensor(wdl[:, m, :], wd_raw[:, m, :], wdh[:, m, :].bitcast(F32), ALU.subtract).then_inc(w_lo_ready, 1)

        with ExitStack() as rctx:
            def rb(name, shape, dt=F32):
                return rctx.enter_context(nc.sbuf_tensor(f"{tag}_{name}", shape, dt))

            te = [P, NT, E]
            half = rb("half", [P, NT, 4])
            assert E == 8
            lg = c["logits"][:, 1:, :].rearrange("p b (t e) -> p (b t) e", e=E)
            eq, sc, l2, ex, lc = (rb(n, te) for n in ("eq", "sc", "l2", "ex", "lc"))
            mask = [rb(f"mask{i}", te) for i in range(2)]
            mask16 = [rb(f"mask16_{i}", te, BF16) for i in range(2)]
            m = [rb(f"m{i}", [P, NT]) for i in range(2)]
            rk = [rb(f"rk{i}", [P, NT]) for i in range(2)]
            z, g1, g2, dn, d2, loc, over = (rb(n, [P, NT]) for n in ("z", "top_g1", "top_g2", "dn", "d2", "loc", "over"))
            et = [P, E, NT]
            tot, inc, base = rb("tot", et), rb("inc", et), rb("base", et)
            total1 = rb("total1", [P, E, 1])
            sloti, ai, bi = rb("sloti", [P, NT], I32), rb("ai", [P, NT], I32), rb("bi", [P, NT], I32)
            cola = [rb(f"cola{i}", [P, NT], BF16) for i in range(2)]
            colb = [rb(f"colb{i}", [P, NT], BF16) for i in range(2)]
            meta = rb("meta", [P, NT, MW])
            TPH = 8
            NH = 2 * NT // TPH
            NOH = 3
            eqa = [rb(f"eqa{i}", [P, TPH, P], BF16) for i in range(NOH)]
            oha = [rb(f"oha{i}", [P, TPH, 2, P], BF16) for i in range(NOH)]
            ohb = [rb(f"ohb{i}", [P, TPH, P], BF16) for i in range(NOH)]
            parts = rb("parts", [P, 2, NCOL])
            tab, emp = rb("tab", [P, NCOL]), rb("emp", [P, NCOL])
            ps_before = [rctx.enter_context(nc.psum_tensor(f"{tag}_ps_before{i}", [P, E * NT], F32)) for i in range(2)]
            ps_tot = [rctx.enter_context(nc.psum_tensor(f"{tag}_ps_tot{i}", [P, E * NT], F32)) for i in range(2)]
            ps_tab = rctx.enter_context(nc.psum_tensor(f"{tag}_ps_tab", [P, 2, NCOL], F32))

            def rs(name):
                return rctx.enter_context(nc.semaphore(f"{tag}_{name}"))

            chain, mask_ready, counted = rs("chain"), rs("mask_ready"), rs("counted")
            ex_in, ex_out, meta_ready = rs("ex_in"), rs("ex_out"), rs("meta_ready")
            topped, gate_chain, z_ready, gates_ready = (rs(n) for n in ("topped", "gate_chain", "z_ready", "gates_ready"))
            matched, hot, hot_part, hot_tile, placed = (rs(n) for n in ("matched", "hot", "hot_part", "hot_tile", "placed"))
            next_raw = [rb(f"next_raw{n}", [P, KD, D]) for n in range(len(w_next))]
            next_in, next_hi = rs("next_in"), rs("next_hi")
            block = rctx.enter_context(nc.Block())
            over_e = lambda a: a[:].unsqueeze(2).to_broadcast(te)
            rank = c["rank"][:].unsqueeze(1).to_broadcast(te)

            @block.sync
            def _(sp):
                sp.dma_start(wg_raw[:], w_gate[0].rearrange("(k p) f -> p k f", p=P)).then_inc(wraw_in, 16)
                sp.dma_start(wd_raw[:], w_down[0].rearrange("(m p) d -> p m d", p=P)).then_inc(wraw_in, 16)
                for raw, w in zip(next_raw, w_next):
                    sp.dma_start(raw[:], w.rearrange("(k p) f -> p k f", p=P)).then_inc(next_in, 16)
                sp.wait_ge(meta_ready, 1)
                sp.wait_ge(gates_ready, 1)
                with nc.allow_non_contiguous_dma(reason="a few words for each token"):
                    if table is None:
                        sp.dma_start(x_meta.rearrange("(t p) w -> p t w", p=P), meta[:]).then_inc(rows_sent, 16)
                    else:
                        sp.dma_start(table[BLK:, D:].rearrange("(t p) w -> p t w", p=P),
                                     meta[:, :, 0:ROW - D]).then_inc(rows_sent, 16)
                        sp.dma_start(table[0:BLK, D:].rearrange("(t p) w -> p t w", p=P),
                                     meta[:, 0:TPB, 0:ROW - D]).then_inc(rows_sent, 16)
                sp.wait_ge(rows_sent, 16 if table is None else 32)
                if table is None:
                    sp.dma_start(acc[0:T].rearrange("(a b) d -> a (b d)", a=P),
                                 x.rearrange("(a b) d -> a (b d)", a=P)).then_inc(acc_set, 16)
                    sp.dma_start(acc[T:T + CAP].rearrange("(a b) d -> a (b d)", a=P),
                                 x[0:CAP].rearrange("(a b) d -> a (b d)", a=P)).then_inc(acc_set, 16)
                    sp.wait_ge(acc_set, 32)
                sp.wait_ge(wraw_in, 32)

            @block.gpsimd
            def _(pool):
                gch = Count(pool, gate_chain)
                pool.wait_ge(topped, 1)
                nc.gpsimd.tensor_tensor(ex[:], lg, over_e(m[0]), ALU.subtract).then_inc(ex_in, 1)
                pool.wait_ge(topped, 2)
                nc.gpsimd.tensor_tensor(g2[:], m[1][:], m[0][:], ALU.subtract).then_inc(ex_in, 1)
                if table is None:
                    nc.gpsimd.tensor_copy(meta[:, :, 4], c["mean"][:].rearrange("p n t -> p (n t)"))
                    nc.gpsimd.tensor_copy(meta[:, :, 5], c["rstd"][:].rearrange("p n t -> p (n t)"))
                pool.wait_ge(ex_out, 2)
                gch.link(nc.gpsimd.tensor_tensor(half[:], ex[:, :, 0:4], ex[:, :, 4:8], ALU.add))
                gch.link(nc.gpsimd.tensor_tensor(half[:, :, 0:2], half[:, :, 0:2], half[:, :, 2:4], ALU.add))
                nc.gpsimd.tensor_tensor(z[:], half[:, :, 0], half[:, :, 1], ALU.add).then_inc(z_ready, 1)
                for chunk in range(MF):
                    pool.wait_ge(w_hi_ready, chunk + 1)
                    low(nc.gpsimd, chunk)
                for n, (raw, name) in enumerate(zip(next_raw, "qkvo")):
                    pool.wait_ge(next_hi, n + 1)
                    nc.gpsimd.tensor_tensor(c["w_lo"][name][:], raw[:], c["w_hi"][name][:].bitcast(F32), ALU.subtract)
                for n in range(NH):
                    pool.wait_ge(matched, n + 1)
                    tiles = slice(n % (NH // 2) * TPH, (n % (NH // 2) + 1) * TPH)
                    nc.gpsimd.tensor_tensor(oha[n % NOH][:, :, 0, :], eqa[n % NOH][:],
                                            c["tile_id"][:, tiles].unsqueeze(2).to_broadcast([P, TPH, P]),
                                            ALU.mult).then_inc(hot_tile, 1)

            @block.scalar
            def _(act):
                act.wait_ge(ex_in, 2)
                nc.scalar.activation(ex[:], ex[:], ACT.Exp).then_inc(ex_out, 1)
                nc.scalar.activation(g2[:], g2[:], ACT.Exp).then_inc(ex_out, 1)
                act.wait_ge(wraw_in, 32)
                for m in range(MF):
                    high(m)
                if w_next:
                    act.wait_ge(next_in, 16 * len(w_next))
                for raw, name in zip(next_raw, "qkvo"):
                    nc.scalar.copy(c["w_hi"][name][:], raw[:]).then_inc(next_hi, 1)
                for n in range(NH):
                    act.wait_ge(matched, n + 1)
                    nc.scalar.activation(oha[n % NOH][:, :, 1, :], eqa[n % NOH][:], ACT.Copy,
                                         scale=c["part_id"][:]).then_inc(hot_part, 1)

            @block.vector
            def _(dve):
                ch = Count(dve, chain)
                src = lg
                for i in range(2):
                    top = nc.vector.tensor_reduce(m[i][:], src, AX_X, ALU.max)
                    top.then_inc(topped, 1)
                    dve.wait_ge(topped, i + 1)
                    ch.link(nc.vector.tensor_tensor(eq[:], src, over_e(m[i]), ALU.is_equal))
                    ch.link(nc.vector.tensor_tensor(sc[:], eq[:], rank, ALU.mult))
                    ch.link(nc.vector.tensor_reduce(rk[i][:], sc[:], AX_X, ALU.max))
                    ch.link(nc.vector.tensor_tensor(mask[i][:], sc[:], over_e(rk[i]), ALU.is_equal))
                    nc.vector.tensor_copy(mask16[i][:], mask[i][:]).then_inc(mask_ready, 1)
                    if i == 0:
                        ch.link(nc.vector.scalar_tensor_tensor(l2[:], mask[0][:], NEG, lg, ALU.mult, ALU.add))
                        src = l2[:]
                nc.vector.tensor_scalar(meta[:, :, 2], rk[0][:], -1.0, float(E), ALU.mult, ALU.add)
                nc.vector.tensor_scalar(meta[:, :, 3], rk[1][:], -1.0, float(E), ALU.mult, ALU.add).then_inc(meta_ready, 1)
                dve.wait_ge(meta_ready, 1)
                for i in range(2):
                    dve.wait_ge(counted, i + 1)
                    tot_f = tot[:].rearrange("p e t -> p (e t)")
                    inc_f = inc[:].rearrange("p e t -> p (e t)")
                    ch.link(nc.vector.tensor_copy(tot_f, ps_tot[i][:]))
                    ch.link(nc.vector.tensor_tensor_scan(inc_f, c["restart"][:].rearrange("p e t -> p (e t)"),
                                                         tot_f, 0.0, ALU.mult, ALU.add))
                    ch.link(nc.vector.tensor_tensor(base[:], inc[:], tot[:], ALU.subtract))
                    if i == 1:
                        ch.link(nc.vector.tensor_tensor(base[:], base[:], total1[:].to_broadcast(et), ALU.add))
                    else:
                        ch.link(nc.vector.tensor_copy(total1[:], inc[:, :, NT - 1:NT]))
                    ch.link(nc.vector.tensor_tensor(base[:], base[:],
                                                    ps_before[i][:].rearrange("p (e t) -> p e t", e=E), ALU.add))
                    ch.link(nc.vector.tensor_tensor(lc[:], mask[i][:], base[:].rearrange("p e t -> p t e"), ALU.mult))
                    ch.link(nc.vector.tensor_reduce(loc[:], lc[:], AX_X, ALU.add))
                    ch.link(nc.vector.tensor_scalar(over[:], loc[:], float(CAP), float(NSLOT), ALU.is_ge, ALU.mult))
                    ch.link(nc.vector.tensor_tensor(loc[:], loc[:], over[:], ALU.add))
                    ch.link(nc.vector.scalar_tensor_tensor(loc[:], meta[:, :, 2 + i], float(CAP), loc[:],
                                                           ALU.mult, ALU.add))
                    ch.link(nc.vector.tensor_copy(sloti[:], loc[:]))
                    nc.vector.tensor_scalar(ai[:], sloti[:], 7, None, ALU.arith_shift_right)
                    ch.link(nc.vector.tensor_scalar(bi[:], sloti[:], P - 1, None, ALU.bitwise_and))
                    nc.vector.tensor_copy(cola[i][:], ai[:])
                    ch.link(nc.vector.tensor_copy(colb[i][:], bi[:]))
                dve.wait_ge(z_ready, 1)
                ch.link(nc.vector.reciprocal(g1[:], z[:]))
                ch.link(nc.vector.tensor_tensor(g2[:], g2[:], g1[:], ALU.mult))
                ch.link(nc.vector.tensor_tensor(dn[:], g1[:], g2[:], ALU.add))
                ch.link(nc.vector.tensor_scalar(dn[:], dn[:], 1e-9, None, ALU.max))
                ch.link(nc.vector.reciprocal(d2[:], dn[:]))
                ch.link(nc.vector.tensor_scalar(d2[:], d2[:], 0.5, None, ALU.mult))
                nc.vector.tensor_tensor(meta[:, :, 0], g1[:], d2[:], ALU.mult)
                nc.vector.tensor_tensor(meta[:, :, 1], g2[:], d2[:], ALU.mult).then_inc(gates_ready, 1)
                hot_shape = [P, TPH, P]
                iota = c["iota"][:].unsqueeze(1).to_broadcast(hot_shape)
                for n in range(NH):
                    i, s = n // (NH // 2), n % NOH
                    tiles = slice(n % (NH // 2) * TPH, (n % (NH // 2) + 1) * TPH)
                    over_cols = lambda a: a[:, tiles].unsqueeze(2).to_broadcast(hot_shape)
                    if n >= NOH:
                        dve.wait_ge(placed, n - NOH + 1)
                    nc.vector.tensor_tensor(eqa[s][:], iota, over_cols(cola[i]), ALU.is_equal).then_inc(matched, 1)
                    nc.vector.tensor_tensor(ohb[s][:], iota, over_cols(colb[i]), ALU.is_equal).then_inc(hot, 1)
                dve.wait_ge(placed, NH)
                ch.link(nc.vector.tensor_copy(parts[:], ps_tab[:]))
                ch.link(nc.vector.scalar_tensor_tensor(tab[:], parts[:, 0, :], float(P), parts[:, 1, :],
                                                       ALU.mult, ALU.add))
                ch.link(nc.vector.tensor_scalar(emp[:], tab[:], 0.0, None, ALU.is_equal))
                ch.link(nc.vector.tensor_tensor(emp[:], emp[:], c["dummy_row"][:], ALU.mult))
                ch.link(nc.vector.tensor_tensor(emp[:], emp[:], tab[:], ALU.add))
                ch.link(nc.vector.tensor_scalar(emp[:], emp[:], -1.0 - BLK, None, ALU.add))
                nc.vector.tensor_copy(slot_acc[:], emp[:])
                ch.link(nc.vector.tensor_scalar(tab[:], tab[:], -1.0 if table is not None else -1.0 - BLK, 0.0,
                                                ALU.add, ALU.max))
                nc.vector.tensor_copy(slot_row[:, 0:NCOL], tab[:])
                nc.vector.memset(slot_row[:, NCOL:], 0)

            @block.tensor
            def _(pe):
                for i in range(2):
                    pe.wait_ge(mask_ready, i + 1)
                    by_expert = mask16[i][:].rearrange("p t e -> p e t")
                    nc.tensor.matmul(ps_before[i][:], c["before"][:], by_expert, start=True, stop=True)
                    nc.tensor.matmul(ps_tot[i][:], c["ones"][:], by_expert, start=True, stop=True).then_inc(counted, 1)
                for n in range(NH):
                    pe.wait_ge(hot, n + 1)
                    pe.wait_ge(hot_part, n + 1)
                    pe.wait_ge(hot_tile, n + 1)
                    for t in range(TPH):
                        last = nc.tensor.matmul(ps_tab[:], ohb[n % NOH][:, t, :], oha[n % NOH][:, t],
                                                start=(n == 0 and t == 0), stop=(n == NH - 1 and t == TPH - 1))
                    last.then_inc(placed, 1)

        xg = [sb(f"xg{i}", [P, TPB, D + MW]) for i in range(2)]
        GATHERS = 16 * TPB * (2 if table is None else 1)
        xh = [sb(f"xh{i}", [P, KD, BLK], F32R) for i in range(2)]
        xl = [sb(f"xl{i}", [P, KD, BLK], F32R) for i in range(2)]
        g = [sb(f"gelu{i}", [P, BLK]) for i in range(2)]
        gh = [sb(f"gh{i}", [P, BLK], F32R) for i in range(2)]
        gl = [sb(f"gl{i}", [P, BLK], F32R) for i in range(2)]
        rows = [sb(f"rows{i}", [P, TPB, D]) for i in range(2)]
        both = sb("both", [P, TPB, 2])
        gate = [sb(f"gate{i}", [P, TPB]) for i in range(2)]
        expert = sb("expert", [P, 1])
        idx_row, idx_acc = sb("idx_row", [P, TPB], I32), sb("idx_acc", [P, TPB], I32)
        ps_in = ps("ps_in", [P, KD, BLK])
        ps_up = [ps(f"ps_up{i}", [P, BLK]) for i in range(2)]
        ps_out = [ps(f"ps_out{i}", [P, TPB, D]) for i in range(2)]
        gathered = [sem(f"gathered{i}") for i in range(2)]
        in_t, xh_ready, xl_ready = sem("in_t"), sem("xh_ready"), sem("xl_ready")
        up_done, g_ready, gh_ready, gl_ready, dn_done = (sem(n) for n in ("up_done", "g_ready", "gh_ready", "gl_ready", "dn_done"))
        rows_ready, added, idx_set = sem("rows_ready"), sem("added"), sem("idx_set")
        chain2, normed = sem("chain2"), sem("normed")
        block = ctx.enter_context(nc.Block())

        @block.sync
        def _(sp):
            def weights(e, n):
                sp.wait_ge(w_hi_ready, MF * n)
                sp.wait_ge(w_lo_ready, MF * n)
                sp.dma_start(wg_raw[:], w_gate[e].rearrange("(k p) f -> p k f", p=P)).then_inc(wraw_in, 16)
                sp.dma_start(wd_raw[:], w_down[e].rearrange("(m p) d -> p m d", p=P)).then_inc(wraw_in, 16)

            with sp.Fori(0, E - 1) as e:
                weights(e + 1, e + 1)
            weights(0, E)
            sp.wait_ge(wraw_in, 32 * (E + 1))

        @block.gpsimd
        def _(pool):
            def gather(s, n_col, n_prev):
                ins = nc.gpsimd.tensor_copy(idx_row[:], slot_row[:, n_col:n_col + TPB] if isinstance(n_col, int)
                                            else slot_row[:, bass.ds(n_col, TPB)])
                ins.then_inc(idx_set, 1)
                pool.wait_ge(idx_set, n_prev)
                step_past(pool, c["passed"])
                sources = [(slice(0, D), x), (slice(D, D + MW), x_meta)] if table is None else [(slice(0, ROW), table)]
                for t in range(TPB):
                    for cols, source in sources:
                        nc.gpsimd.indirect_dma_start(xg[s][:, t, cols], None, source,
                                                     bass.IndirectOffsetOnAxis(ap=idx_row[:, t:t + 1], axis=0)
                                                     ).then_inc(gathered[s], 16)

            gather(0, 0, 1)
            pool.wait_ge(gathered[0], GATHERS)
            gather(1, TPB, 2)
            with pool.Fori(0, E) as e:
                for j in range(JB):
                    n, s = JB * e + j, j % 2
                    pool.wait_ge(xl_ready, n + 1)
                    pool.wait_ge(gathered[1 - s], GATHERS * (2 * e + (j + 1) // 2 + 1))
                    gather(s, (n + 2) * TPB, 2 * n + 3)
                    pool.wait_ge(rows_ready, 2 * n + 2)
                    nc.gpsimd.tensor_copy(idx_acc[:], slot_acc[:, bass.ds(n * TPB, TPB)]).then_inc(idx_set, 1)
                    pool.wait_ge(idx_set, 2 * n + 4)
                    step_past(pool, c["passed"])
                    for t in range(TPB):
                        nc.gpsimd.indirect_dma_start(acc, bass.IndirectOffsetOnAxis(ap=idx_acc[:, t:t + 1], axis=0),
                                                     rows[s][:, t, :], None, compute_op=ALU.add).then_inc(added, 16)
                    pool.wait_ge(added, 16 * TPB * (n + 1))
            for s in range(2):
                pool.wait_ge(gathered[s], GATHERS * (NBLK // 2 + 1))

        @block.scalar
        def _(act):
            def gelu(s, n_up):
                act.wait_ge(up_done, n_up)
                nc.scalar.activation(g[s][:], ps_up[s][:], ACT.Gelu).then_inc(g_ready, 1)

            act.wait_ge(in_t, 1)
            nc.scalar.copy(xh[0][:], ps_in[:]).then_inc(xh_ready, 1)
            gelu(0, 1)
            with act.Fori(0, E) as e:
                for j in range(JB):
                    n = JB * e + j
                    if j == JB - 1:
                        act.wait_ge(wraw_in, 32 * (e + 2))
                    for m in range(MF):
                        gelu((m + 1) % 2, MF * n + m + 2)
                        if j == JB - 1 and m >= 1:
                            act.wait_ge(dn_done, MF * n + m)
                            high(m - 1)
                        if m == TURN:
                            act.wait_ge(in_t, n + 2)
                            nc.scalar.copy(xh[(j + 1) % 2][:], ps_in[:]).then_inc(xh_ready, 1)
                    act.wait_ge(dn_done, MF * n + MF)
                    for t in range(TPB // 2):
                        last = nc.scalar.activation(rows[j % 2][:, t, :], ps_out[j % 2][:, t, :], ACT.Copy,
                                                    scale=gate[j % 2][:, t:t + 1])
                    last.then_inc(rows_ready, 1)
                    if j == JB - 1:
                        high(MF - 1)

        @block.vector
        def _(dve):
            def slot_gates(s):
                ch.link(nc.vector.scalar_tensor_tensor(both[:], xg[s][:, :, D + 2:D + 4], expert[:],
                                                       xg[s][:, :, D:D + 2], ALU.is_equal, ALU.mult))
                ch.link(nc.vector.tensor_reduce(gate[s][:], both[:], AX_X, ALU.add))

            def rows_out(s):
                for t in range(TPB // 2, TPB):
                    last = nc.vector.tensor_scalar(rows[s][:, t, :], ps_out[s][:, t, :], gate[s][:, t:t + 1], None, ALU.mult)
                last.then_inc(rows_ready, 1)

            def parts(s, n):
                dve.wait_ge(g_ready, n)
                nc.vector.tensor_copy(gh[s][:], g[s][:]).then_inc(gh_ready, 1)
                dve.wait_ge(gh_ready, n)
                split_low(nc, gl[s][:], g[s][:], gh[s][:]).then_inc(gl_ready, 1)

            def norm(s, n_in):
                dve.wait_ge(gathered[s], n_in)
                for t in range(TPB):
                    last = nc.vector.tensor_scalar(xg[s][:, t, 0:D], xg[s][:, t, 0:D], xg[s][:, t, D + 4:D + 5],
                                                   xg[s][:, t, D + 5:D + 6], ALU.subtract, ALU.mult)
                last.then_inc(normed, 1)

            ch = Count(dve, chain2)
            ch.link(nc.vector.memset(expert[:], 0.0))
            if table is None:
                norm(0, GATHERS)
            dve.wait_ge(xh_ready, 1)
            slot_gates(0)
            split_low(nc, xl[0][:], ps_in[:], xh[0][:]).then_inc(xl_ready, 1)
            per = 2 * JB + 1
            start = ch.n
            parts(0, 1)
            with dve.Fori(0, E) as e:
                ch = Count(dve, chain2, per * e + start)
                for j in range(JB):
                    n = JB * e + j
                    for m in range(MF):
                        parts((m + 1) % 2, MF * n + m + 2)
                        if j == JB - 1 and m >= 1:
                            dve.wait_ge(w_hi_ready, MF * (e + 1) + m)
                            low(nc.vector, m - 1)
                        if m == TURN - 2 and table is None:
                            norm(1 - j % 2, GATHERS * (2 * e + (j + 1) // 2 + 1))
                        if m == TURN:
                            if j == JB - 1:
                                ch.link(nc.vector.tensor_scalar(expert[:], expert[:], 1.0, None, ALU.add))
                            dve.wait_ge(xh_ready, n + 2)
                            slot_gates((j + 1) % 2)
                            split_low(nc, xl[(j + 1) % 2][:], ps_in[:], xh[(j + 1) % 2][:]).then_inc(xl_ready, 1)
                    dve.wait_ge(dn_done, MF * n + MF)
                    rows_out(j % 2)
                    if j == JB - 1:
                        dve.wait_ge(w_hi_ready, MF * (e + 1) + MF)
                        low(nc.vector, MF - 1)
                assert ch.n == per

        @block.tensor
        def _(pe):
            def turn_in(s):
                for k in range(KD):
                    for t in range(TPB):
                        last = nc.tensor.transpose(ps_in[:, k, t * P:(t + 1) * P], xg[s][:, t, k * P:(k + 1) * P],
                                                   c["ident"][:])
                last.then_inc(in_t, 1)

            def up(m, s):
                for k in range(KD):
                    last = three(nc, ps_up[m % 2][:], wgh[:, k, m * P:(m + 1) * P], wgl[:, k, m * P:(m + 1) * P],
                                 xh[s][:, k, :], xl[s][:, k, :], k == 0, k == KD - 1)
                last.then_inc(up_done, 1)

            def down(m, s, n):
                pe.wait_ge(gl_ready, MF * n + m + 1)
                for t in range(TPB):
                    slots = slice(t * P, (t + 1) * P)
                    last = three(nc, ps_out[s][:, t, :], gh[m % 2][:, slots], gl[m % 2][:, slots],
                                 wdh[:, m, :], wdl[:, m, :], m == 0 and t % 2 == 0, m == MF - 1 and t % 2 == 1)
                last.then_inc(dn_done, 1)

            if table is None:
                pe.wait_ge(normed, 1)
            else:
                pe.wait_ge(gathered[0], GATHERS)
            turn_in(0)
            pe.wait_ge(xl_ready, 1)
            pe.wait_ge(w_lo_ready, 1)
            up(0, 0)
            with pe.Fori(0, E) as e:
                for j in range(JB):
                    n = JB * e + j
                    s = j % 2
                    for m in range(MF):
                        if m == TURN:
                            if table is None:
                                pe.wait_ge(normed, n + 2)
                            else:
                                pe.wait_ge(gathered[1 - s], GATHERS * (2 * e + (j + 1) // 2 + 1))
                            turn_in(1 - s)
                        if m + 1 < MF:
                            if j == 0:
                                pe.wait_ge(w_lo_ready, MF * e + m + 2)
                            up(m + 1, s)
                        else:
                            pe.wait_ge(xl_ready, n + 2)
                            if j == JB - 1:
                                pe.wait_ge(w_lo_ready, MF * e + MF + 1)
                            up(0, 1 - s)
                        down(m, s, n)


USES = (["kv0", "s00", "s01", "s02", "s03", "kv1", "s10", "s11", "s12", "s13", "kv2", "y0", "s20", "s21", "s22", "s23",
         "kv3", "y1", "q0", "q1", "k0", "k1", "s30", "s31", "s32", "s33", "y2", "y3"])
NW = 4
PER_BANK = len(USES) // NW


def attention(nc, c, acc, bq, bk, bv, bo, table, out):
    with ExitStack() as ctx:
        def sb(name, shape, dt=F32):
            return ctx.enter_context(nc.sbuf_tensor(f"a_{name}", shape, dt))

        def sem(name):
            return ctx.enter_context(nc.semaphore(f"a_{name}"))

        def ps(name, shape):
            return ctx.enter_context(nc.psum_tensor(f"a_{name}", shape, F32))

        def pair(name, shape, dt=F32):
            return [sb(f"{name}{i}", shape, dt) for i in range(2)]

        w_hi, w_lo = c["w_hi"], c["w_lo"]
        bq_c, bk_c = sb("bq_c", [P, KD]), sb("bk_c", [P, KD])
        bkv_r = sb("bkv_r", [P, 2 * D])
        bo_r = sb("bo_r", [P, D])
        xb, x2 = pair("xb", [P, TPB, D]), pair("x2", [P, TPB, D])
        xn, xn3 = sb("xn", [P, TPB, D]), sb("xn3", [P, TPB, D])
        xth, xtl = pair("xth", [P, KD, BLK], F32R), pair("xtl", [P, KD, BLK], F32R)
        xt3, lt = sb("xt3", [P, KD, BLK]), sb("lt", [P, P])
        qt, kt = pair("qt", [P, KD, BLK]), pair("kt", [P, KD, BLK])
        q2 = pair("q2", [P, 2, KD, BLK], F32R)
        kh, kl = pair("kh", [P, KD, BLK], F32R), pair("kl", [P, KD, BLK], F32R)
        qd = pair("qd", [P, 2, KD, HH, CH], F32R)
        ss = pair("ss", [P, H, CH])
        kv = pair("kv", [P, 2 * D])
        vx = pair("vx", [P, H, 2 * HD])
        oth, otl = pair("oth", [P, KD, CH], F32R), pair("otl", [P, KD, CH], F32R)
        state, fresh = pair("state", [P, KD, P]), sb("fresh", [P, KD, P])
        stats2, mv2, sd2, rs2 = sb("st2", [P, TPB, 6]), sb("mv2", [P, TPB, 2]), sb("sd2", [P, TPB]), sb("rs2", [P, TPB])
        stats3, mv3, sd3, rs3 = sb("st3", [P, TPB, 6]), sb("mv3", [P, TPB, 2]), sb("sd3", [P, TPB]), sb("rs3", [P, TPB])
        nm3 = sb("nm3", [P, TPB])
        ps_t = ps("ps_t", [P, KD, BLK])
        ps_w = [ps(f"ps_w{i}", [P, BLK]) for i in range(NW)]
        ps_o = ps("ps_o", [P, KD, CH])
        ps_st = ps("ps_st", [P, KD, P])

        b_in, chain = sem("b_in"), sem("chain")
        x_in, x2_out = [sem(f"x_in{i}") for i in range(2)], [sem(f"x2_out{i}") for i in range(2)]
        qd_in = [sem(f"qd_in{i}") for i in range(2)]
        full, free = [sem(f"full{i}") for i in range(NW)], [sem(f"free{i}") for i in range(NW)]
        lt_done, lt_ready = sem("lt_done"), sem("lt_s")
        kh_ready, masked = sem("kh_s"), sem("masked")
        rs3_ready, centred = sem("rs3_s"), sem("centred")
        ve2, sd2_ready, xn_ready, xr_ready = sem("ve2"), sem("sd2_s"), sem("xn_s"), sem("xr_s")
        ve3, sd3_ready, xn3_ready, xn3_out = sem("ve3"), sem("sd3_s"), sem("xn3_s"), sem("xn3_out")
        x_turned, xth_ready, xtl_ready = sem("x_turned"), sem("xth_s"), sem("xtl_s")
        qh_ready, q2_ready, kl_ready = sem("qh_s"), sem("q2_s"), sem("kl_s")
        vx_ready, o_done, oth_ready, otl_ready = (sem(n) for n in ("vx_s", "o_done", "oth_s", "otl_s"))
        st_done, st_added = sem("st_done"), sem("st_added")
        t3_done, xt3_ready, lg_done = (sem(n) for n in ("t3_done", "xt3_s", "lg_done"))

        xv = acc[0:T + 2 * BLK].rearrange("(b i p) d -> b p i d", i=TPB, p=P)
        ov = out[0:T + BLK].rearrange("(b i p) d -> b p i d", i=TPB, p=P)
        tv = table[:, 0:D].rearrange("(b i p) d -> b p i d", i=TPB, p=P)
        RPB = S // BLK
        NC_ROW = S // CH

        def use(name, b):
            u = USES.index(name)
            return u % NW, PER_BANK * b + u // NW + 1

        def filled(eng, name, b):
            bank, n = use(name, b)
            eng.wait_ge(full[bank], n + 1)

        def emptied(eng, name, b):
            bank, n = use(name, b)
            eng.wait_ge(free[bank], n + 1)

        with nc.Block() as block:

            @block.sync
            def _(sp):
                with nc.allow_non_contiguous_dma(reason="two columns of biases"):
                    sp.dma_start(bq_c[:], bq.rearrange("(k p) -> p k", p=P)).then_inc(b_in, 16)
                    sp.dma_start(bk_c[:], bk.rearrange("(k p) -> p k", p=P)).then_inc(b_in, 16)
                sp.dma_start(bkv_r[:, D:], bv.unsqueeze(0).to_broadcast([P, D])).then_inc(b_in, 16)
                sp.dma_start(bo_r[:], bo.unsqueeze(0).to_broadcast([P, D])).then_inc(b_in, 16)
                sp.wait_ge(b_in, 16 * 4)

            @block.gpsimd
            def _(pool):
                pool.dma_start(xb[0][:], xv[0]).then_inc(x_in[0], 16)
                pool.dma_start(xb[1][:], xv[1]).then_inc(x_in[1], 16)
                nc.gpsimd.memset(qd[0][:].bitcast(F32), 0.0)
                nc.gpsimd.memset(vx[0][:], 0.0)
                nc.gpsimd.memset(vx[1][:], 0.0)
                nc.gpsimd.memset(x2[1][:], 1.0)
                nc.gpsimd.memset(bkv_r[:, 0:D], 0.0)

            @block.vector
            def _(dve):
                nc.vector.memset(qd[1][:].bitcast(F32), 0.0)

        block = ctx.enter_context(nc.Block())

        @block.sync
        def _(sp):
            with sp.Fori(0, B) as r:
                for s in range(RPB):
                    b = RPB * r + s
                    sp.wait_ge(q2_ready, b + 1)
                    for t in range(TPB):
                        if t == 1:
                            filled(sp, "s33", b - 1)
                        if t >= 2:
                            filled(sp, f"s{t - 2}3", b)
                        for h in range(HH):
                            rows = slice(h * HD, (h + 1) * HD)
                            sp.dma_start(qd[t % 2][rows, :, :, h, :].bitcast(F32),
                                         q2[s][rows, :, :, t * CH:(t + 1) * CH].bitcast(F32)).then_inc(qd_in[t % 2], 16)

        @block.gpsimd
        def _(pool):
            def residual(s, n):
                pool.wait_ge(xn_ready, n)
                nc.gpsimd.tensor_tensor(xb[s][:], xb[s][:], bo_r[:].unsqueeze(1).to_broadcast([P, TPB, D]),
                                        ALU.add).then_inc(xr_ready, 1)

            def store_rows(b):
                pool.wait_ge(xn3_ready, b + 1)
                pool.dma_start(tv[b], xn3[:]).then_inc(xn3_out, 16)

            def masked_scores(t, b):
                emptied(pool, f"s{t}3", b)
                step_past(pool, c["passed"])
                nc.gpsimd.tensor_tensor(ss[t % 2][:, 12:16, :], ss[t % 2][:, 12:16, :],
                                        c["causal"][:].unsqueeze(1).to_broadcast([P, 4, CH]),
                                        ALU.mult).then_inc(masked, 1)

            def low_keys(s, n):
                pool.wait_ge(kh_ready, n)
                step_past(pool, c["passed"])
                nc.gpsimd.tensor_tensor(kl[s][:], kt[s][:], kh[s][:].bitcast(F32), ALU.subtract).then_inc(kl_ready, 1)

            pool.dma_start(ov[NB], x2[1][:]).then_inc(x2_out[1], 16)
            residual(0, 1)
            low_keys(0, 1)
            with pool.Fori(0, B) as r:
                for s in range(RPB):
                    b = RPB * r + s
                    for t in range(TPB):
                        p = t % 2
                        emptied(pool, f"kv{t}", b)
                        step_past(pool, c["passed"])
                        v4 = kv[p][:, D:].rearrange("p (g e d) -> p g e d", e=2, d=HD)
                        x4 = vx[p][:].rearrange("p (g e) d -> p g e d", e=2)
                        nc.gpsimd.tensor_copy(x4[:, :, 0, 0:HD], v4[:, :, 0, :])
                        nc.gpsimd.tensor_copy(x4[:, :, 1, HD:], v4[:, :, 1, :]).then_inc(vx_ready, 1)
                        masked_scores(t, b)
                        if t == 1:
                            store_rows(b)
                            residual(1 - s, b + 2)
                    low_keys(1 - s, b + 2)
                    emptied(pool, "y3", b)
                    pool.dma_start(xb[s][:], xv[b + 2]).then_inc(x_in[s], 16)
                    pool.dma_start(ov[b], x2[s][:]).then_inc(x2_out[s], 16)
            store_rows(NB)
            pool.wait_ge(xn3_out, 16 * (NB + 1))
            for s in range(2):
                pool.wait_ge(x2_out[s], 16 * (B + s))
                pool.wait_ge(x_in[s], 16 * (B + 1))

        @block.scalar
        def _(act):
            def root(sd, ve, ready, n):
                act.wait_ge(ve, n)
                nc.scalar.activation(sd[:], sd[:], ACT.Sqrt).then_inc(ready, 1)

            def turned(s, n):
                act.wait_ge(x_turned, n)
                nc.scalar.copy(xth[s][:], ps_t[:]).then_inc(xth_ready, 1)

            def keys(s, banks, q_bank, q_n):
                for k, (bank, m) in enumerate(banks):
                    act.wait_ge(full[bank], m)
                    nc.scalar.activation(kt[s][:, k, :], ps_w[bank][:], ACT.Identity,
                                         bias=bk_c[:, k:k + 1]).then_inc(free[bank], 1)
                    if k == 0:
                        act.wait_ge(free[q_bank], q_n)
                        nc.scalar.copy(q2[s][:, 0], qt[s][:]).then_inc(qh_ready, 1)
                act.wait_ge(free[banks[1][0]], banks[1][1])
                nc.scalar.copy(kh[s][:], kt[s][:]).then_inc(kh_ready, 1)

            def scores(t, b):
                bank, n = use(f"s{t}3", b)
                act.wait_ge(full[bank], n + 1)
                nc.scalar.copy(ss[t % 2][:, 12:16, :], ps_w[bank][:].rearrange("p (h i) -> p h i", h=4)
                               ).then_inc(free[bank], 1)

            def heads(t, q):
                act.wait_ge(o_done, q + 1)
                nc.scalar.copy(oth[t % 2][:], ps_o[:]).then_inc(oth_ready, 1)

            def rows3(n):
                act.wait_ge(t3_done, n)
                nc.scalar.copy(xt3[:], ps_t[:]).then_inc(xt3_ready, 1)

            def rows_out(s, b):
                act.wait_ge(rs3_ready, b + 1)
                for i in range(TPB):
                    last = nc.scalar.activation(xn3[:, i, :], x2[s][:, i, :], ACT.Identity, bias=nm3[:, i:i + 1])
                last.then_inc(centred, 1)
                act.wait_ge(centred, b + 1)
                for i in range(TPB):
                    last = nc.scalar.activation(xn3[:, i, :], xn3[:, i, :], ACT.Copy, scale=rs3[:, i:i + 1])
                last.then_inc(xn3_ready, 1)

            def by_expert(n):
                act.wait_ge(lt_done, n)
                nc.scalar.copy(lt[:], ps_t[:, 0, 0:P]).then_inc(lt_ready, 1)

            def rows_left(b):
                act.wait_ge(xn3_out, 16 * (b + 1))

            root(sd2, ve2, sd2_ready, 1)
            turned(0, 1)
            keys(0, [(2, 1), (3, 1)], 1, 1)
            with act.Fori(0, B) as r:
                for s in range(RPB):
                    b = RPB * r + s
                    root(sd3, ve3, sd3_ready, b + 1)
                    scores(0, b)
                    rows_out(1 - s, b)
                    scores(1, b)
                    root(sd2, ve2, sd2_ready, b + 2)
                    heads(0, TPB * b)
                    scores(2, b)
                    turned(1 - s, b + 2)
                    heads(1, TPB * b + 1)
                    keys(1 - s, [(bank, n + 1) for bank, n in (use("k0", b), use("k1", b))],
                         use("q1", b)[0], use("q1", b)[1] + 1)
                    scores(3, b)
                    heads(2, TPB * b + 2)
                    rows3(b + 1)
                    heads(3, TPB * b + 3)
                    by_expert(b + 1)
                    rows_left(b)
            root(sd3, ve3, sd3_ready, NB + 1)
            rows_out(1, NB)
            rows3(NB + 1)
            by_expert(NB + 1)

        @block.vector
        def _(dve):
            def statistics_in(s, n_in):
                dve.wait_ge(x_in[s], n_in)
                return statistics(nc, xb[s], stats2, range(TPB))

            def rows_in(ch, s, n):
                dve.wait_ge(sd2_ready, n)
                ch.link(nc.vector.reciprocal(rs2[:], sd2[:]))
                normalise(nc.vector, xb[s], mv2, rs2, xn, TPB).then_inc(xn_ready, 1)

            def roots_out(b):
                nc.vector.tensor_scalar(nm3[:], mv3[:, :, 0], -1.0, None, ALU.mult)
                dve.wait_ge(sd3_ready, b + 1)
                nc.vector.reciprocal(rs3[:], sd3[:]).then_inc(rs3_ready, 1)

            def variances_out(ch, s, b):
                dve.wait_ge(free[use("y3", 0)[0]], PER_BANK * b + 1)
                variances(nc, c, dve, ch, statistics(nc, x2[s], stats3, range(2, TPB)), stats3, mv3, sd3, ve3, TPB)

            def statistics_out(t, b, s):
                bank, n = use(f"y{t}", b)
                dve.wait_ge(free[bank], n + 1)
                statistics(nc, x2[s], stats3, [t])

            def turned(s, n):
                dve.wait_ge(xth_ready, n)
                split_low(nc, xtl[s][:], ps_t[:], xth[s][:]).then_inc(xtl_ready, 1)

            def queries(s, half, n, banks):
                for k, (bank, m) in enumerate(banks):
                    dve.wait_ge(full[bank], m)
                    nc.vector.scalar_tensor_tensor(qt[s][:, k, :], ps_w[bank][:], bq_c[:, k:k + 1],
                                                   c["decay"][:, k, half * BLK:(half + 1) * BLK],
                                                   ALU.add, ALU.mult).then_inc(free[bank], 1)
                dve.wait_ge(qh_ready, n)
                split_low(nc, q2[s][:, 1], qt[s][:], q2[s][:, 0]).then_inc(q2_ready, 1)

            def keys_values(t, b):
                bank, n = use(f"kv{t}", b)
                dve.wait_ge(full[bank], n + 1)
                nc.vector.tensor_tensor(kv[t % 2][:], ps_w[bank][:], bkv_r[:], ALU.add).then_inc(free[bank], 1)

            def scores(t, b):
                for g in range(3):
                    bank, n = use(f"s{t}{g}", b)
                    dve.wait_ge(full[bank], n + 1)
                    nc.vector.tensor_tensor(ss[t % 2][:, 4 * g:4 * g + 4, :],
                                            ps_w[bank][:].rearrange("p (h i) -> p h i", h=4),
                                            c["causal"][:].unsqueeze(1).to_broadcast([P, 4, CH]),
                                            ALU.mult).then_inc(free[bank], 1)

            def outputs(ch, t, b, s, r):
                q = TPB * b + t
                dve.wait_ge(oth_ready, q + 1)
                split_low(nc, otl[t % 2][:], ps_o[:], oth[t % 2][:]).then_inc(otl_ready, 1)
                i = TPB * s + t
                if i < NC_ROW - 1:
                    dve.wait_ge(st_done, (NC_ROW - 1) * r + i + 1)
                    mask = c["head_mask"][:].unsqueeze(1).to_broadcast([P, KD, P])
                    if i == 0:
                        nc.vector.tensor_tensor(state[0][:], ps_st[:], mask, ALU.mult).then_inc(st_added, 1)
                    else:
                        ch.link(nc.vector.tensor_tensor(fresh[:], ps_st[:], mask, ALU.mult))
                        nc.vector.tensor_tensor(state[i % 2][:], fresh[:], state[(i - 1) % 2][:],
                                                ALU.add).then_inc(st_added, 1)

            def logits_out(b):
                dve.wait_ge(lg_done, b + 1)
                nc.vector.tensor_copy(c["logits"][:, b, :].rearrange("p (t e) -> p t e", e=E), of_experts(ps_t[:, 1, 0:P]))

            def buffers_left(s, r):
                dve.wait_ge(x2_out[1 - s], 16 * (r + 1))

            def projected(t, b, s, r):
                bank, n = use(f"y{t}", b)
                dve.wait_ge(full[bank], n + 1)
                if t == 0:
                    dve.wait_ge(xr_ready, b + 1)
                nc.vector.tensor_tensor(x2[s][:, t, :], ps_w[bank][:, 0:D], xb[s][:, t, :],
                                        ALU.add).then_inc(free[bank], 1)

            ch = Count(dve, chain)
            variances(nc, c, dve, ch, statistics_in(0, 16), stats2, mv2, sd2, ve2, TPB)
            rows_in(ch, 0, 1)
            statistics(nc, x2[1], stats3, range(2))
            turned(0, 1)
            queries(0, 0, 1, [(0, 1), (1, 1)])
            start, per = ch.n, 2 * 5 + NC_ROW - 2
            with dve.Fori(0, B) as r:
                ch = Count(dve, chain, per * r + start)
                for s in range(RPB):
                    b = RPB * r + s
                    keys_values(0, b)
                    variances_out(ch, 1 - s, b)
                    scores(0, b)
                    roots_out(b)
                    keys_values(1, b)
                    last = statistics_in(1 - s, 16 * (r + 1 + s))
                    scores(1, b)
                    variances(nc, c, dve, ch, last, stats2, mv2, sd2, ve2, TPB)
                    outputs(ch, 0, b, s, r)
                    keys_values(2, b)
                    projected(0, b, s, r)
                    dve.wait_ge(x_turned, b + 1)
                    rows_in(ch, 1 - s, b + 2)
                    scores(2, b)
                    statistics_out(0, b, s)
                    turned(1 - s, b + 2)
                    outputs(ch, 1, b, s, r)
                    keys_values(3, b)
                    projected(1, b, s, r)
                    queries(1 - s, 1 - s, b + 2, [(bank, n + 1) for bank, n in (use("q0", b), use("q1", b))])
                    scores(3, b)
                    statistics_out(1, b, s)
                    outputs(ch, 2, b, s, r)
                    projected(2, b, s, r)
                    outputs(ch, 3, b, s, r)
                    projected(3, b, s, r)
                    logits_out(b)
                    buffers_left(s, r)
                assert ch.n == per
            ch = Count(dve, chain, per * B + start)
            variances_out(ch, 1, NB)
            roots_out(NB)
            logits_out(NB)

        @block.tensor
        def _(pe):
            def turn(src):
                for k in range(KD):
                    for t in range(TPB):
                        last = nc.tensor.transpose(ps_t[:, k, t * P:(t + 1) * P], src[:, t, k * P:(k + 1) * P],
                                                   c["ident"][:])
                return last

            def project(name, k, s, bank):
                for j in range(KD):
                    cols = slice(k * P, (k + 1) * P)
                    last = three(nc, ps_w[bank][:], w_hi[name][:, j, cols], w_lo[name][:, j, cols],
                                 xth[s][:, j, :], xtl[s][:, j, :], j == 0, j == KD - 1)
                last.then_inc(full[bank], 1)

            def take(name, b):
                bank, n = use(name, b)
                pe.wait_ge(free[bank], n)
                return bank

            def keys_values(t, b, s):
                bank = take(f"kv{t}", b)
                pos = slice(t * CH, (t + 1) * CH)
                for k in range(KD):
                    nc.tensor.transpose(ps_w[bank][:, k * P:(k + 1) * P], kt[s][:, k, pos], c["ident"][:])
                for k in range(KD):
                    last = three(nc, ps_w[bank][:, D:], xth[s][:, k, pos], xtl[s][:, k, pos],
                                 w_hi["v"][:, k, :], w_lo["v"][:, k, :], k == 0, k == KD - 1)
                last.then_inc(full[bank], 1)

            def scores(t, b, s):
                pe.wait_ge(qd_in[t % 2], 16 * HH * (2 * b + t // 2 + 1))
                pos = slice(t * CH, (t + 1) * CH)
                for g in range(4):
                    bank = take(f"s{t}{g}", b)
                    k, hs = g // 2, slice(4 * (g % 2), 4 * (g % 2) + 4)
                    last = three(nc, ps_w[bank][:], kh[s][:, k, pos], kl[s][:, k, pos],
                                 qd[t % 2][:, 0, k, hs, :], qd[t % 2][:, 1, k, hs, :], True, True)
                    last.then_inc(full[bank], 1)

            def outputs(t, b, s, r):
                q, i, p = TPB * b + t, TPB * s + t, t % 2
                emptied(pe, f"s{t}2", b)
                pe.wait_ge(vx_ready, q + 1)
                pe.wait_ge(masked, q + 1)
                if i > 0:
                    pe.wait_ge(st_added, (NC_ROW - 1) * r + i)
                for k in range(KD):
                    if i > 0:
                        nc.tensor.matmul(ps_o[:, k, :], state[(i - 1) % 2][:, k, :], qt[s][:, k, t * CH:(t + 1) * CH],
                                         start=True, stop=False, skip_group_check=True)
                    for odd in range(2):
                        for g in range(HH // 2):
                            h = HH * k + 2 * g + odd
                            last = nc.tensor.matmul(ps_o[32 * g:32 * g + 32, k, :], vx[p][:, h, :], ss[p][:, h, :],
                                                    start=(i == 0 and odd == 0), stop=(odd == 1), skip_group_check=True)
                last.then_inc(o_done, 1)
                if i < NC_ROW - 1:
                    for k in range(KD):
                        last = nc.tensor.matmul(ps_st[:, k, :], kv[p][:, k * P:(k + 1) * P],
                                                kv[p][:, D + k * P:D + (k + 1) * P], start=True, stop=True)
                    last.then_inc(st_done, 1)

            def result(t, b):
                pe.wait_ge(otl_ready, TPB * b + t + 1)
                bank = take(f"y{t}", b)
                for k in range(KD):
                    last = three(nc, ps_w[bank][:, 0:D], oth[t % 2][:, k, :], otl[t % 2][:, k, :],
                                 w_hi["o"][:, k, :], w_lo["o"][:, k, :], k == 0, k == KD - 1)
                last.then_inc(full[bank], 1)

            def turn_rows3(n):
                pe.wait_ge(xn3_ready, n)
                turn(xn3).then_inc(t3_done, 1)

            def logits_up(n):
                pe.wait_ge(xt3_ready, n)
                logits_by_expert(nc, c, ps_t[:, 0, 0:P], xt3).then_inc(lt_done, 1)

            def logits_turned(n):
                pe.wait_ge(lt_ready, n)
                nc.tensor.transpose(ps_t[:, 1, 0:P], lt[:], c["ident"][:]).then_inc(lg_done, 1)

            pe.wait_ge(xn_ready, 1)
            turn(xn).then_inc(x_turned, 1)
            pe.wait_ge(xtl_ready, 1)
            for bank, (name, k) in enumerate((("q", 0), ("q", 1), ("k", 0), ("k", 1))):
                project(name, k, 0, bank)
            with pe.Fori(0, B) as r:
                for s in range(RPB):
                    b = RPB * r + s
                    pe.wait_ge(kl_ready, b + 1)
                    keys_values(0, b, s)
                    scores(0, b, s)
                    keys_values(1, b, s)
                    scores(1, b, s)
                    outputs(0, b, s, r)
                    keys_values(2, b, s)
                    result(0, b)
                    scores(2, b, s)
                    pe.wait_ge(xn_ready, b + 2)
                    turn(xn).then_inc(x_turned, 1)
                    outputs(1, b, s, r)
                    keys_values(3, b, s)
                    result(1, b)
                    pe.wait_ge(xtl_ready, b + 2)
                    for name, k in (("q", 0), ("q", 1), ("k", 0), ("k", 1)):
                        project(name, k, 1 - s, take(f"{name}{k}", b))
                    scores(3, b, s)
                    outputs(2, b, s, r)
                    turn_rows3(b + 1)
                    result(2, b)
                    outputs(3, b, s, r)
                    logits_up(b + 1)
                    result(3, b)
                    logits_turned(b + 1)
            turn_rows3(NB + 1)
            logits_up(NB + 1)
            logits_turned(NB + 1)


def macaron(nc, x, wqt, bq, wkt, bk, wvt, bv, wot, bo, gamma, wg, w_gate, w_down, out):
    with ExitStack() as ctx:
        def sb(name, shape, dt=F32):
            return ctx.enter_context(nc.sbuf_tensor(name, shape, dt))

        c = {
            "ident": sb("ident", [P, P]), "causal": sb("causal", [P, P]), "before": sb("before", [P, P], BF16),
            "ones": sb("ones", [P, P], BF16), "iota": sb("iota", [P, P], BF16),
            "tile_id": sb("tile_id", [P, NT], BF16), "part_id": sb("part_id", [P, 1]),
            "dummy_row": sb("dummy_row", [P, NCOL]), "rank": sb("rank", [P, E]),
            "restart": sb("restart", [P, E, NT]), "head_mask": sb("head_mask", [P, P]),
            "passed": ctx.enter_context(nc.semaphore("passed")),
            "decay": sb("decay", [P, KD, S]), "gamma_col": sb("gamma_col", [P, KD]), "gamma_dram": gamma,
            "w_hi": {n: sb(f"w{n}h", [P, KD, D], F32R) for n in "qkvo"},
            "w_lo": {n: sb(f"w{n}l", [P, KD, D], F32R) for n in "qkvo"},
            "mean": sb("mean", [P, NT // 8, 8]), "rstd": sb("rstd", [P, NT // 8, 8]),
            "wg": sb("wg", [P, KD, 32]), "logits": sb("logits", [P, NB + 1, TPB * E]), "wg_dram": wg,
        }
        table = nc.dram_tensor("dispatch_rows", (BLK + T, ROW), F32, kind="Internal").ap()
        acc = nc.dram_tensor("after_moe1", (T + CAP, D), F32, kind="Internal").ap()
        build_constants(nc, c)
        x_meta = nc.dram_tensor("token_gates", (T, MW), F32, kind="Internal").ap()
        route_first(nc, c, x)
        moe(nc, c, w_gate, w_down, None, acc, "f1", x, x_meta, (wqt, wkt, wvt, wot))
        attention(nc, c, acc, bq, bk, bv, bo, table, out)
        moe(nc, c, w_gate, w_down, table, out, "f2")


def kernel(**inputs):
    import numpy as np
    from concourse import bacc
    from concourse.bass_utils import run_bass_kernel_spmd

    given = {n.removeprefix("L0_"): np.asarray(a) for n, a in inputs.items()}
    laid = {"x": given["attn_x"].reshape(T, D)}
    for n in "qkvo":
        laid[f"w{n}"] = given[f"attn_W{n}"].T
        laid[f"b{n}"] = given[f"attn_b{n}"]
    laid["gamma"] = given["attn_gamma"]
    laid["wg"] = given["ffn_wg"]
    laid["w_gate"] = given["ffn_w_gate"]
    laid["w_down"] = given["ffn_w_down"]
    nc = bacc.Bacc("TRN2", target_bir_lowering=False, num_devices=1)
    arrays, args = {}, []
    for n, a in laid.items():
        arrays[f"in_{n}"] = np.ascontiguousarray(a)
        args.append(nc.dram_tensor(f"in_{n}", a.shape, F32, kind="ExternalInput").ap())
    args.append(nc.dram_tensor("out_rows", (T + CAP, D), F32, kind="ExternalOutput").ap())
    macaron(nc, *args)
    got = run_bass_kernel_spmd(nc, [arrays], core_ids=[0]).results[0]["out_rows"]
    return got[:T].reshape(B, S, D)
```
